# Optimizing a Trainium2 kernel written in Bass

```python
import numpy as np
import jax
import jax.numpy as jnp

def _softmax(x, axis=-1):
    return jax.nn.softmax(x, axis=axis)

def _gelu(x):
    return jax.nn.gelu(x, approximate=True)

def _silu(x):
    return jax.nn.silu(x)

def _sigmoid(x):
    return jax.nn.sigmoid(x)

def _layernorm(x, axis=-1, eps=1e-05):
    m = jnp.mean(x, axis=axis, keepdims=True)
    v = jnp.var(x, axis=axis, keepdims=True)
    return (x - m) / jnp.sqrt(v + eps)

def _scatter_add(tgt, idx, src, axis=0):
    return tgt.at[idx].add(src)

def _segment_sum(src, seg, n):
    return jax.ops.segment_sum(src, seg, n)
kernel_name = 'mk_metaformer_d2_conv_nhwc256_r2_6b2faf'

def setup_inputs(seed: int=0):
    np.random.seed(seed)
    _w = jnp.asarray

    def _rec_inputs():
        import jax
        import jax.numpy as jnp
        _gk = jax.random.key(seed)
        x = 7.22e-05 + 1 * jax.random.normal(jax.random.fold_in(_gk, 1), (1, 64, 128, 128), jnp.float32)
        return x
    x = _rec_inputs()

    def _L0_conv_setup():
        import jax, jax.numpy as jnp
        import numpy as np
        C_S = 128
        C_Z = 64
        C_HIDDEN = 32
        NO_HEADS = 8
        INF = 1000000000.0
        EPS = 1e-05

        def _layernorm(x, w, b):
            mu = jnp.mean(x, axis=-1, keepdims=True)
            var = jnp.var(x, axis=-1, keepdims=True)
            return (x - mu) * jax.lax.rsqrt(var + EPS) * w + b
        key = jax.random.key(seed)
        ks = jax.random.split(key, 12)
        B, S, R = (1, 64, 128)
        H, D = (NO_HEADS, C_HIDDEN)
        hd = H * D
        inp = {'s': jax.random.normal(ks[0], (B, S, R, C_S), dtype=jnp.float32), 'z': jax.random.normal(ks[1], (B, R, R, C_Z), dtype=jnp.float32), 'mask': jnp.ones((B, S, R), dtype=jnp.float32), 'ln_s_w': jnp.ones((C_S,), dtype=jnp.float32), 'ln_s_b': jnp.zeros((C_S,), dtype=jnp.float32), 'ln_z_w': jnp.ones((C_Z,), dtype=jnp.float32), 'ln_z_b': jnp.zeros((C_Z,), dtype=jnp.float32), 'w_z': jax.random.normal(ks[2], (C_Z, H), dtype=jnp.float32) * 0.02, 'w_q': jax.random.normal(ks[3], (C_S, hd), dtype=jnp.float32) * (1.0 / np.sqrt(C_S)), 'w_k': jax.random.normal(ks[4], (C_S, hd), dtype=jnp.float32) * (1.0 / np.sqrt(C_S)), 'w_v': jax.random.normal(ks[5], (C_S, hd), dtype=jnp.float32) * (1.0 / np.sqrt(C_S)), 'w_g': jax.random.normal(ks[6], (C_S, hd), dtype=jnp.float32) * 0.02, 'b_g': jnp.ones((hd,), dtype=jnp.float32), 'w_o': jax.random.normal(ks[7], (hd, C_S), dtype=jnp.float32) * (1.0 / np.sqrt(hd)), 'b_o': jnp.zeros((C_S,), dtype=jnp.float32)}
        return inp
    _L0_conv_all = _L0_conv_setup()
    _L0_conv_in = {k: v for k, v in _L0_conv_all.items() if k in ('z', 'mask', 'ln_s_w', 'ln_s_b', 'ln_z_w', 'ln_z_b', 'w_z', 'w_q', 'w_k', 'w_v', 'w_g', 'b_g', 'w_o', 'b_o')}
    del _L0_conv_all

    def _L0_ffn_setup():
        import jax, jax.numpy as jnp
        import numpy as np
        B, N, D = (16, 2048, 128)
        NUM_EXPERTS, TOP_K, HEADS = (4, 2, 4)
        N_EDGES = 524288
        LN_EPS = 1e-05

        def _layernorm(x, g, b):
            mu = x.mean(-1, keepdims=True)
            var = ((x - mu) ** 2).mean(-1, keepdims=True)
            return (x - mu) * jax.lax.rsqrt(var + LN_EPS) * g + b

        def _forward(x, edge_index, W_gat, att_src, att_dst, b_gat, ln_gamma, ln_beta, W1, b1, W2, b2):
            Bc, Nc, Dc = x.shape
            M = Bc * Nc
            x_flat = x.reshape(M, Dc)
            h = (x_flat @ W_gat).reshape(M, HEADS, NUM_EXPERTS)
            loops = jnp.arange(M, dtype=edge_index.dtype)
            src = jnp.concatenate([edge_index[0], loops])
            dst = jnp.concatenate([edge_index[1], loops])
            a_src = (h * att_src).sum(-1)
            a_dst = (h * att_dst).sum(-1)
            e = jax.nn.leaky_relu(a_src[src] + a_dst[dst], negative_slope=0.2)
            e_max = jax.ops.segment_max(e, dst, num_segments=M)
            ee = jnp.exp(e - e_max[dst])
            denom = jax.ops.segment_sum(ee, dst, num_segments=M)
            alpha = ee / (denom[dst] + 1e-16)
            msg = h[src] * alpha[:, :, None]
            agg = jax.ops.segment_sum(msg, dst, num_segments=M).reshape(M, HEADS * NUM_EXPERTS) + b_gat
            scores = _layernorm(agg, ln_gamma, ln_beta).reshape(M, HEADS, NUM_EXPERTS).mean(1)
            scores = scores.reshape(Bc, Nc, NUM_EXPERTS)
            topk_s, topk_i = jax.lax.top_k(scores, TOP_K)
            w = jax.nn.softmax(topk_s, axis=-1)
            out = jnp.zeros_like(x)
            for ei in range(NUM_EXPERTS):
                g = jnp.where(topk_i == ei, w, 0.0).sum(-1)
                hh = jax.nn.gelu(x @ W1[ei] + b1[ei], approximate=False)
                out = out + g[..., None] * (hh @ W2[ei] + b2[ei])
            return out
        key = jax.random.key(seed)
        ks = jax.random.split(key, 8)
        s = 0.05
        return {'x': jax.random.normal(ks[0], (B, N, D), jnp.float32), 'W_gat': jax.random.normal(ks[1], (D, HEADS * NUM_EXPERTS), jnp.float32) * s, 'att_src': jax.random.normal(ks[2], (HEADS, NUM_EXPERTS), jnp.float32) * s, 'att_dst': jax.random.normal(ks[3], (HEADS, NUM_EXPERTS), jnp.float32) * s, 'b_gat': jnp.zeros((HEADS * NUM_EXPERTS,), jnp.float32), 'ln_gamma': jnp.ones((HEADS * NUM_EXPERTS,), jnp.float32), 'ln_beta': jnp.zeros((HEADS * NUM_EXPERTS,), jnp.float32), 'W1': jax.random.normal(ks[4], (NUM_EXPERTS, D, 2 * D), jnp.float32) * s, 'b1': jnp.zeros((NUM_EXPERTS, 2 * D), jnp.float32), 'W2': jax.random.normal(ks[5], (NUM_EXPERTS, 2 * D, D), jnp.float32) * s, 'b2': jnp.zeros((NUM_EXPERTS, D), jnp.float32), 'edge_index': jax.random.randint(ks[6], (2, N_EDGES), 0, B * N, jnp.int32)}
    _L0_ffn_all = _L0_ffn_setup()
    _L0_ffn_in = {k: v for k, v in _L0_ffn_all.items() if k in ('W_gat', 'att_src', 'att_dst', 'b_gat', 'ln_gamma', 'ln_beta', 'W1', 'b1', 'W2', 'b2', 'edge_index')}
    del _L0_ffn_all

    def _L1_conv_setup():
        import jax, jax.numpy as jnp
        import numpy as np
        H = 4
        TEMP = 1.0
        key = jax.random.key(seed)
        ks = jax.random.split(key, 7)
        B, F, T, D = (4, 64, 128, 128)
        s = 0.02
        return {'x': jax.random.normal(ks[0], (B, F, T, D), jnp.float32), 'Wqk': jax.random.normal(ks[1], (D, 2 * H * D), jnp.float32) * s, 'bqk': jax.random.normal(ks[2], (2 * H * D,), jnp.float32) * s, 'Wv': jax.random.normal(ks[3], (D, H * D), jnp.float32) * s, 'bv': jax.random.normal(ks[4], (H * D,), jnp.float32) * s, 'Wproj': jax.random.normal(ks[5], (H * D, D), jnp.float32) * s, 'bproj': jax.random.normal(ks[6], (D,), jnp.float32) * s}
    _L1_conv_all = _L1_conv_setup()
    _L1_conv_in = {k: v for k, v in _L1_conv_all.items() if k in ('Wqk', 'bqk', 'Wv', 'bv', 'Wproj', 'bproj')}
    del _L1_conv_all

    def _L1_ffn_setup():
        import jax, jax.numpy as jnp
        import numpy as np
        NUM_EXPERTS = 8
        TOP_K = 2
        B, S, D = (8, 4096, 128)

        def _moe(tokens, router_w, w1, b1, w2, b2):
            N = tokens.shape[0]
            E = router_w.shape[0]
            logits = tokens.astype(jnp.float32) @ router_w.astype(jnp.float32).T
            probs = jax.nn.softmax(logits, axis=-1)
            rw, re = jax.lax.top_k(probs, TOP_K)
            if TOP_K > 1:
                rw = rw / jnp.maximum(rw.sum(-1, keepdims=True), 1e-12)
            rw = rw.astype(tokens.dtype)
            combine = jnp.zeros((N, E), tokens.dtype).at[jnp.arange(N)[:, None], re].set(rw)
            out = tokens
            for e in range(E):
                h = jax.nn.gelu(tokens @ w1[e] + b1[e], approximate=False)
                y = h @ w2[e] + b2[e]
                out = out + combine[:, e:e + 1] * y
            return out
        key = jax.random.key(seed)
        ks = jax.random.split(key, 4)
        scale = 1.0 / np.sqrt(D).astype(np.float32)
        return {'input_embeddings': jax.random.normal(ks[0], (B, S, D), jnp.float32), 'router_w': jax.random.normal(ks[1], (NUM_EXPERTS, D), jnp.float32) * scale, 'w1': jax.random.normal(ks[2], (NUM_EXPERTS, D, D), jnp.float32) * scale, 'b1': jnp.zeros((NUM_EXPERTS, D), jnp.float32), 'w2': jax.random.normal(ks[3], (NUM_EXPERTS, D, D), jnp.float32) * scale, 'b2': jnp.zeros((NUM_EXPERTS, D), jnp.float32)}
    _L1_ffn_all = _L1_ffn_setup()
    _L1_ffn_in = {k: v for k, v in _L1_ffn_all.items() if k in ('router_w', 'w1', 'b1', 'w2', 'b2')}
    del _L1_ffn_all
    return {'x': x, 'L0_conv_z': _L0_conv_in['z'], 'L0_conv_mask': _L0_conv_in['mask'], 'L0_conv_ln_s_w': _L0_conv_in['ln_s_w'], 'L0_conv_ln_s_b': _L0_conv_in['ln_s_b'], 'L0_conv_ln_z_w': _L0_conv_in['ln_z_w'], 'L0_conv_ln_z_b': _L0_conv_in['ln_z_b'], 'L0_conv_w_z': _L0_conv_in['w_z'], 'L0_conv_w_q': _L0_conv_in['w_q'], 'L0_conv_w_k': _L0_conv_in['w_k'], 'L0_conv_w_v': _L0_conv_in['w_v'], 'L0_conv_w_g': _L0_conv_in['w_g'], 'L0_conv_b_g': _L0_conv_in['b_g'], 'L0_conv_w_o': _L0_conv_in['w_o'], 'L0_conv_b_o': _L0_conv_in['b_o'], 'L0_ffn_W_gat': _L0_ffn_in['W_gat'], 'L0_ffn_att_src': _L0_ffn_in['att_src'], 'L0_ffn_att_dst': _L0_ffn_in['att_dst'], 'L0_ffn_b_gat': _L0_ffn_in['b_gat'], 'L0_ffn_ln_gamma': _L0_ffn_in['ln_gamma'], 'L0_ffn_ln_beta': _L0_ffn_in['ln_beta'], 'L0_ffn_W1': _L0_ffn_in['W1'], 'L0_ffn_b1': _L0_ffn_in['b1'], 'L0_ffn_W2': _L0_ffn_in['W2'], 'L0_ffn_b2': _L0_ffn_in['b2'], 'L0_ffn_edge_index': _L0_ffn_in['edge_index'], 'L1_conv_Wqk': _L1_conv_in['Wqk'], 'L1_conv_bqk': _L1_conv_in['bqk'], 'L1_conv_Wv': _L1_conv_in['Wv'], 'L1_conv_bv': _L1_conv_in['bv'], 'L1_conv_Wproj': _L1_conv_in['Wproj'], 'L1_conv_bproj': _L1_conv_in['bproj'], 'L1_ffn_router_w': _L1_ffn_in['router_w'], 'L1_ffn_w1': _L1_ffn_in['w1'], 'L1_ffn_b1': _L1_ffn_in['b1'], 'L1_ffn_w2': _L1_ffn_in['w2'], 'L1_ffn_b2': _L1_ffn_in['b2']}

def reference(x, L0_conv_z, L0_conv_mask, L0_conv_ln_s_w, L0_conv_ln_s_b, L0_conv_ln_z_w, L0_conv_ln_z_b, L0_conv_w_z, L0_conv_w_q, L0_conv_w_k, L0_conv_w_v, L0_conv_w_g, L0_conv_b_g, L0_conv_w_o, L0_conv_b_o, L0_ffn_W_gat, L0_ffn_att_src, L0_ffn_att_dst, L0_ffn_b_gat, L0_ffn_ln_gamma, L0_ffn_ln_beta, L0_ffn_W1, L0_ffn_b1, L0_ffn_W2, L0_ffn_b2, L0_ffn_edge_index, L1_conv_Wqk, L1_conv_bqk, L1_conv_Wv, L1_conv_bv, L1_conv_Wproj, L1_conv_bproj, L1_ffn_router_w, L1_ffn_w1, L1_ffn_b1, L1_ffn_w2, L1_ffn_b2):
    import jax
    import jax.numpy as jnp

    def _L0_conv_ref(s, z, mask, ln_s_w, ln_s_b, ln_z_w, ln_z_b, w_z, w_q, w_k, w_v, w_g, b_g, w_o, b_o):
        import jax, jax.numpy as jnp
        import numpy as np
        C_S = 128
        C_Z = 64
        C_HIDDEN = 32
        NO_HEADS = 8
        INF = 1000000000.0
        EPS = 1e-05

        def _layernorm(x, w, b):
            mu = jnp.mean(x, axis=-1, keepdims=True)
            var = jnp.var(x, axis=-1, keepdims=True)
            return (x - mu) * jax.lax.rsqrt(var + EPS) * w + b
        B, S, R, _ = s.shape
        H, D = (NO_HEADS, C_HIDDEN)
        s_n = _layernorm(s, ln_s_w, ln_s_b)
        mask_bias = (INF * (mask - 1.0))[..., :, None, None, :]
        z_n = _layernorm(z, ln_z_w, ln_z_b)
        pair_bias = jnp.einsum('bqkc,ch->bhqk', z_n, w_z)[:, None]
        q = jnp.einsum('bsqc,cx->bsqx', s_n, w_q).reshape(B, S, R, H, D)
        k = jnp.einsum('bskc,cx->bskx', s_n, w_k).reshape(B, S, R, H, D)
        v = jnp.einsum('bskc,cx->bskx', s_n, w_v).reshape(B, S, R, H, D)
        q = q * (1.0 / np.sqrt(D))
        logits = jnp.einsum('bsqhd,bskhd->bshqk', q, k) + mask_bias + pair_bias
        attn = jax.nn.softmax(logits, axis=-1)
        o = jnp.einsum('bshqk,bskhd->bsqhd', attn, v).reshape(B, S, R, H * D)
        g = jax.nn.sigmoid(jnp.einsum('bsqc,cx->bsqx', s_n, w_g) + b_g)
        o = o * g
        out = jnp.einsum('bsqx,xc->bsqc', o, w_o) + b_o
        return out

    def _L0_ffn_ref(x, W_gat, att_src, att_dst, b_gat, ln_gamma, ln_beta, W1, b1, W2, b2, edge_index):
        import jax, jax.numpy as jnp
        import numpy as np
        B, N, D = (16, 2048, 128)
        NUM_EXPERTS, TOP_K, HEADS = (4, 2, 4)
        N_EDGES = 524288
        LN_EPS = 1e-05

        def _layernorm(x, g, b):
            mu = x.mean(-1, keepdims=True)
            var = ((x - mu) ** 2).mean(-1, keepdims=True)
            return (x - mu) * jax.lax.rsqrt(var + LN_EPS) * g + b

        def _forward(x, edge_index, W_gat, att_src, att_dst, b_gat, ln_gamma, ln_beta, W1, b1, W2, b2):
            Bc, Nc, Dc = x.shape
            M = Bc * Nc
            x_flat = x.reshape(M, Dc)
            h = (x_flat @ W_gat).reshape(M, HEADS, NUM_EXPERTS)
            loops = jnp.arange(M, dtype=edge_index.dtype)
            src = jnp.concatenate([edge_index[0], loops])
            dst = jnp.concatenate([edge_index[1], loops])
            a_src = (h * att_src).sum(-1)
            a_dst = (h * att_dst).sum(-1)
            e = jax.nn.leaky_relu(a_src[src] + a_dst[dst], negative_slope=0.2)
            e_max = jax.ops.segment_max(e, dst, num_segments=M)
            ee = jnp.exp(e - e_max[dst])
            denom = jax.ops.segment_sum(ee, dst, num_segments=M)
            alpha = ee / (denom[dst] + 1e-16)
            msg = h[src] * alpha[:, :, None]
            agg = jax.ops.segment_sum(msg, dst, num_segments=M).reshape(M, HEADS * NUM_EXPERTS) + b_gat
            scores = _layernorm(agg, ln_gamma, ln_beta).reshape(M, HEADS, NUM_EXPERTS).mean(1)
            scores = scores.reshape(Bc, Nc, NUM_EXPERTS)
            topk_s, topk_i = jax.lax.top_k(scores, TOP_K)
            w = jax.nn.softmax(topk_s, axis=-1)
            out = jnp.zeros_like(x)
            for ei in range(NUM_EXPERTS):
                g = jnp.where(topk_i == ei, w, 0.0).sum(-1)
                hh = jax.nn.gelu(x @ W1[ei] + b1[ei], approximate=False)
                out = out + g[..., None] * (hh @ W2[ei] + b2[ei])
            return out
        return _forward(x, edge_index, W_gat, att_src, att_dst, b_gat, ln_gamma, ln_beta, W1, b1, W2, b2)

    def _L1_conv_ref(x, Wqk, bqk, Wv, bv, Wproj, bproj):
        import jax, jax.numpy as jnp
        import numpy as np
        H = 4
        TEMP = 1.0
        B, F, T, D = x.shape
        scale = 1.0 / jnp.sqrt(jnp.asarray(D, x.dtype))
        xm = jnp.mean(x, axis=2)
        qk = (xm @ Wqk + bqk).reshape(B, F, H, D, 2)
        q = qk[..., 0] * scale
        k = qk[..., 1] * scale
        scores = jnp.einsum('bfhd,bghd->bhfg', q, k) / TEMP
        w = jax.nn.softmax(scores, axis=-1)
        v = (x @ Wv + bv).reshape(B, F, T, H, D)
        out = jnp.einsum('bhfg,bgthd->bfthd', w, v)
        out = out.reshape(B, F, T, H * D)
        return out @ Wproj + bproj

    def _L1_ffn_ref(input_embeddings, router_w, w1, b1, w2, b2):
        import jax, jax.numpy as jnp
        import numpy as np
        NUM_EXPERTS = 8
        TOP_K = 2
        B, S, D = (8, 4096, 128)

        def _moe(tokens, router_w, w1, b1, w2, b2):
            N = tokens.shape[0]
            E = router_w.shape[0]
            logits = tokens.astype(jnp.float32) @ router_w.astype(jnp.float32).T
            probs = jax.nn.softmax(logits, axis=-1)
            rw, re = jax.lax.top_k(probs, TOP_K)
            if TOP_K > 1:
                rw = rw / jnp.maximum(rw.sum(-1, keepdims=True), 1e-12)
            rw = rw.astype(tokens.dtype)
            combine = jnp.zeros((N, E), tokens.dtype).at[jnp.arange(N)[:, None], re].set(rw)
            out = tokens
            for e in range(E):
                h = jax.nn.gelu(tokens @ w1[e] + b1[e], approximate=False)
                y = h @ w2[e] + b2[e]
                out = out + combine[:, e:e + 1] * y
            return out
        b, s, d = input_embeddings.shape
        tokens = input_embeddings.reshape(b * s, d)
        return _moe(tokens, router_w, w1, b1, w2, b2).reshape(b, s, d)

    def _gn(v, G=32, eps=1e-05):
        B_, H_, W_, C_ = v.shape
        g = v.reshape(B_, H_, W_, G, C_ // G)
        m = jnp.mean(g, axis=(1, 2, 4), keepdims=True)
        s = jnp.var(g, axis=(1, 2, 4), keepdims=True)
        return ((g - m) / jnp.sqrt(s + eps)).reshape(v.shape)

    def _ln_c(v, eps=1e-06):
        m = jnp.mean(v, axis=-1, keepdims=True)
        s = jnp.var(v, axis=-1, keepdims=True)
        return (v - m) / jnp.sqrt(s + eps)

    def _ln_t(v, eps=1e-05):
        m = jnp.mean(v, axis=-1, keepdims=True)
        s = jnp.var(v, axis=-1, keepdims=True)
        return (v - m) / jnp.sqrt(s + eps)

    def _to_tokens(v):
        B_, H_, W_, C_ = v.shape
        return v.reshape(B_, H_ * W_, C_)

    def _from_tokens(t, like):
        return t.reshape(like.shape)
    x = x + _L0_conv_ref(_ln_c(x), L0_conv_z, L0_conv_mask, L0_conv_ln_s_w, L0_conv_ln_s_b, L0_conv_ln_z_w, L0_conv_ln_z_b, L0_conv_w_z, L0_conv_w_q, L0_conv_w_k, L0_conv_w_v, L0_conv_w_g, L0_conv_b_g, L0_conv_w_o, L0_conv_b_o)
    t = _to_tokens(x)
    t = t + _L0_ffn_ref(_ln_t(t), L0_ffn_W_gat, L0_ffn_att_src, L0_ffn_att_dst, L0_ffn_b_gat, L0_ffn_ln_gamma, L0_ffn_ln_beta, L0_ffn_W1, L0_ffn_b1, L0_ffn_W2, L0_ffn_b2, L0_ffn_edge_index)
    x = _from_tokens(t, x)
    x = x + _L1_conv_ref(_ln_c(x), L1_conv_Wqk, L1_conv_bqk, L1_conv_Wv, L1_conv_bv, L1_conv_Wproj, L1_conv_bproj)
    t = _to_tokens(x)
    t = t + _L1_ffn_ref(_ln_t(t), L1_ffn_router_w, L1_ffn_w1, L1_ffn_b1, L1_ffn_w2, L1_ffn_b2)
    x = _from_tokens(t, x)
    return x

_drawn_inputs = setup_inputs


def setup_inputs(seed=0):
    import zlib

    import numpy as np

    out = dict(_drawn_inputs(seed))
    spreads = {'L0_conv_ln_s_w': (1.0, 0.2),
     'L0_conv_ln_s_b': (0.0, 0.1),
     'L0_conv_ln_z_w': (1.0, 0.6),
     'L0_conv_ln_z_b': (0.0, 2.0),
     'L0_conv_b_g': (1.0, 0.6),
     'L0_conv_b_o': (0.0, 0.1),
     'L0_ffn_b_gat': (0.0, 0.1),
     'L0_ffn_ln_gamma': (1.0, 0.2),
     'L0_ffn_ln_beta': (0.0, 0.1),
     'L0_ffn_b1': (0.0, 0.1),
     'L0_ffn_b2': (0.0, 0.1),
     'L1_ffn_b1': (0.0, 0.327),
     'L1_ffn_b2': (0.0, 0.1)}
    factors = {'L0_conv_w_g': 3.081,
     'L0_ffn_att_src': 2.848,
     'L0_ffn_att_dst': 3.595,
     'L1_conv_Wqk': 200.0,
     'L1_conv_bqk': 200.0,
     'L1_conv_bv': 3.021}
    for name, (base, spread) in spreads.items():
        noise = np.random.default_rng([zlib.crc32(name.encode()), seed]).standard_normal(out[name].shape)
        drawn = base * np.exp(spread * noise) if base else spread * noise
        out[name] = jnp.asarray(drawn.astype(out[name].dtype))
    for name, factor in factors.items():
        out[name] = (out[name] * factor).astype(out[name].dtype)
    return out
```

```python
import math
from contextlib import ExitStack

import numpy as np
import concourse.bass as bass
from concourse import mybir

F32 = mybir.dt.float32
BF16 = mybir.dt.bfloat16
I32 = mybir.dt.int32
ALU = mybir.AluOpType
ACT = mybir.ActivationFunctionType
AX = mybir.AxisListType
ds = bass.ds

P = 128
F, T, C = 64, 128, 128
TOKENS = F * T
TILES = TOKENS // P
HEADS, DH = 8, 32
HD = HEADS * DH
CZ = 64
INF = 1e9
EPS_C, EPS_T = 1e-6, 1e-5
BANK = 512
GROUP = BANK // P
GROUPS = TILES // GROUP

GHEADS, EXPERTS0 = 4, 4
GF = GHEADS * EXPERTS0
EDGES = 524288
ECOLS = EDGES // P
NODE_BITS = 13
LO_BITS = 7
SLOT = 8
BLOCKS = 4
BCOLS = ECOLS // BLOCKS
KCOLS = ECOLS + 2 * BLOCKS * SLOT + P
PART = 20
ROW = GF + 2 * GHEADS
HID0 = 256
EXPERTS1 = 8
LH = 4

VALID = 1 << 30
NEAR = 1 << 26


class Chain:

    def __init__(self, engine, semaphore):
        self.engine, self.semaphore, self.steps = engine, semaphore, 0

    def __call__(self, instruction):
        self.steps += 1
        instruction.then_inc(self.semaphore, 1)
        self.engine.wait_ge(self.semaphore, self.steps)


def identity(nc, pool, tile, made, first):
    pool.memset(tile, 0.0).then_inc(made, 1)
    pool.wait_ge(made, first + 1)
    pool.affine_select(out=tile, in_=tile, compare_op=ALU.not_equal, fill=1.0, base=0,
                       pattern=[[-1, P]], channel_multiplier=1).then_inc(made, 1)


def layer_statistics(nc, v, link, x, bn, mean, spread, tmp):
    def tiles(i):
        for k in range(8):
            last = nc.vector.bn_stats(bn[:, ds((i * 8 + k) * 6, 6)], x[:, ds((i * 8 + k) * C, C)])
        return last
    with v.Fori(0, TILES // 8 - 1) as i:
        tiles(i)
    link(tiles(TILES // 8 - 1))
    b = bn[:, :].rearrange("p (s k) -> p s k", k=6)
    link(nc.vector.tensor_tensor(mean, b[:, :, 1], b[:, :, 4], ALU.add))
    link(nc.vector.tensor_scalar(mean, mean, 0.5, None, ALU.mult))
    link(nc.vector.tensor_tensor(spread, b[:, :, 1], b[:, :, 4], ALU.subtract))
    link(nc.vector.scalar_tensor_tensor(out=spread, in0=spread, scalar=0.25, in1=spread,
                                        op0=ALU.mult, op1=ALU.mult))
    link(nc.vector.tensor_tensor(tmp, b[:, :, 2], b[:, :, 5], ALU.add))
    link(nc.vector.scalar_tensor_tensor(out=spread, in0=tmp, scalar=1.0 / C, in1=spread,
                                        op0=ALU.mult, op1=ALU.add))


def pair_bias(nc, sem, sb, A, X, PB, ident, mean, rstd):
    with ExitStack() as ctx:
        local = lambda n, s, d=F32: ctx.enter_context(nc.sbuf_tensor("sb_" + n, s, d))
        z = local("z", [P, T * CZ])
        sq = local("z_sq", [P, T * CZ])
        ztr = local("z_tr", [P, 2, BANK])
        zs = local("z_stat", [P, 4, T])
        bn = local("bn", [P, TILES * 6])
        wz = local("wz", [P, 2, HEADS])
        wzr = local("wzr", [P, 2])
        b_bc = local("b_bc", [CZ, P])
        pbc = local("pbc", [P, HEADS])
        tmp = local("stat_tmp", [P, 2, TILES])
        ptr = [ctx.enter_context(nc.psum_tensor(f"z_ptr{k}", [P, BANK], F32)) for k in range(2)]
        pzb = ctx.enter_context(nc.psum_tensor("pzb", [P, BANK], F32))
        pzb2 = ctx.enter_context(nc.psum_tensor("pzb2", [P, BANK], F32))
        pcc = ctx.enter_context(nc.psum_tensor("pcc", [P, BANK], F32))
        z_in, x_in, w_in = sem("z_in"), sem("x_in"), sem("zw_in")
        id_made, wz_zero = sem("id_made"), sem("wz_zero")
        zn, z_sq, z_rt, v_chain = sem("z_normal"), sem("z_squared"), sem("z_root"), sem("pair_chain")
        w_scaled = sem("wz_scaled")
        ztd, zev, zmm, const_mm = sem("z_transposed"), sem("z_evacuated"), sem("z_projected"), sem("pair_const")
        x_root = sem("x_root")
        x_var = sem("x_variance")
        block = ctx.enter_context(nc.Block())
        X2 = X[:, :, :].rearrange("p s c -> p (s c)")
        zz = z[:, :].rearrange("p (k c) -> p k c", c=CZ)
        sqz = sq[:, :].rearrange("p (k c) -> p k c", c=CZ)

        @block.sync
        def _(sp):
            sp.dma_start(z[:, :], A["z"][0].rearrange("q k c -> q (k c)")).then_inc(z_in, 16)
            sp.wait_ge(wz_zero, 1)
            for k in range(2):
                sp.dma_start(wz[k * CZ:(k + 1) * CZ, k, :], A["w_z"]).then_inc(w_in, 16)
                sp.dma_start(wzr[k * CZ:(k + 1) * CZ, 0:1], A["ln_z_w"].unsqueeze(1)).then_inc(w_in, 16)
            sp.dma_start(wzr[0:CZ, 1:2], A["ln_z_b"].unsqueeze(1)).then_inc(w_in, 16)
            sp.wait_ge(z_in, 16)
            sp.wait_ge(w_in, 80)

        @block.scalar
        def _(act):
            act.dma_start(X[:, :, :], A["x"][0].rearrange("s r c -> r s c")).then_inc(x_in, 16)
            act.wait_ge(zn, 1)
            nc.scalar.activation(sq[:, :], z[:, :], ACT.Square).then_inc(z_sq, 1)
            act.wait_ge(x_var, 1)
            nc.scalar.activation(tmp[:, 0, :], tmp[:, 1, :], ACT.Sqrt).then_inc(x_root, 1)
            act.wait_ge(x_var, 2)
            nc.scalar.activation(tmp[:, 0, :], tmp[:, 1, :], ACT.Sqrt).then_inc(x_root, 1)
            act.wait_ge(zn, 2)
            nc.scalar.activation(zs[:, 2, :], zs[:, 1, :], ACT.Sqrt).then_inc(z_rt, 1)
            act.wait_ge(x_in, 16)

        @block.gpsimd
        def _(pool):
            pool.memset(wz[:, :, :], 0.0).then_inc(wz_zero, 1)
            identity(nc, pool, ident[:, :], id_made, 0)

        @block.vector
        def _(v):
            link = Chain(v, v_chain)
            v.wait_ge(z_in, 16)
            link(nc.vector.tensor_reduce(zs[:, 0, :], zz, AX.X, ALU.add))
            link(nc.vector.tensor_scalar(zs[:, 0, :], zs[:, 0, :], 1.0 / CZ, None, ALU.mult))
            nc.vector.tensor_tensor(zz, zz, zs[:, 0, :].unsqueeze(2).to_broadcast([P, T, CZ]),
                                    ALU.subtract).then_inc(zn, 1)
            v.wait_ge(x_in, 16)
            layer_statistics(nc, v, link, X2, bn, mean, rstd, tmp[:, 0, :])
            link(nc.vector.tensor_scalar(tmp[:, 1, :], rstd, EPS_C, None, ALU.add))
            v.sem_inc(x_var, 1)
            v.wait_ge(x_root, 1)
            link(nc.vector.reciprocal(tmp[:, 0, :], tmp[:, 0, :]))
            link(nc.vector.tensor_tensor(tmp[:, 1, :], tmp[:, 0, :], tmp[:, 0, :], ALU.mult))
            link(nc.vector.tensor_tensor(tmp[:, 1, :], tmp[:, 1, :], rstd, ALU.mult))
            link(nc.vector.tensor_copy(rstd, tmp[:, 0, :]))
            link(nc.vector.tensor_scalar(tmp[:, 1, :], tmp[:, 1, :], EPS_T, None, ALU.add))
            v.sem_inc(x_var, 1)
            v.wait_ge(x_root, 2)
            link(nc.vector.reciprocal(tmp[:, 0, :], tmp[:, 0, :]))
            link(nc.vector.tensor_tensor(rstd, rstd, tmp[:, 0, :], ALU.mult))
            v.wait_ge(z_sq, 1)
            link(nc.vector.tensor_reduce(zs[:, 1, :], sqz, AX.X, ALU.add))
            v.wait_ge(zn, 1)
            nc.vector.tensor_scalar(zs[:, 1, :], zs[:, 1, :], 1.0 / CZ, EPS_T,
                                    ALU.mult, ALU.add).then_inc(zn, 1)
            v.wait_ge(z_rt, 1)
            link(nc.vector.reciprocal(zs[:, 3, :], zs[:, 2, :]))
            nc.vector.tensor_tensor(zz, zz, zs[:, 3, :].unsqueeze(2).to_broadcast([P, T, CZ]),
                                    ALU.mult).then_inc(zn, 1)
            v.wait_ge(w_in, 80)
            link(nc.vector.memset(b_bc[:, :], 1.0))
            nc.vector.tensor_scalar(b_bc[:, :], b_bc[:, :], wzr[0:CZ, 1:2], None, ALU.mult)\
                .then_inc(w_scaled, 1)
            v.wait_ge(const_mm, 1)
            link(nc.vector.tensor_copy(pbc[:, :], pcc[:, 0:HEADS]))
            nc.vector.tensor_scalar(wz[:, :, :], wz[:, :, :], wzr[:, 0:1], None, ALU.mult)\
                .then_inc(w_scaled, 1)
            for g in range(T * CZ // (GROUP * P)):
                v.wait_ge(ztd, g + 1)
                if g >= 2:
                    v.wait_ge(zmm, g - 1)
                nc.vector.tensor_copy(ztr[:, g % 2, :], ptr[g % 2][:, :]).then_inc(zev, 1)
            v.wait_ge(zmm, T * CZ // (GROUP * P))
            half = T // 2
            for n, bank in enumerate((pzb, pzb2)):
                for j in range(2):
                    link(nc.vector.tensor_tensor(
                        PB[:, :, n * half:(n + 1) * half].rearrange("p (r j) k -> p r j k", j=2)[:, :, j, :],
                        bank[:, :].rearrange("p (k j r) -> p j r k", j=2, r=4)[:, j, :, :],
                        pbc[:, j * 4:(j + 1) * 4].unsqueeze(2).to_broadcast([P, 4, half]), ALU.add))

        @block.tensor
        def _(pe):
            pe.wait_ge(w_scaled, 1)
            pe.wait_ge(w_in, 80)
            nc.tensor.matmul(pcc[:, 0:HEADS], b_bc[:, :], wz[0:CZ, 0, :], start=True, stop=True)\
                .then_inc(const_mm, 1)
            pe.wait_ge(id_made, 2)
            pe.wait_ge(w_scaled, 2)
            pe.wait_ge(zn, 3)
            n_groups = T * CZ // (GROUP * P)

            def turn(g):
                if g >= 2:
                    pe.wait_ge(zev, g - 1)
                for j in range(GROUP):
                    c = (g * GROUP + j) * P
                    last = nc.tensor.transpose(ptr[g % 2][:, j * P:(j + 1) * P], z[:, c:c + P], ident[:, :])
                last.then_inc(ztd, 1)

            def project(g):
                pe.wait_ge(zev, g + 1)
                for j in range(GROUP):
                    pair = g * GROUP + j
                    bank, col = (pzb, pair) if pair < 32 else (pzb2, pair - 32)
                    last = nc.tensor.matmul(bank[:, col * 16:col * 16 + 16],
                                            ztr[:, g % 2, j * P:(j + 1) * P],
                                            wz[:, :, :].rearrange("p a h -> p (a h)"), start=True, stop=True)
                last.then_inc(zmm, 1)

            turn(0)
            for g in range(1, n_groups):
                turn(g)
                project(g - 1)
            project(n_groups - 1)


def row_attention(nc, sem, sb, A, X, PB, ident, mean, rstd):
    with ExitStack() as ctx:
        local = lambda n, s, d=F32: ctx.enter_context(nc.sbuf_tensor("sb_" + n, s, d))
        bank = lambda n, s=(P, BANK): ctx.enter_context(nc.psum_tensor(n, list(s), F32))
        MB = local("mask_bias", [P, F * T])
        BM = local("bias", [P, 2, HEADS, T])
        wq, wk = local("wq", [C, HD]), local("wk", [C, HD])
        wvg = local("wvg", [C, 2 * HD])
        wo = local("wo", [P, 2, C])
        lnw, lnb = local("lnw", [C, 1]), local("lnb", [C, 1])
        ones = local("ones", [1, P])
        bg, bo = local("bg", [1, HD]), local("bo", [1, C])
        XN = local("xn", [P, C])
        SNT = local("snT", [C, T])
        QT, KT = local("qT", [P, 2, T]), local("kT", [P, 2, T])
        V, TH = local("v", [T, 2, HD]), local("gate", [T, 2, HD])
        LG = local("logits", [T, HEADS, T])
        PR = local("probs", [T, 2, HEADS, T])
        NM = local("neg_max", [T, HEADS])
        SM, RI = local("row_sum", [T, 2, HEADS]), local("inv_sum", [T, HEADS])
        PT = local("probsT", [T, HEADS, T])
        OG, OGT = local("gated", [T, HD]), local("gatedT", [P, 2, T])
        L = bank("p_logits", (P, 4, BANK))
        TA, TB_ = bank("p_ta"), bank("p_tb")
        PROJ, MISC = bank("p_proj"), bank("p_misc")
        w_in, m_in, ones_set = sem("att_w_in"), sem("mask_in"), sem("ones_set")
        mb_made = sem("mask_bias_made")
        bias_made = sem("bias_made")
        xn_made, xn_turned, sn_made = sem("xn_made"), sem("xn_turned"), sem("sn_made")
        qk_done, qk_out = sem("qk_done"), sem("qk_out")
        vg_done, v_out = sem("vg_done"), sem("v_out")
        score_done, logit_made, max_made, exp_done = sem("score_done"), sem("logit_made"), sem("max_made"), sem("exp_done")
        ta_done, tb_done, ta_out, tb_out = sem("ta_done"), sem("tb_done"), sem("ta_out"), sem("tb_out")
        pv_done, inv_made, og_raw, og_made = sem("pv_done"), sem("inv_made"), sem("og_raw"), sem("og_made")
        og_turned, ogt_out, out_done, x_added = sem("og_turned"), sem("ogt_out"), sem("out_done"), sem("x_added")
        block = ctx.enter_context(nc.Block())
        X2 = X[:, :, :].rearrange("p s c -> p (s c)")
        N_W = 10

        @block.sync
        def _(sp):
            sp.dma_start(MB[:, :], A["mask"][0].rearrange("s k -> (s k)").partition_broadcast(P)).then_inc(m_in, 16)
            for dst, src in ((wq[:, :], A["w_q"]), (wk[:, :], A["w_k"]), (wvg[:, 0:HD], A["w_v"]),
                             (wvg[:, HD:2 * HD], A["w_g"]),
                             (wo[:, :, :], A["w_o"].rearrange("(a p) c -> p a c", a=2)),
                             (lnw[:, :], A["ln_s_w"].unsqueeze(1)), (lnb[:, :], A["ln_s_b"].unsqueeze(1)),
                             (bg[:, :], A["b_g"].unsqueeze(0)), (bo[:, :], A["b_o"].unsqueeze(0))):
                sp.dma_start(dst, src).then_inc(w_in, 16)
            sp.wait_ge(w_in, 16 * 9)
            sp.wait_ge(m_in, 16)

        @block.gpsimd
        def _(pool):
            pool.wait_ge(m_in, 16)
            pool.tensor_scalar(MB[:, :], MB[:, :], 1.0, INF, ALU.subtract, ALU.mult).then_inc(mb_made, 1)
            pool.wait_ge(mb_made, 1)

            def bias(s, u):
                nc.gpsimd.tensor_tensor(
                    BM[:, u, :, :], PB[:, :, :],
                    MB[:, ds(s * T, T)].unsqueeze(1).to_broadcast([P, HEADS, T]), ALU.add).then_inc(bias_made, 1)

            bias(0, 0)
            bias(1, 1)
            with pool.Fori(0, F // 2 - 1) as it:
                for u in range(2):
                    pool.wait_ge(logit_made, it * 2 + u + 1)
                    bias(it * 2 + u + 2, u)

        @block.vector
        def _(v):
            nc.vector.memset(ones[:, :], 1.0).then_inc(ones_set, 1)
            v.wait_ge(w_in, 16 * 9)

            def normalise(s):
                nc.vector.tensor_scalar(XN[:, :], X2[:, ds(s * C, C)], mean[:, ds(s, 1)], rstd[:, ds(s, 1)],
                                        ALU.subtract, ALU.mult).then_inc(xn_made, 1)

            def scale_shift(s):
                v.wait_ge(xn_turned, s + 1)
                nc.vector.tensor_scalar(SNT[:, :], MISC[:, 0:T], lnw[:, :], lnb[:, :],
                                        ALU.mult, ALU.add).then_inc(sn_made, 1)

            def logits(s, u):
                v.wait_ge(score_done, s + 1)
                v.wait_ge(bias_made, s + 1)
                nc.vector.scalar_tensor_tensor(
                    out=LG[:, :, :].rearrange("p (r j) k -> p r (j k)", j=2),
                    in0=L[:, :, 0:2 * T], scalar=1.0 / math.sqrt(DH),
                    in1=BM[:, u, :, :].rearrange("p (r j) k -> p r (j k)", j=2),
                    op0=ALU.mult, op1=ALU.add).then_inc(logit_made, 1)
                v.wait_ge(logit_made, s + 1)
                nc.vector.tensor_reduce(NM[:, :], LG[:, :, :], AX.X, ALU.max, negate=True).then_inc(max_made, 1)

            def finish(s, u, first=False):
                v.wait_ge(exp_done, s + 1)
                nc.vector.reciprocal(RI[:, :], SM[:, u, :]).then_inc(inv_made, 1)
                v.wait_ge(tb_done, s + 1)
                nc.vector.tensor_copy(PT[:, 4:8, :], TB_[:, :].rearrange("p (h k) -> p h k", k=T)).then_inc(tb_out, 1)
                v.wait_ge(pv_done, s + 1)
                v.wait_ge(v_out, s + 1)
                nc.vector.scalar_tensor_tensor(out=OG[:, :], in0=TH[:, u, :], scalar=1.0, in1=MISC[:, 0:HD],
                                               op0=ALU.add, op1=ALU.mult).then_inc(og_raw, 1)
                v.wait_ge(og_raw, s + 1)
                v.wait_ge(inv_made, s + 1)
                nc.vector.scalar_tensor_tensor(
                    out=OG[:, :].rearrange("p (h d) -> p h d", d=DH), in0=OG[:, :].rearrange("p (h d) -> p h d", d=DH),
                    scalar=0.5, in1=RI[:, :].unsqueeze(2).to_broadcast([P, HEADS, DH]),
                    op0=ALU.mult, op1=ALU.mult).then_inc(og_made, 1)
                v.wait_ge(og_turned, s + 1)
                nc.vector.tensor_copy(OGT[:, :, :], MISC[:, 0:HD].rearrange("p (a q) -> p a q", a=2)).then_inc(ogt_out, 1)
                v.wait_ge(out_done, s + 1)
                xs = X2[:, ds(s * C, C)]
                nc.vector.tensor_tensor(xs, MISC[:, 0:C], xs, ALU.add).then_inc(x_added, 1)

            normalise(0)
            scale_shift(0)
            logits(0, 0)
            v.wait_ge(xn_turned, 1)
            normalise(1)
            scale_shift(1)
            with v.Fori(0, F // 2 - 1) as it:
                for u in range(2):
                    s = it * 2 + 1 + u
                    logits(s, (1 + u) % 2)
                    finish(s - 1, u)
                    v.wait_ge(xn_turned, s + 1)
                    normalise(s + 1)
                    scale_shift(s + 1)
            logits(F - 1, 1)
            finish(F - 2, 0)
            finish(F - 1, 1)

        @block.scalar
        def _(act):
            def projections(s, u):
                act.wait_ge(qk_done, s + 1)
                nc.scalar.activation(QT[:, :, :], PROJ[:, 0:HD].rearrange("p (a q) -> p a q", a=2), ACT.Copy)
                nc.scalar.activation(KT[:, :, :], PROJ[:, HD:2 * HD].rearrange("p (a q) -> p a q", a=2), ACT.Copy)\
                    .then_inc(qk_out, 1)
                act.wait_ge(vg_done, s + 1)
                nc.scalar.activation(V[:, u, :], PROJ[:, 0:HD], ACT.Copy)
                nc.scalar.activation(TH[:, u, :], PROJ[:, HD:2 * HD], ACT.Tanh, scale=0.5).then_inc(v_out, 1)

            def softmax(s, u):
                act.wait_ge(max_made, s + 1)
                if not (isinstance(s, int) and s < 2):
                    act.wait_ge(tb_done, s - 1)
                    act.wait_ge(inv_made, s - 1)
                for r in range(4):
                    for j in range(2):
                        last = nc.scalar.activation(PR[:, u, 2 * r + j, :], LG[:, 2 * r + j, :], ACT.Exp,
                                                    bias=NM[:, 2 * r + j:2 * r + j + 1],
                                                    accum_out=SM[:, u, r + 4 * j:r + 4 * j + 1])
                last.then_inc(exp_done, 1)

            def turned(s):
                act.wait_ge(ta_done, s + 1)
                nc.scalar.activation(PT[:, 0:4, :], TA[:, :].rearrange("p (h k) -> p h k", k=T), ACT.Copy).then_inc(ta_out, 1)

            projections(0, 0)
            softmax(0, 0)
            projections(1, 1)
            with act.Fori(0, F // 2 - 1) as it:
                for u in range(2):
                    s = it * 2 + 1 + u
                    turned(s - 1)
                    act.wait_ge(pv_done, s)
                    act.wait_ge(og_raw, s)
                    softmax(s, (1 + u) % 2)
                    projections(s + 1, u)
            turned(F - 2)
            softmax(F - 1, 1)
            turned(F - 1)

        @block.tensor
        def _(pe):
            pe.wait_ge(w_in, 16 * 9)
            pe.wait_ge(ones_set, 1)

            def project(s, before):
                pe.wait_ge(xn_made, s + 1)
                if before is not None:
                    pe.wait_ge(x_added, before)
                nc.tensor.transpose(MISC[:, 0:T], XN[:, :], ident[:, :]).then_inc(xn_turned, 1)
                pe.wait_ge(sn_made, s + 1)
                if not (isinstance(s, int) and s == 0):
                    pe.wait_ge(v_out, s)
                for a in range(2):
                    nc.tensor.matmul(PROJ[:, a * T:(a + 1) * T], wq[:, a * P:(a + 1) * P], SNT[:, :], start=True, stop=True)
                for a in range(2):
                    last = nc.tensor.matmul(PROJ[:, (2 + a) * T:(3 + a) * T], wk[:, a * P:(a + 1) * P], SNT[:, :],
                                            start=True, stop=True)
                last.then_inc(qk_done, 1)

            def project_vg(s):
                pe.wait_ge(qk_out, s + 1)
                nc.tensor.matmul(PROJ[:, :], SNT[:, :], wvg[:, :], start=True, stop=False)
                nc.tensor.matmul(PROJ[:, HD:2 * HD], ones[:, :], bg[:, :], start=False, stop=True).then_inc(vg_done, 1)

            def score(s):
                pe.wait_ge(qk_out, s + 1)
                if not (isinstance(s, int) and s == 0):
                    pe.wait_ge(logit_made, s)
                for j in range(2):
                    for r in range(4):
                        rows = slice(r * DH, (r + 1) * DH)
                        last = nc.tensor.matmul(L[:, r, j * T:(j + 1) * T], QT[rows, j, :], KT[rows, j, :],
                                                start=True, stop=True, tile_position=(r * DH, 0))
                last.then_inc(score_done, 1)

            def turn(s, u):
                pe.wait_ge(exp_done, s + 1)
                for h in range(4):
                    last = nc.tensor.transpose(TA[:, h * T:(h + 1) * T], PR[:, u, h, :], ident[:, :])
                last.then_inc(ta_done, 1)
                for h in range(4):
                    last = nc.tensor.transpose(TB_[:, h * T:(h + 1) * T], PR[:, u, 4 + h, :], ident[:, :])
                last.then_inc(tb_done, 1)

            def attend(s, u):
                pe.wait_ge(ta_out, s + 1)
                pe.wait_ge(v_out, s + 1)
                for slot in range(8):
                    if slot == 4:
                        pe.wait_ge(tb_out, s + 1)
                    h = slot // 2 + 4 * (slot % 2)
                    last = nc.tensor.matmul(MISC[:, h * DH:(h + 1) * DH], PT[:, slot, :], V[:, u, h * DH:(h + 1) * DH],
                                            start=True, stop=True)
                last.then_inc(pv_done, 1)

            def project_out(s):
                pe.wait_ge(og_made, s + 1)
                for a in range(2):
                    last = nc.tensor.transpose(MISC[:, a * T:(a + 1) * T], OG[:, a * P:(a + 1) * P], ident[:, :])
                last.then_inc(og_turned, 1)
                pe.wait_ge(ogt_out, s + 1)
                for a in range(2):
                    nc.tensor.matmul(MISC[:, 0:C], OGT[:, a, :], wo[:, a, :], start=(a == 0), stop=False)
                nc.tensor.matmul(MISC[:, 0:C], ones[:, :], bo[:, :], start=False, stop=True).then_inc(out_done, 1)

            project(0, None)
            project_vg(0)
            score(0)
            pe.wait_ge(sn_made, 1)
            project(1, None)
            project_vg(1)
            with pe.Fori(0, F // 2 - 1) as it:
                for u in range(2):
                    s = it * 2 + 1 + u
                    score(s)
                    turn(s - 1, u)
                    attend(s - 1, u)
                    project_out(s - 1)
                    project(s + 1, s)
                    project_vg(s + 1)
            score(F - 1)
            turn(F - 2, 0)
            attend(F - 2, 0)
            project_out(F - 2)
            pe.wait_ge(x_added, F - 1)
            turn(F - 1, 1)
            attend(F - 1, 1)
            project_out(F - 1)


def compact_edges(nc, sem, A, KG, KC, CN, n_general, n_clamped):
    with ExitStack() as ctx:
        local = lambda n, s, d=F32: ctx.enter_context(nc.sbuf_tensor("sb_" + n, s, d))
        SRC, DST = local("src", [P, ECOLS], I32), local("dst", [P, ECOLS], I32)
        TMP = local("key_tmp", [P, ECOLS], I32)
        CNT = local("counts", [P, 2 * BLOCKS])
        CNA = local("counts_max", [P, 2 * BLOCKS])
        PASS = local("passes", [P, 2, BLOCKS + 1], I32)
        M8, JOIN = local("max8", [P, SLOT]), local("join", [P, 1])
        iota_i = local("iota_i", [P, P], I32)
        LOHI = local("cl_lohi", [P, 2, 2 * SLOT], I32)
        OL, OH = local("onehot_lo", [P, 2, SLOT, P], BF16), local("onehot_hi", [P, 2, SLOT, TILES], BF16)
        pc = ctx.enter_context(nc.psum_tensor("p_count", [P, BANK], F32))
        e_in, chain, counted, summed, iota_made = sem("edges_in"), sem("edge_chain"), sem("counted"), sem("count_max"), sem("iota_made")
        passes_made = sem("passes_made")
        maxed = [[sem(f"maxed{b}{k}") for k in range(2)] for b in range(BLOCKS)]
        slotted, zeroed, taken = sem("slotted"), sem("zeroed"), sem("taken")
        decoded, hot_made, hot_used, cn_done = sem("cl_decoded"), sem("hot_made"), sem("hot_used"), sem("cn_done")
        block = ctx.enter_context(nc.Block())
        KEY = SRC[:, :].bitcast(F32)

        @block.sync
        def _(sp):
            sp.dma_start(SRC[:, :], A["edge_index"][0].rearrange("(p e) -> p e", p=P)).then_inc(e_in, 16)
            sp.dma_start(DST[:, :], A["edge_index"][1].rearrange("(p e) -> p e", p=P)).then_inc(e_in, 16)
            sp.wait_ge(e_in, 32)

        @block.gpsimd
        def _(pool):
            pool.memset(KG[:, :], 0.0)
            pool.memset(KC[:, :], 0.0).then_inc(zeroed, 1)
            pool.iota(iota_i[:, :], pattern=[[1, P]], base=0, channel_multiplier=0).then_inc(iota_made, 1)
            pool.wait_ge(counted, 1)
            pool.partition_all_reduce(CNA[:, :], CNT[:, :], P, bass.bass_isa.ReduceOp.max).then_inc(summed, 1)

        @block.vector
        def _(v):
            link = Chain(v, chain)
            v.wait_ge(e_in, 32)
            link(nc.vector.tensor_scalar(TMP[:, :], SRC[:, :], TOKENS - 1, NEAR >> NODE_BITS, ALU.is_lt, ALU.mult))
            link(nc.vector.tensor_scalar(SRC[:, :], SRC[:, :], TOKENS - 1, None, ALU.min))
            link(nc.vector.scalar_tensor_tensor(out=TMP[:, :], in0=TMP[:, :], scalar=VALID >> NODE_BITS,
                                                in1=DST[:, :], op0=ALU.add, op1=ALU.add))
            link(nc.vector.tensor_scalar(TMP[:, :], TMP[:, :], NODE_BITS, None, ALU.logical_shift_left))
            link(nc.vector.tensor_scalar(DST[:, :], DST[:, :], TOKENS, -1, ALU.is_lt, ALU.mult))
            link(nc.vector.tensor_tensor(SRC[:, :], SRC[:, :], TMP[:, :], ALU.bitwise_or))
            link(nc.vector.tensor_tensor(SRC[:, :], SRC[:, :], DST[:, :], ALU.bitwise_and))
            link(nc.vector.tensor_scalar(TMP[:, :], SRC[:, :], 4, None, ALU.logical_shift_right))
            link(nc.vector.tensor_scalar(TMP[:, :], TMP[:, :], 22, 1, ALU.logical_shift_right, ALU.bitwise_and))
            link(nc.vector.tensor_reduce(CNT[:, 0:BLOCKS], TMP[:, :].rearrange("p (b e) -> p b e", b=BLOCKS), AX.X, ALU.add))
            link(nc.vector.tensor_reduce(CNT[:, BLOCKS:], DST[:, :].rearrange("p (b e) -> p b e", b=BLOCKS), AX.X, ALU.add))
            nc.vector.tensor_scalar(CNT[:, BLOCKS:], CNT[:, BLOCKS:], -1.0, None, ALU.mult).then_inc(counted, 1)
            v.wait_ge(summed, 1)
            both = PASS[:, :, 0:BLOCKS]
            link(nc.vector.tensor_scalar(both, CNA[:, :].rearrange("p (a b) -> p a b", a=2), 7.0, None, ALU.add))
            link(nc.vector.tensor_scalar(both, both, 3, None, ALU.logical_shift_right))
            link(nc.vector.tensor_scalar(PASS[:, 0, 0:BLOCKS], PASS[:, 0, 0:BLOCKS], 1, None, ALU.max))
            link(nc.vector.tensor_tensor(PASS[:, 1, 0:BLOCKS], PASS[:, 1, 0:BLOCKS], PASS[:, 0, 0:BLOCKS], ALU.subtract))
            link(nc.vector.tensor_scalar(PASS[:, 1, 0:BLOCKS], PASS[:, 1, 0:BLOCKS], 1, None, ALU.max))
            with nc.allow_low_precision("small whole numbers"):
                link(nc.vector.tensor_reduce(PASS[:, :, BLOCKS:], both, AX.X, ALU.add))
            link(nc.vector.tensor_scalar(PASS[:, :, BLOCKS:], PASS[:, :, BLOCKS:], 1, None, ALU.add))
            link(nc.vector.tensor_scalar(PASS[:, :, BLOCKS:], PASS[:, :, BLOCKS:], 1, None, ALU.logical_shift_right))
            nc.vector.tensor_copy(n_general[:, :], PASS[:, :, BLOCKS:]).then_inc(passes_made, 1)
            v.wait_ge(passes_made, 1)
            v.wait_ge(zeroed, 1)
            at = [0, 0]
            for b in range(BLOCKS):
                keys = KEY[:, b * BCOLS:(b + 1) * BCOLS]
                for kind, KEEP in enumerate((KG, KC)):
                    n = v.value_load(PASS[0:1, kind, b:b + 1], min_val=1, max_val=BCOLS // SLOT)
                    base = at[kind]
                    with v.Fori(0, n) as i:
                        v.wait_ge(maxed[b][kind], i * 2)
                        v.sem_inc(taken, 1)
                        nc.vector.max(M8[:, :], keys).then_inc(maxed[b][kind], 1)
                        v.wait_ge(maxed[b][kind], i * 2 + 1)
                        v.sem_inc(taken, 1)
                        nc.vector.match_replace(keys, M8[:, :], keys, 0.0)
                        nc.vector.tensor_copy(KEEP[:, ds((base + i) * SLOT, SLOT)], M8[:, :])\
                            .then_inc(maxed[b][kind], 1)
                    link(nc.vector.memset(JOIN[:, :], 0.0))
                    at[kind] = at[kind] + n
            v.sem_inc(slotted, 1)
            v.wait_ge(iota_made, 1)

            def decode(i):
                bits = KC[:, ds(i * 2 * SLOT, 2 * SLOT)].bitcast(I32)
                nc.vector.tensor_scalar(LOHI[:, 0, :], bits, NODE_BITS, P - 1, ALU.logical_shift_right, ALU.bitwise_and)
                nc.vector.tensor_scalar(LOHI[:, 1, :], bits, NODE_BITS + LO_BITS, (VALID >> 20) + TILES - 1,
                                        ALU.logical_shift_right, ALU.bitwise_and).then_inc(decoded, 1)

            nc_pairs = v.value_load(n_general[0:1, 1, 0:1], min_val=1, max_val=ECOLS // (2 * SLOT) + BLOCKS)
            with v.Fori(0, nc_pairs) as i:
                v.wait_ge(hot_made, i * 2)
                decode(i)
                v.wait_ge(decoded, i * 2 + 1)
                nc.vector.tensor_scalar(LOHI[:, 1, :], LOHI[:, 1, :], VALID >> 20, None, ALU.subtract).then_inc(decoded, 1)
                v.wait_ge(decoded, i * 2 + 2)
                for u in range(2):
                    v.wait_ge(hot_used, i * 2 + u)
                    sl = slice(u * SLOT, (u + 1) * SLOT)
                    nc.vector.tensor_tensor(OL[:, u, :, :], iota_i[:, :].unsqueeze(1).to_broadcast([P, SLOT, P]),
                                            LOHI[:, 0, sl].unsqueeze(2).to_broadcast([P, SLOT, P]), ALU.is_equal)
                    nc.vector.tensor_tensor(OH[:, u, :, :], iota_i[:, 0:TILES].unsqueeze(1).to_broadcast([P, SLOT, TILES]),
                                            LOHI[:, 1, sl].unsqueeze(2).to_broadcast([P, SLOT, TILES]),
                                            ALU.is_equal).then_inc(hot_made, 1)
            v.wait_ge(cn_done, 1)
            link(nc.vector.tensor_copy(CN[:, :], pc[:, 0:TILES]))

        @block.tensor
        def _(pe):
            pe.wait_ge(passes_made, 1)
            pe.wait_ge(zeroed, 1)
            nc_pairs = pe.value_load(n_general[0:1, 1, 0:1], min_val=1, max_val=ECOLS // (2 * SLOT) + BLOCKS)
            zero = KC[:, KC.shape[1] - P:].bitcast(BF16)
            nc.tensor.matmul(pc[:, 0:TILES], zero[:, 0:P], zero[:, 0:TILES], start=True, stop=False, skip_group_check=True)
            with pe.Fori(0, nc_pairs) as i:
                for u in range(2):
                    pe.wait_ge(hot_made, i * 2 + u + 1)
                    for k in range(SLOT):
                        last = nc.tensor.matmul(pc[:, 0:TILES], OL[:, u, k, :], OH[:, u, k, :], start=False, stop=False,
                                                skip_group_check=True)
                    last.then_inc(hot_used, 1)
            nc.tensor.matmul(pc[:, 0:TILES], zero[:, 0:P], zero[:, 0:TILES], start=False, stop=True,
                             skip_group_check=True).then_inc(cn_done, 1)


def turn_tokens(nc, sem, tag, ctx, X2, ident, mean, rstd, TT, W, width, OUT, eps, load_w):
    local = lambda n, s, d=F32: ctx.enter_context(nc.sbuf_tensor(f"sb_{tag}_{n}", s, d))
    pbank = lambda n: ctx.enter_context(nc.psum_tensor(f"{tag}_{n}", [P, BANK], F32))
    XN = local("xn", [P, 2, BANK])
    SG = local("sg", [P, 2, BANK])
    bn = local("bn", [P, TILES * 6])
    tmp = local("tmp", [P, 2, TILES])
    pt = [pbank(f"pt{k}") for k in range(2)]
    ph = [pbank(f"ph{k}") for k in range(2)]
    w_in, chain, var, root = sem(tag + "_w_in"), sem(tag + "_chain"), sem(tag + "_var"), sem(tag + "_root")
    normed, turned, staged, kept = (sem(f"{tag}_{n}") for n in ("normed", "turned", "staged", "kept"))
    mixed, mixed_out = sem(tag + "_mixed"), sem(tag + "_mixed_out")
    block = ctx.enter_context(nc.Block())

    @block.sync
    def _(sp):
        sp.dma_start(W, load_w, allow_slow_non_contiguous=True).then_inc(w_in, 16)
        sp.wait_ge(w_in, 16)

    @block.scalar
    def _(act):
        act.wait_ge(var, 1)
        nc.scalar.activation(tmp[:, 0, :], tmp[:, 1, :], ACT.Sqrt).then_inc(root, 1)
        with act.Fori(0, GROUPS // 2) as i:
            for u in range(2):
                g = i * 2 + u
                act.wait_ge(turned, g + 1)
                nc.scalar.activation(TT[:, ds(g * BANK, BANK)], pt[u][:, :], ACT.Copy)
                act.wait_ge(mixed, i * 2)
                nc.scalar.activation(SG[:, u, :], pt[u][:, :], ACT.Copy).then_inc(staged, 1)

    @block.vector
    def _(v):
        link = Chain(v, chain)
        layer_statistics(nc, v, link, X2, bn, mean, rstd, tmp[:, 0, :])
        link(nc.vector.tensor_scalar(tmp[:, 1, :], rstd, eps, None, ALU.add))
        v.sem_inc(var, 1)
        v.wait_ge(root, 1)
        link(nc.vector.reciprocal(rstd, tmp[:, 0, :]))

        def out(g, u):
            v.wait_ge(mixed, g + 1)
            nc.vector.tensor_copy(OUT[:, ds(g * GROUP, GROUP), :],
                                  ph[u][:, 0:GROUP * width].rearrange("p (t w) -> p t w", w=width)).then_inc(mixed_out, 1)

        with v.Fori(0, GROUPS // 2) as i:
            for u in range(2):
                g = i * 2 + u
                v.wait_ge(turned, i * 2)
                for k in range(GROUP):
                    t = g * GROUP + k
                    last = nc.vector.tensor_scalar(XN[:, u, k * P:(k + 1) * P], X2[:, ds(t * C, C)],
                                                   mean[:, ds(t, 1)], rstd[:, ds(t, 1)], ALU.subtract, ALU.mult)
                last.then_inc(normed, 1)
            for u in range(2):
                out(i * 2 + u, u)

    @block.tensor
    def _(pe):
        pe.wait_ge(w_in, 16)
        with pe.Fori(0, GROUPS // 2) as i:
            for u in range(2):
                g = i * 2 + u
                pe.wait_ge(normed, g + 1)
                pe.wait_ge(staged, i * 2 + u - 1 if False else i * 2)
                for k in range(GROUP):
                    last = nc.tensor.transpose(pt[u][:, k * P:(k + 1) * P], XN[:, u, k * P:(k + 1) * P], ident[:, :])
                last.then_inc(turned, 1)
            for u in range(2):
                g = i * 2 + u
                pe.wait_ge(staged, g + 1)
                pe.wait_ge(mixed_out, i * 2)
                for k in range(GROUP):
                    last = nc.tensor.matmul(ph[u][:, k * width:(k + 1) * width], SG[:, u, k * P:(k + 1) * P], W,
                                            start=True, stop=True)
                last.then_inc(mixed, 1)


def graph_tables(nc, sem, A, H, GT, SRC_T, DST_T, LAST):
    with ExitStack() as ctx:
        local = lambda n, s, d=F32: ctx.enter_context(nc.sbuf_tensor("sb_gt_" + n, s, d))
        ATT = local("att", [P, 2, GF])
        PROD = local("prod", [P, TILES, GF])
        S, D = local("s", [P, TILES, GHEADS]), local("d", [P, TILES, GHEADS])
        M = local("m", [P, TILES, GHEADS])
        TOP, TOPA = local("top", [P, GHEADS]), local("topa", [P, GHEADS])
        ROWS = local("rows", [P, TILES, ROW])
        a_in, chain, topped, topped_all = sem("att_in"), sem("gt_chain"), sem("top"), sem("top_all")
        args, exps, rows_in, stored, last_in = sem("gt_args"), sem("gt_exps"), sem("gt_rows"), sem("gt_stored"), sem("last_in")
        block = ctx.enter_context(nc.Block())

        @block.sync
        def _(sp):
            for k, n in enumerate(("att_src", "att_dst")):
                sp.dma_start(ATT[:, k, :], A[n].rearrange("h e -> (h e)").partition_broadcast(P)).then_inc(a_in, 16)
            sp.wait_ge(rows_in, 1)
            sp.wait_ge(exps, 4)
            sp.dma_start(SRC_T.rearrange("(s r) w -> r s w", r=P), ROWS[:, :, :]).then_inc(stored, 16)
            sp.dma_start(DST_T.rearrange("(s r) w -> r s w", r=P), GT[:, :, 2 * GHEADS:]).then_inc(stored, 16)
            sp.wait_ge(stored, 32)
            sp.dma_start(LAST[:, :], SRC_T[TOKENS - 1, :].partition_broadcast(P)).then_inc(last_in, 16)
            sp.wait_ge(last_in, 16)

        @block.gpsimd
        def _(pool):
            pool.wait_ge(topped, 1)
            pool.partition_all_reduce(TOPA[:, :], TOP[:, :], P, bass.bass_isa.ReduceOp.max).then_inc(topped_all, 1)

        @block.scalar
        def _(act):
            act.wait_ge(args, 1)
            nc.scalar.activation(GT[:, :, 0:4], S[:, :, :], ACT.Exp).then_inc(exps, 1)
            nc.scalar.activation(GT[:, :, 4:8], S[:, :, :], ACT.Exp, scale=0.2).then_inc(exps, 1)
            act.wait_ge(args, 2)
            nc.scalar.activation(GT[:, :, 8:12], M[:, :, :], ACT.Exp).then_inc(exps, 1)
            nc.scalar.activation(GT[:, :, 12:16], D[:, :, :], ACT.Exp).then_inc(exps, 1)

        @block.vector
        def _(v):
            link = Chain(v, chain)
            v.wait_ge(a_in, 32)
            for k, dst in enumerate((S, D)):
                link(nc.vector.tensor_tensor(PROD[:, :, :], H[:, :, :], ATT[:, k, :].unsqueeze(1).to_broadcast([P, TILES, GF]),
                                             ALU.mult))
                link(nc.vector.tensor_reduce(dst[:, :, :], PROD[:, :, :].rearrange("p s (h e) -> p s h e", e=EXPERTS0),
                                             AX.X, ALU.add))
            link(nc.vector.tensor_reduce(TOP[:, :], S[:, :, :].rearrange("p s h -> p h s"), AX.X, ALU.max))
            v.sem_inc(topped, 1)
            v.wait_ge(topped_all, 1)
            top = TOPA[:, :].unsqueeze(1).to_broadcast([P, TILES, GHEADS])
            link(nc.vector.tensor_tensor(S[:, :, :], S[:, :, :], top, ALU.subtract))
            v.sem_inc(args, 1)
            link(nc.vector.tensor_tensor(D[:, :, :], D[:, :, :], top, ALU.add))
            link(nc.vector.scalar_tensor_tensor(out=M[:, :, :], in0=D[:, :, :], scalar=0.2, in1=D[:, :, :],
                                                op0=ALU.mult, op1=ALU.max))
            link(nc.vector.tensor_tensor(PROD[:, :, 0:4], D[:, :, :], M[:, :, :], ALU.subtract))
            link(nc.vector.scalar_tensor_tensor(out=D[:, :, :], in0=D[:, :, :], scalar=0.2, in1=M[:, :, :],
                                                op0=ALU.mult, op1=ALU.subtract))
            link(nc.vector.tensor_copy(M[:, :, :], PROD[:, :, 0:4]))
            v.sem_inc(args, 1)
            link(nc.vector.tensor_copy(ROWS[:, :, 0:GF], H[:, :, :]))
            v.wait_ge(exps, 2)
            nc.vector.tensor_copy(ROWS[:, :, GF:], GT[:, :, 0:8]).then_inc(rows_in, 1)


def graph_edges(nc, sem, KG, SRC_T, DST_T, n_passes, SUMS):
    with ExitStack() as ctx:
        local = lambda n, s, d=F32: ctx.enter_context(nc.sbuf_tensor("sb_ge_" + n, s, d))
        iota_i = local("iota_i", [P, P], I32)
        iota_f = local("iota_f", [P, P])
        IDX = local("idx", [P, 2, 2, SLOT], I32)
        LO, HI = local("lo", [P, 2, SLOT], I32), local("hi", [P, 2, SLOT], I32)
        HIF = local("hif", [P, 2, SLOT])
        GS, GD = local("gs", [P, 2, SLOT, ROW]), local("gd", [P, 2, SLOT, 2 * GHEADS])
        W2 = local("w2", [P, SLOT, 2 * GHEADS])
        MSG = local("msg", [P, SLOT, PART])
        OL = local("ol", [P, 2, SLOT, P])
        NB = 4
        B = local("b", [P, NB, TILES, PART])
        CHUNKS = ((0, 22), (22, 22), (44, 20))
        ACC = ctx.enter_context(nc.psum_tensor("acc", [P, 3, BANK], F32))
        gathers_on, iota_made = sem("ge_gathers_on"), sem("ge_iota")
        iota_cast = sem("ge_iota_cast")
        decoded, gathered_s, gathered_d = sem("ge_decoded"), [sem(f"ge_src{u}") for u in range(2)], [sem(f"ge_dst{u}") for u in range(2)]
        products, weights, messages, ol_made = sem("ge_products"), sem("ge_weights"), sem("ge_messages"), sem("ge_ol")
        b_made, b_free, half_used, acc_done, chain = sem("ge_b_made"), sem("ge_b_free"), sem("ge_half_used"), sem("ge_done"), sem("ge_chain")
        block = ctx.enter_context(nc.Block())
        limit = ECOLS // (2 * SLOT) + BLOCKS

        @block.gpsimd
        def _(pool):
            pool.iota(iota_i[:, :], pattern=[[1, P]], base=0, channel_multiplier=0).then_inc(iota_made, 1)
            n = pool.value_load(n_passes, min_val=1, max_val=limit)
            with pool.Fori(0, n) as i:
                for u in range(2):
                    pool.wait_ge(decoded, i * 2 + u + 1)
                    pool.wait_ge(messages, i * 2)
                    pool.sem_inc(gathers_on, 1)
                    for k in range(SLOT):
                        pool.indirect_dma_start(GS[:, u, k, :], None, SRC_T,
                                                bass.IndirectOffsetOnAxis(ap=IDX[:, u, 0, k:k + 1], axis=0)).then_inc(gathered_s[u], 16)
                        pool.indirect_dma_start(GD[:, u, k, :], None, DST_T,
                                                bass.IndirectOffsetOnAxis(ap=IDX[:, u, 1, k:k + 1], axis=0)).then_inc(gathered_d[u], 16)

        @block.vector
        def _(v):
            v.wait_ge(iota_made, 1)
            nc.vector.tensor_copy(iota_f[:, :], iota_i[:, :]).then_inc(iota_cast, 1)

            def decode(n, u):
                bits = KG[:, ds(n * SLOT, SLOT)].bitcast(I32)
                nc.vector.tensor_scalar(IDX[:, u, 0, :], bits, TOKENS - 1, None, ALU.bitwise_and)
                nc.vector.tensor_scalar(IDX[:, u, 1, :], bits, NODE_BITS, TOKENS - 1, ALU.logical_shift_right, ALU.bitwise_and)
                nc.vector.tensor_scalar(LO[:, u, :], bits, NODE_BITS, P - 1, ALU.logical_shift_right, ALU.bitwise_and)
                nc.vector.tensor_scalar(HI[:, u, :], bits, NODE_BITS + LO_BITS, (VALID >> 20) + TILES - 1,
                                        ALU.logical_shift_right, ALU.bitwise_and).then_inc(decoded, 1)

            n_iter = v.value_load(n_passes, min_val=1, max_val=limit)
            v.wait_ge(iota_cast, 1)
            decode(0, 0)
            decode(1, 1)
            with v.Fori(0, n_iter) as i:
                for u in range(2):
                    n = i * 2 + u
                    v.wait_ge(decoded, n + 1)
                    v.wait_ge(half_used, i * 2)
                    nc.vector.tensor_scalar(HIF[:, u, :], HI[:, u, :], VALID >> 20, None, ALU.subtract)
                    nc.vector.tensor_tensor(OL[:, u, :, :], iota_f[:, :].unsqueeze(1).to_broadcast([P, SLOT, P]),
                                            LO[:, u, :].unsqueeze(2).to_broadcast([P, SLOT, P]), ALU.is_equal).then_inc(ol_made, 1)
                    v.wait_ge(gathered_s[u], (i + 1) * 16 * SLOT)
                    v.wait_ge(gathered_d[u], (i + 1) * 16 * SLOT)
                    v.wait_ge(messages, n)
                    nc.vector.tensor_tensor(W2[:, :, :], GS[:, u, :, GF:], GD[:, u, :, :], ALU.mult).then_inc(products, 1)
                    v.wait_ge(products, n + 1)
                    v.wait_ge(b_made, n * SLOT)
                    nc.vector.tensor_tensor(MSG[:, :, GF:], W2[:, :, 0:GHEADS], W2[:, :, GHEADS:], ALU.max).then_inc(weights, 1)
                    v.wait_ge(weights, n + 1)
                    nc.vector.tensor_tensor(MSG[:, :, 0:GF].rearrange("p k (h e) -> p k h e", e=EXPERTS0),
                                            GS[:, u, :, 0:GF].rearrange("p k (h e) -> p k h e", e=EXPERTS0),
                                            MSG[:, :, GF:].unsqueeze(3).to_broadcast([P, SLOT, GHEADS, EXPERTS0]),
                                            ALU.mult).then_inc(messages, 1)
                    v.wait_ge(messages, n + 1)
                    for k in range(SLOT):
                        v.wait_ge(b_free, n * SLOT + k + 1)
                        nc.vector.scalar_tensor_tensor(
                            out=B[:, k % NB, :, :], in0=iota_f[:, 0:TILES].unsqueeze(2).to_broadcast([P, TILES, PART]),
                            scalar=HIF[:, u, k:k + 1], in1=MSG[:, k, :].unsqueeze(1).to_broadcast([P, TILES, PART]),
                            op0=ALU.is_equal, op1=ALU.mult).then_inc(b_made, 1)
                    v.wait_ge(b_made, (n + 1) * SLOT)
                    decode(n + 2, u)
            v.wait_ge(acc_done, 1)
            for c, (h0, hn) in enumerate(CHUNKS):
                last = nc.vector.tensor_copy(SUMS[:, h0:h0 + hn, :], ACC[:, c, 0:hn * PART].rearrange("p (h w) -> p h w", w=PART))
            last.then_inc(chain, 1)
            v.wait_ge(chain, 1)

        @block.tensor
        def _(pe):
            n_iter = pe.value_load(n_passes, min_val=1, max_val=limit)
            zero = KG[:, KG.shape[1] - P:]

            def add(left, right, **flags):
                for c, (h0, hn) in enumerate(CHUNKS):
                    last = nc.tensor.matmul(ACC[:, c, 0:hn * PART], left, right(h0, hn), skip_group_check=True, **flags)
                return last

            zeros = lambda h0, hn: zero.unsqueeze(1).to_broadcast([P, 4, P]).rearrange("p a b -> p a b")[:, :, 0:hn * 5]
            pe.sem_inc(b_free, NB)
            add(zero, zeros, start=True, stop=False)
            with pe.Fori(0, n_iter) as i:
                for u in range(2):
                    n = i * 2 + u
                    pe.wait_ge(ol_made, n + 1)
                    for k in range(SLOT):
                        pe.wait_ge(b_made, n * SLOT + k + 1)
                        b = B[:, k % NB, :, :].rearrange("p h w -> p (h w)")
                        last = add(OL[:, u, k, :], lambda h0, hn: b[:, h0 * PART:(h0 + hn) * PART], start=False, stop=False)
                        last.then_inc(b_free, 1)
                    pe.wait_ge(b_free, (n + 1) * SLOT + NB)
                    pe.sem_inc(half_used, 1)
            add(zero, zeros, start=False, stop=True).then_inc(acc_done, 1)


def rank_gates(nc, link, score, experts, tmp, tmp2, tmp3, earlier, keep):
    shape = [P, TILES, experts, experts]
    view = lambda t: t.rearrange("p (s a b) -> p s a b", a=experts, b=experts)
    this, other = score.unsqueeze(3).to_broadcast(shape), score.unsqueeze(2).to_broadcast(shape)
    flat = lambda t: t
    link(nc.vector.tensor_tensor(view(tmp), other, this, ALU.is_gt))
    link(nc.vector.tensor_tensor(view(tmp2), other, this, ALU.is_equal))
    link(nc.vector.tensor_tensor(view(tmp2), view(tmp2),
                                 earlier.unsqueeze(1).to_broadcast(shape), ALU.mult))
    link(nc.vector.tensor_tensor(tmp, tmp, tmp2, ALU.add))
    link(nc.vector.tensor_reduce(keep, view(tmp), AX.X, ALU.add))
    link(nc.vector.tensor_scalar(keep, keep, 2.0, None, ALU.is_lt))


def earlier_mask(nc, pool, earlier, experts, made):
    pool.memset(earlier, 1.0).then_inc(made, 1)
    pool.wait_ge(made, 1)
    pool.affine_select(out=earlier, in_=earlier, compare_op=ALU.is_gt, fill=0.0, base=0,
                       pattern=[[1, experts], [-1, experts]], channel_multiplier=0).then_inc(made, 1)


def graph_gates(nc, sem, A, H, GT, LAST, SUMS, CN, G):
    with ExitStack() as ctx:
        local = lambda n, s, d=F32: ctx.enter_context(nc.sbuf_tensor("sb_gg_" + n, s, d))
        vec = local("vec", [P, 3, GF])
        W2 = local("w2", [P, TILES, 8])
        W1 = local("w1", [P, TILES, 4])
        M = local("m", [P, TILES, GF])
        AG = local("ag", [P, TILES, GF])
        st = local("st", [P, 4, TILES])
        RD = local("rd", [P, TILES, 4])
        t1, t2 = local("t1", [P, TILES * 16]), local("t2", [P, TILES * 16])
        earlier = local("earlier", [P, 4, 4])
        SC, KEEP = local("sc", [P, TILES, 4]), local("keep", [P, TILES, 4])
        v_in, made, chain, var, root, shifted, exped = (sem("gg_" + n) for n in ("in", "made", "chain", "var", "root", "shifted", "exped"))
        block = ctx.enter_context(nc.Block())

        @block.sync
        def _(sp):
            for k, n in enumerate(("b_gat", "ln_gamma", "ln_beta")):
                sp.dma_start(vec[:, k, :], A[n].partition_broadcast(P)).then_inc(v_in, 16)
            sp.wait_ge(v_in, 48)

        @block.gpsimd
        def _(pool):
            earlier_mask(nc, pool, earlier[:, :, :], 4, made)

        @block.scalar
        def _(act):
            act.wait_ge(var, 1)
            nc.scalar.activation(st[:, 2, :], st[:, 1, :], ACT.Sqrt).then_inc(root, 1)
            act.wait_ge(shifted, 1)
            nc.scalar.activation(SC[:, :, :], SC[:, :, :], ACT.Exp).then_inc(exped, 1)

        @block.vector
        def _(v):
            link = Chain(v, chain)
            h4 = lambda t: t.rearrange("p s (h e) -> p s h e", e=4)
            w4 = lambda: W1[:, :, :].unsqueeze(3).to_broadcast([P, TILES, 4, 4])
            v.wait_ge(v_in, 48)
            link(nc.vector.tensor_tensor(W2[:, :, :], GT[:, :, 0:8], GT[:, :, 8:16], ALU.mult))
            link(nc.vector.tensor_tensor(W1[:, :, :], W2[:, :, 0:4], W2[:, :, 4:8], ALU.max))
            link(nc.vector.tensor_tensor(h4(M[:, :, :]), h4(H[:, :, :]), w4(), ALU.mult))
            link(nc.vector.tensor_tensor(SUMS[:, :, 0:GF], SUMS[:, :, 0:GF], M[:, :, :], ALU.add))
            link(nc.vector.tensor_tensor(SUMS[:, :, GF:], SUMS[:, :, GF:], W1[:, :, :], ALU.add))
            link(nc.vector.tensor_tensor(W2[:, :, :], LAST[:, GF:].unsqueeze(1).to_broadcast([P, TILES, 8]), GT[:, :, 8:16], ALU.mult))
            link(nc.vector.tensor_tensor(W1[:, :, :], W2[:, :, 0:4], W2[:, :, 4:8], ALU.max))
            link(nc.vector.tensor_tensor(W1[:, :, :], W1[:, :, :], CN[:, :].unsqueeze(2).to_broadcast([P, TILES, 4]), ALU.mult))
            link(nc.vector.tensor_tensor(h4(M[:, :, :]), h4(LAST[:, 0:GF].unsqueeze(1).to_broadcast([P, TILES, GF])), w4(), ALU.mult))
            link(nc.vector.tensor_tensor(SUMS[:, :, 0:GF], SUMS[:, :, 0:GF], M[:, :, :], ALU.add))
            link(nc.vector.tensor_tensor(SUMS[:, :, GF:], SUMS[:, :, GF:], W1[:, :, :], ALU.add))
            link(nc.vector.tensor_scalar(RD[:, :, :], SUMS[:, :, GF:], 1e-16, None, ALU.add))
            link(nc.vector.reciprocal(RD[:, :, :], RD[:, :, :]))
            link(nc.vector.tensor_tensor(h4(AG[:, :, :]), h4(SUMS[:, :, 0:GF]), RD[:, :, :].unsqueeze(3).to_broadcast([P, TILES, 4, 4]), ALU.mult))
            bc = lambda k: vec[:, k, :].unsqueeze(1).to_broadcast([P, TILES, GF])
            link(nc.vector.tensor_tensor(AG[:, :, :], AG[:, :, :], bc(0), ALU.add))
            wide = lambda k: st[:, k, :].unsqueeze(2).to_broadcast([P, TILES, GF])
            link(nc.vector.tensor_reduce(st[:, 0, :], AG[:, :, :], AX.X, ALU.add))
            link(nc.vector.tensor_scalar(st[:, 0, :], st[:, 0, :], 1.0 / GF, None, ALU.mult))
            link(nc.vector.tensor_tensor(AG[:, :, :], AG[:, :, :], wide(0), ALU.subtract))
            link(nc.vector.tensor_tensor(M[:, :, :], AG[:, :, :], AG[:, :, :], ALU.mult))
            link(nc.vector.tensor_reduce(st[:, 1, :], M[:, :, :], AX.X, ALU.add))
            link(nc.vector.tensor_scalar(st[:, 1, :], st[:, 1, :], 1.0 / GF, EPS_T, ALU.mult, ALU.add))
            v.sem_inc(var, 1)
            v.wait_ge(root, 1)
            link(nc.vector.reciprocal(st[:, 3, :], st[:, 2, :]))
            link(nc.vector.tensor_tensor(AG[:, :, :], AG[:, :, :], wide(3), ALU.mult))
            link(nc.vector.tensor_tensor(AG[:, :, :], AG[:, :, :], bc(1), ALU.mult))
            link(nc.vector.tensor_tensor(AG[:, :, :], AG[:, :, :], bc(2), ALU.add))
            link(nc.vector.tensor_reduce(SC[:, :, :], AG[:, :, :].rearrange("p s (h e) -> p s e h", e=4), AX.X, ALU.add))
            link(nc.vector.tensor_scalar(SC[:, :, :], SC[:, :, :], 0.25, None, ALU.mult))
            v.wait_ge(made, 2)
            rank_gates(nc, link, SC[:, :, :], 4, t1[:, :], t2[:, :], None, earlier[:, :, :], KEEP[:, :, :])
            link(nc.vector.tensor_reduce(st[:, 0, :], SC[:, :, :], AX.X, ALU.max))
            link(nc.vector.tensor_tensor(SC[:, :, :], SC[:, :, :], st[:, 0, :].unsqueeze(2).to_broadcast([P, TILES, 4]), ALU.subtract))
            v.sem_inc(shifted, 1)
            v.wait_ge(exped, 1)
            link(nc.vector.tensor_tensor(SC[:, :, :], SC[:, :, :], KEEP[:, :, :], ALU.mult))
            link(nc.vector.tensor_reduce(st[:, 0, :], SC[:, :, :], AX.X, ALU.add))
            link(nc.vector.reciprocal(st[:, 1, :], st[:, 0, :]))
            link(nc.vector.tensor_tensor(G[:, :, :], SC[:, :, :], st[:, 1, :].unsqueeze(2).to_broadcast([P, TILES, 4]), ALU.mult))


def run_experts(nc, sem, tag, X2, TT, G, experts, chunks, W1, b1, W2, b2, ident, store=None):
    with ExitStack() as ctx:
        local = lambda n, s, d=F32: ctx.enter_context(nc.sbuf_tensor(f"sb_{tag}_{n}", s, d))
        pbank = lambda n: ctx.enter_context(nc.psum_tensor(f"{tag}_{n}", [P, BANK], F32))
        NCH = experts * chunks
        YB = experts * C // BANK
        w1 = local("w1", [C, NCH * P])
        w2 = local("w2", [P, NCH, C])
        bb1 = local("b1", [P, NCH])
        B2 = local("b2", [GROUP * experts, BANK])
        HT = local("ht", [P, 2, NCH, BANK])
        GC = local("gc", [P, 2, GROUP * experts])
        GTR = local("gtr", [GROUP * experts, P])
        PU = [pbank(f"pu{k}") for k in range(2)]
        NY = 4
        PY = [pbank(f"py{k}") for k in range(NY)]
        PB2, PG = pbank("pb2"), pbank("pg")
        w_in, zero, hidden, up_done = (sem(f"{tag}_{n}") for n in ("w_in", "zero", "hidden", "up_done"))
        gates_in, gates_turned, gates_out, bias_done, bias_added = (sem(f"{tag}_{n}") for n in ("gates_in", "gates_turned", "gates_out", "bias_done", "bias_added"))
        y_done, added, stored = (sem(f"{tag}_{n}") for n in ("y_done", "added", "stored"))
        term = sem(f"{tag}_term")
        block = ctx.enter_context(nc.Block())
        n_w = 3 + GROUP

        @block.sync
        def _(sp):
            sp.dma_start(w1[:, :].rearrange("c (e h) -> c e h", e=experts), W1.rearrange("e c h -> c e h")).then_inc(w_in, 16)
            sp.dma_start(w2[:, :, :], W2.rearrange("e (k p) c -> p (e k) c", p=P)).then_inc(w_in, 16)
            sp.dma_start(bb1[:, :], b1.rearrange("e (k p) -> p (e k)", p=P), allow_slow_non_contiguous=True).then_inc(w_in, 16)
            sp.wait_ge(zero, 1)
            for k in range(GROUP):
                sp.dma_start(B2[k * experts:(k + 1) * experts, k * C:(k + 1) * C], b2).then_inc(w_in, 16)
            sp.wait_ge(w_in, 16 * n_w)
            if store is not None:
                sent = 0
                for part in range(4):
                    sp.wait_ge(added, (part + 1) * GROUPS // 4)
                    sent += store(sp, part, stored)
                sp.wait_ge(stored, 16 * sent)

        @block.gpsimd
        def _(pool):
            pool.memset(B2[:, :], 0.0).then_inc(zero, 1)

        @block.scalar
        def _(act):
            act.wait_ge(w_in, 16 * n_w)

            def hide(g, u):
                act.wait_ge(bias_done, g + 1)
                for c in range(NCH):
                    act.wait_ge(up_done, g * NCH + c + 1)
                    nc.scalar.activation(HT[:, u, c, :], PU[c % 2][:, :], ACT.Gelu, bias=bb1[:, c:c + 1])\
                        .then_inc(hidden, 1)
            with act.Fori(0, GROUPS // 2) as i:
                for u in range(2):
                    hide(i * 2 + u, u)

        @block.tensor
        def _(pe):
            pe.wait_ge(w_in, 16 * n_w)

            def up(g, c):
                pe.wait_ge(hidden, g * NCH + c + 1)
                nc.tensor.matmul(PU[c % 2][:, :], w1[:, c * P:(c + 1) * P], TT[:, ds(g * BANK, BANK)], start=True, stop=True)\
                    .then_inc(up_done, 1)

            def down(g, u, k):
                for b in range(YB):
                    n = (g * GROUP + k) * YB + b
                    pe.wait_ge(term, 4 * n + 4)
                    bank = PY[(k * YB + b) % NY]
                    for e in range(b * 4, b * 4 + 4):
                        for c in range(chunks):
                            last = nc.tensor.matmul(bank[:, (e % 4) * C:(e % 4 + 1) * C],
                                                    HT[:, u, e * chunks + c, k * P:(k + 1) * P], w2[:, e * chunks + c, :],
                                                    start=(c == 0), stop=(c == chunks - 1))
                    last.then_inc(y_done, 1)

            def biases(g, u):
                pe.wait_ge(gates_in, g + 1)
                nc.tensor.transpose(PG[0:GROUP * experts, 0:P], GC[:, u, :], ident[:, :]).then_inc(gates_turned, 1)
                pe.wait_ge(gates_out, g + 1)
                pe.wait_ge(added, g)
                nc.tensor.matmul(PB2[:, :], GTR[:, :], B2[:, :], start=True, stop=True).then_inc(bias_done, 1)

            pe.sem_inc(hidden, 2)
            pe.sem_inc(bias_done, 2)
            pe.sem_inc(term, 4 * NY)
            for c in range(NCH):
                up(0, c)

            def turn(g, u, more):
                pe.wait_ge(hidden, (g + 1) * NCH + 2)
                for c in range(NCH):
                    if more:
                        up(g + 1, c)
                    if c % 2 == 1:
                        if c // 2 < GROUP:
                            down(g, u, c // 2)
                biases(g, u)

            with pe.Fori(0, GROUPS // 2 - 1) as i:
                for u in range(2):
                    turn(i * 2 + u, u, True)
            turn(GROUPS - 2, 0, True)
            turn(GROUPS - 1, 1, False)

        @block.vector
        def _(v):
            v.wait_ge(w_in, 16 * n_w)

            def group(g, u):
                v.wait_ge(gates_turned, g)
                nc.vector.tensor_copy(GC[:, u, :].rearrange("p (t e) -> p t e", e=experts),
                                      G[:, ds(g * GROUP, GROUP), :]).then_inc(gates_in, 1)
                v.wait_ge(gates_in, g + 1)
                for k in range(GROUP):
                    xs = X2[:, ds((g * GROUP + k) * C, C)]
                    for e in range(experts):
                        n = (g * GROUP + k) * experts + e
                        b = e // 4
                        if e % 4 == 0:
                            v.wait_ge(y_done, (g * GROUP + k) * YB + b + 1)
                        v.wait_ge(term, n + 4 * NY)
                        last = nc.vector.scalar_tensor_tensor(
                            out=xs, in0=PY[(k * YB + b) % NY][:, (e % 4) * C:(e % 4 + 1) * C],
                            scalar=GC[:, u, k * experts + e:k * experts + e + 1], in1=xs, op0=ALU.mult, op1=ALU.add)
                        last.then_inc(term, 1)
                v.wait_ge(gates_turned, g + 1)
                nc.vector.tensor_copy(GTR[:, :], PG[0:GROUP * experts, 0:P]).then_inc(gates_out, 1)
                v.wait_ge(bias_done, g + 3)
                v.wait_ge(term, (g + 1) * GROUP * experts + 4 * NY)
                xg = X2[:, ds(g * BANK, BANK)]
                nc.vector.tensor_tensor(xg, PB2[:, :], xg, ALU.add).then_inc(added, 1)

            with v.Fori(0, GROUPS // 2) as i:
                for u in range(2):
                    group(i * 2 + u, u)


def mix_weights(nc, sem, A, X, XN, XN_D, X_D, ident, mean, rstd, WT, U, CB):
    with ExitStack() as ctx:
        local = lambda n, s, d=F32: ctx.enter_context(nc.sbuf_tensor("sb_mw_" + n, s, d))
        pbank = lambda n: ctx.enter_context(nc.psum_tensor("mw_" + n, [P, BANK], F32))
        bn, tmp = local("bn", [P, TILES * 6]), local("tmp", [P, 2, TILES])
        unit = local("unit", [P, 1])
        ROW_M = local("row_m", [1, TOKENS])
        XM, XMT = local("xm", [F, C]), local("xmt", [C, F])
        WQK, BQK = local("wqk", [C, LH, C, 2]), local("bqk", [C, LH, 2])
        WV, WVT = local("wv", [C, LH * C]), local("wvt", [C, LH * C])
        WP = local("wp", [P, LH, C])
        BV, BP = local("bv", [P, LH]), local("bp", [P, 1])
        QK = local("qk", [C, LH, 2, F])
        SCO = local("sco", [F, LH, F])
        sm = local("sm", [F, 2, LH])
        pm = [pbank(f"pm{k}") for k in range(2)]
        px, pq, pv = pbank("px"), pbank("pq"), pbank("pv")
        w_in, chain, var, root, normed = (sem("mw_" + n) for n in ("in", "chain", "var", "root", "normed"))
        x_stored, n_stored, unit_set = sem("x_stored"), sem("n_stored"), sem("unit_set")
        m_done, m_out, rows_in, xm_turned, xmt_out = (sem("mw_" + n) for n in ("m_done", "m_out", "rows_in", "xm_turned", "xmt_out"))
        qk_done, qk_out, sc_done, shifted, exped, prob, wt_done = (sem("mw_" + n) for n in ("qk_done", "qk_out", "sc_done", "shifted", "exped", "prob", "wt_done"))
        wvt_done, wvt_out, u_done = (sem("mw_" + n) for n in ("wvt_done", "wvt_out", "u_done"))
        x_back = sem("x_back")
        block = ctx.enter_context(nc.Block())
        X2 = X[:, :, :].rearrange("p s c -> p (s c)")
        NORM = 4
        part = F // NORM

        @block.sync
        def _(sp):
            sp.dma_start(X_D.rearrange("f t c -> t f c"), X[:, :, :]).then_inc(x_stored, 16)
            sp.wait_ge(x_stored, 16)
            for k in range(NORM):
                sp.wait_ge(normed, (k + 1) * part // 4)
                sp.dma_start(XN_D[k * part:(k + 1) * part].rearrange("f t c -> t f c"),
                             XN[:, k * part * C:(k + 1) * part * C].rearrange("p (f c) -> p f c", c=C)).then_inc(n_stored, 16)
            for a in range(2):
                sp.dma_start(X[a * F:(a + 1) * F, :, :],
                             X_D.rearrange("f (j a) c -> a f j c", a=2)[a]).then_inc(x_back, 16)
            sp.wait_ge(m_out, F // GROUP)
            sp.dma_start(XM[:, :], ROW_M[0, :].rearrange("(f c) -> f c", c=C).unsqueeze(0) if False else ROW_M[0:1, :]).then_inc(rows_in, 16)
            sp.wait_ge(n_stored, 16 * NORM)
            sp.wait_ge(x_back, 32)
            sp.wait_ge(rows_in, 16)

        @block.scalar
        def _(act):
            for dst, src in ((WQK[:, :, :, :].rearrange("c h d k -> c (h d k)"), A["Wqk"]),
                             (BQK[:, :, :], A["bqk"].rearrange("(h d k) -> d h k", h=LH, k=2)),
                             (WV[:, :], A["Wv"]), (WP[:, :, :], A["Wproj"].rearrange("(h d) c -> d h c", h=LH)),
                             (BV[:, :], A["bv"].rearrange("(h d) -> d h", h=LH)), (BP[:, :], A["bproj"].unsqueeze(1))):
                act.dma_start(dst, src, allow_slow_non_contiguous=True).then_inc(w_in, 16)
            act.wait_ge(var, 1)
            nc.scalar.activation(tmp[:, 0, :], tmp[:, 1, :], ACT.Sqrt).then_inc(root, 1)
            for g in range(F // GROUP):
                act.wait_ge(m_done, g + 1)
                nc.scalar.activation(ROW_M[:, g * BANK:(g + 1) * BANK], pm[g % 2][0:1, :], ACT.Copy).then_inc(m_out, 1)
            act.wait_ge(shifted, 1)
            nc.scalar.activation(SCO[:, :, :], SCO[:, :, :], ACT.Exp).then_inc(exped, 1)
            act.wait_ge(w_in, 96)

        @block.vector
        def _(v):
            link = Chain(v, chain)
            nc.vector.memset(unit[:, :], 1.0 / T).then_inc(unit_set, 1)
            v.wait_ge(w_in, 96)
            layer_statistics(nc, v, link, X2, bn, mean, rstd, tmp[:, 0, :])
            link(nc.vector.tensor_scalar(tmp[:, 1, :], rstd, EPS_C, None, ALU.add))
            v.sem_inc(var, 1)
            v.wait_ge(root, 1)
            link(nc.vector.reciprocal(rstd, tmp[:, 0, :]))
            with v.Fori(0, GROUPS) as g:
                for k in range(GROUP):
                    t = g * GROUP + k
                    last = nc.vector.tensor_scalar(XN[:, ds(t * C, C)], X2[:, ds(t * C, C)],
                                                   mean[:, ds(t, 1)], rstd[:, ds(t, 1)], ALU.subtract, ALU.mult)
                last.then_inc(normed, 1)
            v.wait_ge(wvt_done, 1)
            nc.vector.tensor_copy(WVT[:, :], pv[:, :]).then_inc(wvt_out, 1)
            v.wait_ge(u_done, 1)
            link(nc.vector.tensor_copy(U[:, :, :].rearrange("p h c -> p (h c)"), pq[:, :]))
            link(nc.vector.tensor_tensor(CB[:, :], px[:, 0:1], BP[:, :], ALU.add))
            v.sem_inc(wvt_out, 1)
            v.wait_ge(xm_turned, 1)
            nc.vector.tensor_copy(XMT[:, :], pv[:, 0:F]).then_inc(xmt_out, 1)
            v.wait_ge(qk_done, 1)
            for h in range(LH):
                for k in range(2):
                    last = nc.vector.tensor_scalar(QK[:, h, k, :], pq[:, (h * 2 + k) * F:(h * 2 + k + 1) * F],
                                                   BQK[:, h, k:k + 1], 1.0 / math.sqrt(C), ALU.add, ALU.mult)
            last.then_inc(qk_out, 1)
            v.wait_ge(sc_done, 1)
            s3 = px[0:F, 0:LH * F].rearrange("p (h g) -> p h g", g=F)
            wide = lambda k: sm[:, k, :].unsqueeze(2).to_broadcast([F, LH, F])
            link(nc.vector.tensor_reduce(sm[:, 0, :], s3, AX.X, ALU.max))
            link(nc.vector.tensor_tensor(SCO[:, :, :], s3, wide(0), ALU.subtract))
            v.sem_inc(shifted, 1)
            v.wait_ge(exped, 1)
            link(nc.vector.tensor_reduce(sm[:, 0, :], SCO[:, :, :], AX.X, ALU.add))
            link(nc.vector.reciprocal(sm[:, 1, :], sm[:, 0, :]))
            nc.vector.tensor_tensor(SCO[:, :, :], SCO[:, :, :], wide(1), ALU.mult).then_inc(prob, 1)
            v.wait_ge(wt_done, 1)
            link(nc.vector.tensor_copy(WT[:, :], pv[0:F, 0:LH * F]))

        @block.tensor
        def _(pe):
            pe.wait_ge(unit_set, 1)
            pe.wait_ge(w_in, 96)
            for h in range(LH):
                last = nc.tensor.transpose(pv[:, h * C:(h + 1) * C], WV[:, h * C:(h + 1) * C], ident[:, :])
            last.then_inc(wvt_done, 1)
            pe.wait_ge(wvt_out, 1)
            for h in range(LH):
                nc.tensor.matmul(pq[:, h * C:(h + 1) * C], WVT[:, h * C:(h + 1) * C], WP[:, h, :], start=True, stop=True)
            for h in range(LH):
                last = nc.tensor.matmul(px[:, 0:1], WP[:, h, :], BV[:, h:h + 1], start=(h == 0), stop=(h == LH - 1))
            last.then_inc(u_done, 1)
            for g in range(F // GROUP):
                pe.wait_ge(normed, g + 1)
                if g >= 2:
                    pe.wait_ge(m_out, g - 1)
                nc.tensor.matmul(pm[g % 2][0:1, :], unit[:, :], XN[:, g * BANK:(g + 1) * BANK], start=True, stop=True).then_inc(m_done, 1)
            pe.wait_ge(rows_in, 16)
            pe.wait_ge(wvt_out, 2)
            nc.tensor.transpose(pv[:, 0:F], XM[:, :], ident[0:F, 0:F]).then_inc(xm_turned, 1)
            pe.wait_ge(xmt_out, 1)
            for h in range(LH):
                for k in range(2):
                    last = nc.tensor.matmul(pq[:, (h * 2 + k) * F:(h * 2 + k + 1) * F], WQK[:, h, :, k], XMT[:, :], start=True, stop=True)
            last.then_inc(qk_done, 1)
            pe.wait_ge(qk_out, 1)
            for h in range(LH):
                last = nc.tensor.matmul(px[0:F, h * F:(h + 1) * F], QK[:, h, 0, :], QK[:, h, 1, :], start=True, stop=True)
            last.then_inc(sc_done, 1)
            pe.wait_ge(prob, 1)
            for h in range(LH):
                last = nc.tensor.transpose(pv[0:F, h * F:(h + 1) * F], SCO[:, h, :], ident[0:F, 0:F])
            last.then_inc(wt_done, 1)


def mix_rows(nc, sem, X, XN_D, ident, WT, U, CB):
    TG = 8
    N = T // TG
    with ExitStack() as ctx:
        local = lambda n, s, d=F32: ctx.enter_context(nc.sbuf_tensor("sb_mr_" + n, s, d))
        pbank = lambda n: ctx.enter_context(nc.psum_tensor("mr_" + n, [P, BANK], F32))
        XG = local("xg", [F, 2, TG, C])
        ZT = local("zt", [C, 2, LH, TG * F])
        YT = local("yt", [C, 2, TG * F])
        pz = [pbank(f"pz{k}") for k in range(4)]
        py, pt = [pbank(f"py{k}") for k in range(2)], [pbank(f"pt{k}") for k in range(2)]
        loaded = [sem(f"mr_loaded{u}") for u in range(2)]
        z_done, za_out, zv_out, y_done, y_out, t_done, added = (sem("mr_" + n) for n in ("z", "za_out", "zv_out", "y", "y_out", "t", "added"))
        block = ctx.enter_context(nc.Block())
        X2 = X[:, :, :].rearrange("p s c -> p (s c)")
        XF = XN_D.rearrange("f t c -> f (t c)")

        @block.sync
        def _(sp):
            with sp.Fori(0, N // 2) as i:
                for u in range(2):
                    g = i * 2 + u
                    sp.wait_ge(z_done, i * 2)
                    sp.dma_start(XG[:, u, :, :].rearrange("f t c -> f (t c)"), XF[:, ds(g * TG * C, TG * C)]).then_inc(loaded[u], 16)

        def z_copy(copy, g, u, b):
            return copy(ZT[:, u, :, b * 2 * F:(b + 1) * 2 * F].rearrange("p h (t f) -> p t h f", f=F),
                        pz[b][:, :].rearrange("p (t h f) -> p t h f", t=2, f=F))

        @block.scalar
        def _(act):
            with act.Fori(0, N // 2) as i:
                for u in range(2):
                    g = i * 2 + u
                    act.wait_ge(z_done, g + 1)
                    act.wait_ge(y_done, i * 2)
                    for b in (0, 2):
                        last = z_copy(lambda o, x: nc.scalar.activation(o, x, ACT.Copy), g, u, b)
                    last.then_inc(za_out, 1)
                    act.wait_ge(y_done, g + 1)
                    act.wait_ge(t_done, i * 2)
                    nc.scalar.activation(YT[:, u, :], py[u][:, :], ACT.Identity, bias=CB[:, :]).then_inc(y_out, 1)

        @block.vector
        def _(v):
            with v.Fori(0, N // 2) as i:
                for u in range(2):
                    g = i * 2 + u
                    v.wait_ge(z_done, g + 1)
                    v.wait_ge(y_done, i * 2)
                    for b in (1, 3):
                        last = z_copy(nc.vector.tensor_copy, g, u, b)
                    last.then_inc(zv_out, 1)
                    v.wait_ge(t_done, g + 1)
                    xg = X2[:, ds(g * BANK, BANK)]
                    nc.vector.tensor_tensor(xg, pt[u][:, :], xg, ALU.add).then_inc(added, 1)

        @block.tensor
        def _(pe):
            def mix(g, u, i):
                pe.wait_ge(loaded[u], (i + 1) * 16)
                pe.wait_ge(za_out, g)
                pe.wait_ge(zv_out, g)
                for t in range(TG):
                    last = nc.tensor.matmul(pz[t // 2][:, (t % 2) * LH * F:(t % 2 + 1) * LH * F], XG[:, u, t, :], WT[:, :],
                                            start=True, stop=True)
                last.then_inc(z_done, 1)

            def project(g, u):
                pe.wait_ge(za_out, g + 1)
                pe.wait_ge(zv_out, g + 1)
                pe.wait_ge(y_out, u * 0 + g - 1 if isinstance(g, int) and g >= 2 else 0)
                for h in range(LH):
                    last = nc.tensor.matmul(py[u][:, :], U[:, h, :], ZT[:, u, h, :], start=(h == 0), stop=(h == LH - 1))
                last.then_inc(y_done, 1)

            def turn(g, u):
                pe.wait_ge(y_out, g + 1)
                pe.wait_ge(added, g)
                for k in range(GROUP):
                    last = nc.tensor.transpose(pt[u][:, k * P:(k + 1) * P], YT[:, u, k * P:(k + 1) * P], ident[:, :])
                last.then_inc(t_done, 1)

            mix(0, 0, 0)
            with pe.Fori(0, N // 2 - 1) as i:
                mix(i * 2 + 1, 1, i)
                project(i * 2, 0)
                turn(i * 2, 0)
                mix(i * 2 + 2, 0, i + 1)
                project(i * 2 + 1, 1)
                turn(i * 2 + 1, 1)
            mix(N - 1, 1, N // 2 - 1)
            project(N - 2, 0)
            turn(N - 2, 0)
            project(N - 1, 1)
            turn(N - 1, 1)


def route_gates(nc, sem, X, LG, mean, rstd, G):
    E = EXPERTS1
    with ExitStack() as ctx:
        local = lambda n, s, d=F32: ctx.enter_context(nc.sbuf_tensor("sb_rg_" + n, s, d))
        t1, t2 = local("t1", [P, TILES * E * E]), local("t2", [P, TILES * E * E])
        earlier = local("earlier", [P, E, E])
        KEEP, st, scale, shift = local("keep", [P, TILES, E]), local("st", [P, 2, TILES]), local("scale", [P, TILES]), local("shift", [P, TILES])
        made, chain, shifted, exped = (sem("rg_" + n) for n in ("made", "chain", "shifted", "exped"))
        block = ctx.enter_context(nc.Block())
        X2 = X[:, :, :].rearrange("p s c -> p (s c)")

        @block.gpsimd
        def _(pool):
            earlier_mask(nc, pool, earlier[:, :, :], E, made)

        @block.scalar
        def _(act):
            act.wait_ge(shifted, 1)
            nc.scalar.activation(LG[:, :, :], LG[:, :, :], ACT.Exp).then_inc(exped, 1)

        @block.vector
        def _(v):
            link = Chain(v, chain)
            wide = lambda k: st[:, k, :].unsqueeze(2).to_broadcast([P, TILES, E])
            link(nc.vector.tensor_reduce(st[:, 0, :], LG[:, :, :], AX.X, ALU.max))
            link(nc.vector.tensor_tensor(LG[:, :, :], LG[:, :, :], wide(0), ALU.subtract))
            v.sem_inc(shifted, 1)
            link(nc.vector.tensor_scalar(scale[:, :], rstd, 1.0, None, ALU.add))
            link(nc.vector.tensor_tensor(shift[:, :], mean, rstd, ALU.mult))
            with v.Fori(0, TILES // 8) as i:
                for k in range(8):
                    t = i * 8 + k
                    xs = X2[:, ds(t * C, C)]
                    nc.vector.tensor_scalar(xs, xs, scale[:, ds(t, 1)], shift[:, ds(t, 1)], ALU.mult, ALU.subtract)
            v.wait_ge(exped, 1)
            link(nc.vector.tensor_reduce(st[:, 0, :], LG[:, :, :], AX.X, ALU.add))
            link(nc.vector.reciprocal(st[:, 1, :], st[:, 0, :]))
            link(nc.vector.tensor_tensor(LG[:, :, :], LG[:, :, :], wide(1), ALU.mult))
            v.wait_ge(made, 2)
            rank_gates(nc, link, LG[:, :, :], E, t1[:, :], t2[:, :], None, earlier[:, :, :], KEEP[:, :, :])
            link(nc.vector.tensor_tensor(LG[:, :, :], LG[:, :, :], KEEP[:, :, :], ALU.mult))
            link(nc.vector.tensor_reduce(st[:, 0, :], LG[:, :, :], AX.X, ALU.add))
            link(nc.vector.tensor_scalar(st[:, 0, :], st[:, 0, :], 1e-12, None, ALU.max))
            link(nc.vector.reciprocal(st[:, 1, :], st[:, 0, :]))
            link(nc.vector.tensor_tensor(G[:, :, :], LG[:, :, :], wide(1), ALU.mult))


def metaformer(nc, A, out):
    with ExitStack() as ctx:
        sem = lambda n: nc.alloc_semaphore(n)
        sb = lambda n, s, d=F32: ctx.enter_context(nc.sbuf_tensor("sb_" + n, s, d))
        part = lambda prefix: {n[len(prefix):]: a for n, a in A.items() if n.startswith(prefix)}
        c0, f0, c1, f1 = (part(p) for p in ("L0_conv_", "L0_ffn_", "L1_conv_", "L1_ffn_"))
        c0["x"] = A["x"]
        X = sb("X", [P, TILES, C])
        ident = sb("ident", [P, P])
        st = sb("st", [P, 2, TILES])
        mean, rstd = st[:, 0, :], st[:, 1, :]
        X2 = X[:, :, :].rearrange("p s c -> p (s c)")
        SRC_T = nc.dram_tensor("source_rows", [TOKENS, ROW], F32).ap()
        DST_T = nc.dram_tensor("target_rows", [TOKENS, 2 * GHEADS], F32).ap()
        XN_D = nc.dram_tensor("normed_rows", [F, T, C], F32).ap()
        X_D = nc.dram_tensor("x_rows", [F, T, C], F32).ap()
        CN = sb("CN", [P, TILES])
        n_pass = sb("n_pass", [P, 2, 1], I32)
        TT = sb("TT", [P, TOKENS])
        G0, LAST, SUMS, Wg = sb("G0", [P, TILES, EXPERTS0]), sb("LAST", [P, ROW]), sb("SUMS", [P, TILES, PART]), sb("Wg", [C, GF])
        H, GT = sb("H", [P, TILES, GF]), sb("GT", [P, TILES, GF])
        WT, U, CB = sb("WT", [F, LH * F]), sb("U", [C, LH, C]), sb("CB", [C, 1])
        Wr, LG, G1 = sb("Wr", [C, EXPERTS1]), sb("LG", [P, TILES, EXPERTS1]), sb("G1", [P, TILES, EXPERTS1])
        with ExitStack() as c_keys:
            KG = c_keys.enter_context(nc.sbuf_tensor("sb_KG", [P, KCOLS], F32))
            with nc.cleanup_on_exit():
                with ExitStack() as c_clamped:
                    KC = c_clamped.enter_context(nc.sbuf_tensor("sb_KC", [P, KCOLS], F32))
                    compact_edges(nc, sem, f0, KG, KC, CN, n_pass, None)
                with ExitStack() as c_pair:
                    PB = c_pair.enter_context(nc.sbuf_tensor("sb_PB", [P, HEADS, T], F32))
                    pair_bias(nc, sem, sb, c0, X, PB, ident, mean, rstd)
                    row_attention(nc, sem, sb, c0, X, PB, ident, mean, rstd)
            with ExitStack() as c:
                turn_tokens(nc, sem, "t0", c, X2, ident, mean, rstd, TT, Wg[:, :], GF, H, EPS_T, f0["W_gat"])
            graph_tables(nc, sem, f0, H, GT, SRC_T, DST_T, LAST)
            graph_edges(nc, sem, KG, SRC_T, DST_T, n_pass[0:1, 0, 0:1], SUMS)
        graph_gates(nc, sem, f0, H, GT, LAST, SUMS, CN, G0)
        run_experts(nc, sem, "x0", X2, TT, G0, EXPERTS0, HID0 // P, f0["W1"], f0["b1"], f0["W2"], f0["b2"], ident)
        mix_weights(nc, sem, c1, X, TT, XN_D, X_D, ident, mean, rstd, WT, U, CB)
        mix_rows(nc, sem, X, XN_D, ident, WT, U, CB)
        with ExitStack() as c:
            turn_tokens(nc, sem, "t1", c, X2, ident, mean, rstd, TT, Wr[:, :], EXPERTS1, LG, EPS_T,
                        f1["router_w"].rearrange("e c -> c e"))
        route_gates(nc, sem, X, LG, mean, rstd, G1)
        out_v = out[0].rearrange("f (j a) c -> a f j c", a=2)
        quarter = TILES // 4

        def store(sp, k, stored):
            for a in range(2):
                sp.dma_start(out_v[a, :, k * quarter:(k + 1) * quarter, :],
                             X[a * F:(a + 1) * F, k * quarter:(k + 1) * quarter, :]).then_inc(stored, 16)
            return 2
        run_experts(nc, sem, "x1", X2, TT, G1, EXPERTS1, 1, f1["w1"], f1["b1"], f1["w2"], f1["b2"], ident, store)


def kernel(**inputs):
    import numpy as _np
    import concourse.bacc as _bacc
    from concourse import mybir as _mybir
    from concourse.bass_utils import run_bass_kernel_spmd as _run

    nc = _bacc.Bacc("TRN2", target_bir_lowering=False, num_devices=1)
    arrays, A = {}, {}
    for name, a in inputs.items():
        a = _np.ascontiguousarray(a)
        arrays[f"in_{name}"] = a
        A[name] = nc.dram_tensor(f"in_{name}", a.shape, _mybir.dt.from_np(a.dtype), kind="ExternalInput").ap()
    out = nc.dram_tensor("out", (1, F, T, C), F32, kind="ExternalOutput").ap()
    metaformer(nc, A, out)
    r = _run(nc, [arrays], core_ids=[0])
    return r.results[0]["out"]
```

```python
import math
from contextlib import ExitStack

import concourse.bass as bass
from concourse import mybir

F32 = mybir.dt.float32
BF16 = mybir.dt.bfloat16
I32 = mybir.dt.int32
ALU = mybir.AluOpType
ACT = mybir.ActivationFunctionType
AX = mybir.AxisListType
ds = bass.ds

P = 128
F, T, C = 64, 128, 128
TOKENS = F * T
TILES = TOKENS // P
HEADS, DH = 8, 32
HD = HEADS * DH
CZ = 64
INF = 1e9
EPS_C, EPS_T = 1e-6, 1e-5
AHEAD = 1
BANK = 512
GROUP = BANK // P
GROUPS = TILES // GROUP

GHEADS, EXPERTS0 = 4, 4
GF = GHEADS * EXPERTS0
EDGES = 524288
ECOLS = EDGES // P
NODE_BITS = 13
LO_BITS = 7
SLOT = 8
PAIR = 2 * SLOT
BLOCKS = 16
BCOLS = ECOLS // BLOCKS
TAKE = BLOCKS * SLOT
SEARCHES = 5
FOUND = SEARCHES * TAKE
WITH = 4
ROUNDS = -(-BCOLS // SLOT // SEARCHES)
STRIDE = FOUND // PAIR + 1
KCOLS = ROUNDS * STRIDE * PAIR + TAKE + P
PART = 20
ROW = GF + 2 * GHEADS
HID0 = 256
EXPERTS1 = 8
LH = 4

VALID = 1 << 30
NEAR = 1 << 26


class Chain:

    def __init__(self, engine, semaphore):
        self.engine, self.semaphore, self.steps = engine, semaphore, 0

    def __call__(self, instruction):
        self.steps += 1
        instruction.then_inc(self.semaphore, 1)
        self.engine.wait_ge(self.semaphore, self.steps)


def identity(nc, pool, tile, made, first):
    pool.memset(tile, 0.0).then_inc(made, 1)
    pool.wait_ge(made, first + 1)
    pool.affine_select(out=tile, in_=tile, compare_op=ALU.not_equal, fill=1.0, base=0,
                       pattern=[[-1, P]], channel_multiplier=1).then_inc(made, 1)


def layer_statistics(nc, v, link, x, bn, mean, spread, tmp):
    def tiles(i):
        for k in range(8):
            last = nc.vector.bn_stats(bn[:, ds((i * 8 + k) * 6, 6)], x[:, ds((i * 8 + k) * C, C)])
        return last
    with v.Fori(0, TILES // 8 - 1) as i:
        tiles(i)
    link(tiles(TILES // 8 - 1))
    b = bn[:, :].rearrange("p (s k) -> p s k", k=6)
    link(nc.vector.tensor_tensor(mean, b[:, :, 1], b[:, :, 4], ALU.add))
    link(nc.vector.tensor_scalar(mean, mean, 0.5, None, ALU.mult))
    link(nc.vector.tensor_tensor(spread, b[:, :, 1], b[:, :, 4], ALU.subtract))
    link(nc.vector.scalar_tensor_tensor(out=spread, in0=spread, scalar=0.25, in1=spread,
                                        op0=ALU.mult, op1=ALU.mult))
    link(nc.vector.tensor_tensor(tmp, b[:, :, 2], b[:, :, 5], ALU.add))
    link(nc.vector.scalar_tensor_tensor(out=spread, in0=tmp, scalar=1.0 / C, in1=spread,
                                        op0=ALU.mult, op1=ALU.add))


def pair_bias(nc, sem, A, X, z, PB, MB, loads, ident, mean, rstd):
    with ExitStack() as ctx:
        local = lambda n, s, d=F32: ctx.enter_context(nc.sbuf_tensor("sb_" + n, s, d))
        sq = local("z_sq", [P, T * CZ // 2])
        ztr = local("z_tr", [P, 2, BANK])
        zs = local("z_stat", [P, 4, T])
        bn = local("bn", [P, TILES * 6])
        wz = local("wz", [P, 2, HEADS])
        wzr = local("wzr", [P, 2])
        b_bc = local("b_bc", [CZ, P])
        pbc = local("pbc", [P, HEADS])
        tmp = local("stat_tmp", [P, 2, TILES])
        ptr = [ctx.enter_context(nc.psum_tensor(f"z_ptr{k}", [P, BANK], F32)) for k in range(2)]
        pzb = ctx.enter_context(nc.psum_tensor("pzb", [P, BANK], F32))
        pzb2 = ctx.enter_context(nc.psum_tensor("pzb2", [P, BANK], F32))
        pcc = ctx.enter_context(nc.psum_tensor("pcc", [P, BANK], F32))
        z_in, x_in, m_in = loads
        w_in, sq_used = sem("zw_in"), sem("squares_used")
        id_made, wz_zero = sem("id_made"), sem("wz_zero")
        zn, z_sq, z_rt, v_chain = sem("z_normal"), sem("z_squared"), sem("z_root"), sem("pair_chain")
        w_scaled = sem("wz_scaled")
        ztd, zev, zmm, const_mm = sem("z_transposed"), sem("z_evacuated"), sem("z_projected"), sem("pair_const")
        x_root = sem("x_root")
        x_var = sem("x_variance")
        block = ctx.enter_context(nc.Block())
        X2 = X[:, :, :].rearrange("p s c -> p (s c)")
        zz = z[:, :].rearrange("p (k c) -> p k c", c=CZ)
        sqz = sq[:, :].rearrange("p (k c) -> p k c", c=CZ)
        part = lambda n: slice(n * T * CZ // 2, (n + 1) * T * CZ // 2)

        @block.sync
        def _(sp):
            sp.wait_ge(wz_zero, 1)
            for k in range(2):
                sp.dma_start(wz[k * CZ:(k + 1) * CZ, k, :], A["w_z"]).then_inc(w_in, 16)
                sp.dma_start(wzr[k * CZ:(k + 1) * CZ, 0:1], A["ln_z_w"].unsqueeze(1)).then_inc(w_in, 16)
            sp.dma_start(wzr[0:CZ, 1:2], A["ln_z_b"].unsqueeze(1)).then_inc(w_in, 16)
            sp.wait_ge(z_in, 16)
            sp.wait_ge(w_in, 80)

        @block.scalar
        def _(act):
            act.wait_ge(zn, 1)
            nc.scalar.activation(sq[:, :], z[:, part(0)], ACT.Square).then_inc(z_sq, 1)
            act.wait_ge(x_var, 1)
            nc.scalar.activation(tmp[:, 0, :], tmp[:, 1, :], ACT.Sqrt).then_inc(x_root, 1)
            act.wait_ge(x_var, 2)
            nc.scalar.activation(tmp[:, 0, :], tmp[:, 1, :], ACT.Sqrt).then_inc(x_root, 1)
            act.wait_ge(sq_used, 1)
            nc.scalar.activation(sq[:, :], z[:, part(1)], ACT.Square).then_inc(z_sq, 1)
            act.wait_ge(zn, 2)
            nc.scalar.activation(zs[:, 2, :], zs[:, 1, :], ACT.Sqrt).then_inc(z_rt, 1)
            act.wait_ge(x_in, 16)

        @block.gpsimd
        def _(pool):
            pool.memset(wz[:, :, :], 0.0).then_inc(wz_zero, 1)
            identity(nc, pool, ident[:, :], id_made, 0)
            pool.wait_ge(m_in, 16)
            pool.tensor_scalar(MB, MB, 1.0, INF, ALU.subtract, ALU.mult)

        @block.vector
        def _(v):
            link = Chain(v, v_chain)
            v.wait_ge(z_in, 16)
            link(nc.vector.tensor_reduce(zs[:, 0, :], zz, AX.X, ALU.add))
            link(nc.vector.tensor_scalar(zs[:, 0, :], zs[:, 0, :], 1.0 / CZ, None, ALU.mult))
            nc.vector.tensor_tensor(zz, zz, zs[:, 0, :].unsqueeze(2).to_broadcast([P, T, CZ]),
                                    ALU.subtract).then_inc(zn, 1)
            v.wait_ge(x_in, 16)
            layer_statistics(nc, v, link, X2, bn, mean, rstd, tmp[:, 0, :])
            link(nc.vector.tensor_scalar(tmp[:, 1, :], rstd, EPS_C, None, ALU.add))
            v.sem_inc(x_var, 1)
            v.wait_ge(x_root, 1)
            link(nc.vector.reciprocal(tmp[:, 0, :], tmp[:, 0, :]))
            link(nc.vector.tensor_tensor(tmp[:, 1, :], tmp[:, 0, :], tmp[:, 0, :], ALU.mult))
            link(nc.vector.tensor_tensor(tmp[:, 1, :], tmp[:, 1, :], rstd, ALU.mult))
            link(nc.vector.tensor_copy(rstd, tmp[:, 0, :]))
            link(nc.vector.tensor_scalar(tmp[:, 1, :], tmp[:, 1, :], EPS_T, None, ALU.add))
            v.sem_inc(x_var, 1)
            v.wait_ge(x_root, 2)
            link(nc.vector.reciprocal(tmp[:, 0, :], tmp[:, 0, :]))
            link(nc.vector.tensor_tensor(rstd, rstd, tmp[:, 0, :], ALU.mult))
            v.wait_ge(z_sq, 1)
            nc.vector.tensor_reduce(zs[:, 1, 0:T // 2], sqz, AX.X, ALU.add).then_inc(sq_used, 1)
            v.wait_ge(z_sq, 2)
            link(nc.vector.tensor_reduce(zs[:, 1, T // 2:], sqz, AX.X, ALU.add))
            v.wait_ge(zn, 1)
            nc.vector.tensor_scalar(zs[:, 1, :], zs[:, 1, :], 1.0 / CZ, EPS_T,
                                    ALU.mult, ALU.add).then_inc(zn, 1)
            v.wait_ge(z_rt, 1)
            link(nc.vector.reciprocal(zs[:, 3, :], zs[:, 2, :]))
            nc.vector.tensor_tensor(zz, zz, zs[:, 3, :].unsqueeze(2).to_broadcast([P, T, CZ]),
                                    ALU.mult).then_inc(zn, 1)
            v.wait_ge(w_in, 80)
            link(nc.vector.memset(b_bc[:, :], 1.0))
            nc.vector.tensor_scalar(b_bc[:, :], b_bc[:, :], wzr[0:CZ, 1:2], None, ALU.mult)\
                .then_inc(w_scaled, 1)
            v.wait_ge(const_mm, 1)
            link(nc.vector.tensor_copy(pbc[:, :], pcc[:, 0:HEADS]))
            nc.vector.tensor_scalar(wz[:, :, :], wz[:, :, :], wzr[:, 0:1], None, ALU.mult)\
                .then_inc(w_scaled, 1)
            for g in range(T * CZ // (GROUP * P)):
                v.wait_ge(ztd, g + 1)
                if g >= 2:
                    v.wait_ge(zmm, g - 1)
                nc.vector.tensor_copy(ztr[:, g % 2, :], ptr[g % 2][:, :]).then_inc(zev, 1)
            v.wait_ge(zmm, T * CZ // (GROUP * P))
            half = T // 2
            for n, bank in enumerate((pzb, pzb2)):
                link(nc.vector.tensor_tensor(
                    PB[:, :, n * half:(n + 1) * half], bank[:, :].rearrange("p (k h) -> p h k", h=HEADS),
                    pbc[:, :].unsqueeze(2).to_broadcast([P, HEADS, half]), ALU.add))

        @block.tensor
        def _(pe):
            pe.wait_ge(w_scaled, 1)
            pe.wait_ge(w_in, 80)
            nc.tensor.matmul(pcc[:, 0:HEADS], b_bc[:, :], wz[0:CZ, 0, :], start=True, stop=True)\
                .then_inc(const_mm, 1)
            pe.wait_ge(id_made, 2)
            pe.wait_ge(w_scaled, 2)
            pe.wait_ge(zn, 3)
            n_groups = T * CZ // (GROUP * P)

            def turn(g):
                if g >= 2:
                    pe.wait_ge(zev, g - 1)
                for j in range(GROUP):
                    c = (g * GROUP + j) * P
                    last = nc.tensor.transpose(ptr[g % 2][:, j * P:(j + 1) * P], z[:, c:c + P], ident[:, :])
                last.then_inc(ztd, 1)

            def project(g):
                pe.wait_ge(zev, g + 1)
                for j in range(GROUP):
                    pair = g * GROUP + j
                    bank, col = (pzb, pair) if pair < 32 else (pzb2, pair - 32)
                    last = nc.tensor.matmul(bank[:, col * 16:col * 16 + 16],
                                            ztr[:, g % 2, j * P:(j + 1) * P],
                                            wz[:, :, :].rearrange("p a h -> p (a h)"), start=True, stop=True)
                last.then_inc(zmm, 1)

            turn(0)
            for g in range(1, n_groups):
                turn(g)
                project(g - 1)
            project(n_groups - 1)


def after(engine, semaphore, n):
    if not isinstance(n, int) or n > 0:
        engine.wait_ge(semaphore, n)


def row_attention(nc, sem, A, X, PB, MB, ident, mean, rstd):
    with ExitStack() as ctx:
        local = lambda n, s, d=F32: ctx.enter_context(nc.sbuf_tensor("sb_" + n, s, d))
        bank = lambda n, s=(P, BANK): ctx.enter_context(nc.psum_tensor(n, list(s), F32))
        QUAD = P // DH
        BM = local("bias", [P, 2, HEADS, T])
        wq, wk, wv, wg = (local(n, [C, HD]) for n in ("wq", "wk", "wv", "wg"))
        wo = local("wo", [P, 2, C])
        lnw, lnb = local("lnw", [C, 1]), local("lnb", [C, 1])
        ones = local("ones", [1, P])
        bg, bo = local("bg", [P, 2]), local("bo", [1, C])
        XN = local("xn", [P, C])
        SNT = local("snT", [C, T])
        QT = local("qT", [P, 2, T])
        KT = local("kT", [P, 2, QUAD, T])
        V, TH = local("v", [T, 2, HD]), local("gateT", [P, 2, 2, T])
        LG = local("logits", [T, HEADS, T])
        PR = local("probs", [T, 2, HEADS, T])
        NM = local("neg_max", [T, HEADS])
        SM, RI = local("row_sum", [T, 2, HEADS]), local("inv_sum", [T, HEADS])
        PT = local("probsT", [T, HEADS, T])
        OG, OGT = local("heads_out", [T, HD]), local("gatedT", [P, 2, T])
        L = bank("p_logits", (P, 2, BANK))
        TA, TB = bank("p_turned_a"), bank("p_turned_b")
        QPS, PRV, TURN, O = bank("p_q"), bank("p_vg"), bank("p_xn"), bank("p_out")
        w_in, ones_set, kt_zero, bg_half = sem("att_w_in"), sem("ones_set"), sem("kt_zero"), sem("bg_half")
        bias_made = sem("bias_made")
        xn_made, xn_turned, sn_made = sem("xn_made"), sem("xn_turned"), sem("sn_made")
        qk_done, q_out, k_out = sem("qk_done"), sem("q_out"), sem("k_out")
        vg_done, v_out, th_out = sem("vg_done"), sem("v_out"), sem("th_out")
        score_done, logit_made, max_made, exp_a, exp_b = sem("score_done"), sem("logit_made"), sem("max_made"), sem("exp_a"), sem("exp_b")
        ta_done, tb_done, ta_out, tb_out = sem("ta_done"), sem("tb_done"), sem("ta_out"), sem("tb_out")
        pv_done, inv_made, og_made = sem("pv_done"), sem("inv_made"), sem("og_made")
        og_turned, ogt_made, out_done, x_added = sem("og_turned"), sem("ogt_made"), sem("out_done"), sem("x_added")
        block = ctx.enter_context(nc.Block())
        X2 = X[:, :, :].rearrange("p s c -> p (s c)")
        N_W = 10
        real = lambda s: not isinstance(s, int) or 0 <= s < F

        def turns(engine, turn):
            for s in (-2, -1, 0, 1):
                turn(s, s % 2)
            with engine.Fori(0, (F - 4) // 2) as i:
                for u in range(2):
                    turn(i * 2 + (2 + u), u)
            for s in (F - 2, F - 1, F, F + 1):
                turn(s, s % 2)

        @block.sync
        def _(sp):
            for dst, src in ((wq[:, :], A["w_q"]), (wk[:, :], A["w_k"]), (wv[:, :], A["w_v"]), (wg[:, :], A["w_g"]),
                             (wo[:, :, :], A["w_o"].rearrange("(a p) c -> p a c", a=2)),
                             (lnw[:, :], A["ln_s_w"].unsqueeze(1)), (lnb[:, :], A["ln_s_b"].unsqueeze(1)),
                             (bg[:, 0:1], A["b_g"][0:P].unsqueeze(1)), (bg[:, 1:2], A["b_g"][P:HD].unsqueeze(1)),
                             (bo[:, :], A["b_o"].unsqueeze(0))):
                sp.dma_start(dst, src).then_inc(w_in, 16)
            sp.wait_ge(w_in, 16 * N_W)

        @block.gpsimd
        def _(pool):
            pool.memset(KT[:, :, :, :], 0.0).then_inc(kt_zero, 1)

            def bias(s, u):
                nc.gpsimd.tensor_tensor(
                    BM[:, u, :, :], PB[:, :, :],
                    MB[:, ds(s * T, T)].unsqueeze(1).to_broadcast([P, HEADS, T]), ALU.add).then_inc(bias_made, 1)

            bias(0, 0)
            bias(1, 1)
            with pool.Fori(0, F // 2 - 1) as it:
                for u in range(2):
                    pool.wait_ge(logit_made, it * 2 + u + 1)
                    bias(it * 2 + u + 2, u)

        @block.vector
        def _(v):
            nc.vector.memset(ones[:, :], 1.0).then_inc(ones_set, 1)
            v.wait_ge(w_in, 16 * N_W)
            v.wait_ge(kt_zero, 1)
            nc.vector.tensor_scalar(bg[:, :], bg[:, :], 0.5, None, ALU.mult).then_inc(bg_half, 1)

            def turn(s, u):
                if real(s + 2):
                    after(v, xn_turned, s + 2)
                    nc.vector.tensor_scalar(XN[:, :], X2[:, ds((s + 2) * C, C)], mean[:, ds(s + 2, 1)], rstd[:, ds(s + 2, 1)],
                                            ALU.subtract, ALU.mult).then_inc(xn_made, 1)
                if real(s):
                    after(v, score_done, s + 1)
                    after(v, bias_made, s + 1)
                    after(v, exp_b, s)
                    nc.vector.scalar_tensor_tensor(
                        out=LG[:, :, :].rearrange("p (j r) k -> p j (r k)", j=2),
                        in0=L[:, :, :], scalar=1.0 / math.sqrt(DH),
                        in1=BM[:, u, :, :].rearrange("p (j r) k -> p j (r k)", j=2),
                        op0=ALU.mult, op1=ALU.add).then_inc(logit_made, 1)
                if real(s - 2):
                    after(v, out_done, s - 1)
                    xs = X2[:, ds((s - 2) * C, C)]
                    nc.vector.tensor_tensor(xs, O[:, 0:C], xs, ALU.add).then_inc(x_added, 1)
                if real(s):
                    after(v, logit_made, s + 1)
                    nc.vector.tensor_reduce(NM[:, :], LG[:, :, :], AX.X, ALU.max, negate=True).then_inc(max_made, 1)
                if real(s - 1):
                    after(v, tb_done, s)
                    after(v, pv_done, s - 1)
                    nc.vector.tensor_copy(PT[:, 4:8, :], TB[:, :].rearrange("p (h k) -> p h k", k=T)).then_inc(tb_out, 1)
                if real(s + 1):
                    after(v, qk_done, s + 2)
                    after(v, score_done, s + 1)
                    for r in range(QUAD):
                        rows = slice(r * DH, (r + 1) * DH)
                        last = nc.vector.tensor_copy(KT[rows, :, r, :], TURN[rows, T:T + HD].rearrange("p (j k) -> p j k", j=2))
                    last.then_inc(k_out, 1)
                if real(s - 1):
                    after(v, exp_b, s)
                    after(v, og_made, s - 1)
                    nc.vector.reciprocal(RI[:, :], SM[:, 1 - u, :]).then_inc(inv_made, 1)
                    after(v, inv_made, s)
                    after(v, pv_done, s)
                    after(v, og_turned, s - 1)
                    nc.vector.scalar_tensor_tensor(
                        out=OG[:, :].rearrange("p (h d) -> p h d", d=DH), in0=O[:, 0:HD].rearrange("p (h d) -> p h d", d=DH),
                        scalar=0.5, in1=RI[:, :].unsqueeze(2).to_broadcast([P, HEADS, DH]),
                        op0=ALU.mult, op1=ALU.mult).then_inc(og_made, 1)
                if real(s + 2):
                    after(v, xn_turned, s + 3)
                    nc.vector.tensor_scalar(SNT[:, :], TURN[:, 0:T], lnw[:, :], lnb[:, :],
                                            ALU.mult, ALU.add).then_inc(sn_made, 1)
                if real(s - 1):
                    after(v, og_turned, s)
                    after(v, th_out, s)
                    after(v, out_done, s - 1)
                    nc.vector.scalar_tensor_tensor(out=OGT[:, :, :], in0=TH[:, 1 - u, :, :], scalar=1.0,
                                                   in1=TA[:, 0:HD].rearrange("p (a q) -> p a q", a=2),
                                                   op0=ALU.add, op1=ALU.mult).then_inc(ogt_made, 1)

            turns(v, turn)

        @block.scalar
        def _(act):
            act.wait_ge(w_in, 16 * N_W)
            act.wait_ge(kt_zero, 1)
            act.wait_ge(bg_half, 1)

            def softmax(s, u, first):
                for h in range(first, first + 4):
                    last = nc.scalar.activation(PR[:, u, h, :], LG[:, h, :], ACT.Exp, bias=NM[:, h:h + 1],
                                                accum_out=SM[:, u, h:h + 1])
                return last

            def turn(s, u):
                if real(s - 1):
                    after(act, ta_done, s)
                    after(act, pv_done, s - 1)
                    nc.scalar.activation(PT[:, 0:4, :], TA[:, :].rearrange("p (h k) -> p h k", k=T), ACT.Copy).then_inc(ta_out, 1)
                if real(s):
                    after(act, max_made, s + 1)
                    after(act, tb_done, s - 1)
                    after(act, inv_made, s - 1)
                    softmax(s, u, 0).then_inc(exp_a, 1)
                if real(s + 1):
                    after(act, qk_done, s + 2)
                    after(act, score_done, s + 1)
                    nc.scalar.activation(QT[:, :, :], QPS[:, 0:HD].rearrange("p (a q) -> p a q", a=2), ACT.Copy).then_inc(q_out, 1)
                if real(s):
                    softmax(s, u, 4).then_inc(exp_b, 1)
                if real(s + 1):
                    after(act, vg_done, s + 2)
                    after(act, pv_done, s)
                    nc.scalar.activation(V[:, 1 - u, :], PRV[:, 0:HD], ACT.Copy).then_inc(v_out, 1)
                    after(act, ogt_made, s)
                    for a in range(2):
                        last = nc.scalar.activation(TH[:, 1 - u, a, :], PRV[:, HD + a * T:HD + (a + 1) * T], ACT.Tanh,
                                                    scale=0.5, bias=bg[:, a:a + 1])
                    last.then_inc(th_out, 1)

            turns(act, turn)

        @block.tensor
        def _(pe):
            pe.wait_ge(w_in, 16 * N_W)
            pe.wait_ge(ones_set, 1)

            def turn(s, u):
                if real(s):
                    after(pe, q_out, s + 1)
                    after(pe, k_out, s + 1)
                    after(pe, logit_made, s)
                    for j in range(2):
                        last = nc.tensor.matmul(L[:, j, :], QT[:, j, :], KT[:, j, :, :].rearrange("p r k -> p (r k)"),
                                                start=True, stop=True)
                    last.then_inc(score_done, 1)
                if real(s - 2):
                    after(pe, ogt_made, s - 1)
                    for a in range(2):
                        nc.tensor.matmul(O[:, 0:C], OGT[:, a, :], wo[:, a, :], start=(a == 0), stop=False)
                    nc.tensor.matmul(O[:, 0:C], ones[:, :], bo[:, :], start=False, stop=True).then_inc(out_done, 1)
                if real(s - 1):
                    after(pe, exp_a, s)
                    after(pe, ogt_made, s - 1)
                    for h in range(4):
                        last = nc.tensor.transpose(TA[:, h * T:(h + 1) * T], PR[:, 1 - u, h, :], ident[:, :])
                    last.then_inc(ta_done, 1)
                    after(pe, exp_b, s)
                    after(pe, tb_out, s - 1)
                    for h in range(4):
                        last = nc.tensor.transpose(TB[:, h * T:(h + 1) * T], PR[:, 1 - u, 4 + h, :], ident[:, :])
                    last.then_inc(tb_done, 1)
                if real(s + 1):
                    after(pe, sn_made, s + 2)
                    after(pe, q_out, s + 1)
                    after(pe, k_out, s + 1)
                    for bank_of, w, col in ((QPS, wq, 0), (TURN, wk, T)):
                        for a in range(2):
                            last = nc.tensor.matmul(bank_of[:, col + a * T:col + (a + 1) * T], w[:, a * P:(a + 1) * P],
                                                    SNT[:, :], start=True, stop=True)
                    last.then_inc(qk_done, 1)
                if real(s - 1):
                    after(pe, ta_out, s)
                    after(pe, v_out, s)
                    after(pe, x_added, s - 1)
                    after(pe, og_made, s - 1)
                    for h in range(8):
                        if h == 4:
                            after(pe, tb_out, s)
                        last = nc.tensor.matmul(O[:, h * DH:(h + 1) * DH], PT[:, h, :], V[:, 1 - u, h * DH:(h + 1) * DH],
                                                start=True, stop=True)
                    last.then_inc(pv_done, 1)
                if real(s + 1):
                    after(pe, th_out, s + 1)
                    nc.tensor.matmul(PRV[:, 0:HD], SNT[:, :], wv[:, :], start=True, stop=True)
                    for a in range(2):
                        last = nc.tensor.matmul(PRV[:, HD + a * T:HD + (a + 1) * T], wg[:, a * P:(a + 1) * P], SNT[:, :],
                                                start=True, stop=True)
                    last.then_inc(vg_done, 1)
                if real(s + 2):
                    after(pe, xn_made, s + 3)
                    after(pe, sn_made, s + 2)
                    after(pe, k_out, s + 2)
                    nc.tensor.transpose(TURN[:, 0:T], XN[:, :], ident[:, :]).then_inc(xn_turned, 1)
                if real(s - 1):
                    after(pe, og_made, s)
                    for a in range(2):
                        last = nc.tensor.transpose(TA[:, a * T:(a + 1) * T], OG[:, a * P:(a + 1) * P], ident[:, :])
                    last.then_inc(og_turned, 1)

            turns(pe, turn)


def compact_edges(nc, sem, A, KG, KC, TRIPS, prefetch):
    with ExitStack() as ctx:
        local = lambda n, s, d=F32: ctx.enter_context(nc.sbuf_tensor("sb_" + n, s, d))
        SRC = local("src", [P, ECOLS], I32)
        DST, TMP = KG[:, 0:ECOLS].bitcast(I32), KC[:, 0:ECOLS].bitcast(I32)
        NEAR_N, ALL_N, TOTAL_N = slice(0, BLOCKS), slice(BLOCKS, 2 * BLOCKS), slice(2 * BLOCKS, 2 * BLOCKS + 1)
        CNT, CNA = local("counts", [P, 2 * BLOCKS + 1]), local("counts_max", [P, 2 * BLOCKS + 1])
        TOPS = local("tops", [P, 3])
        R, NEAR_P, REST_P, REST, BASE, TMP_I, GATHERED, CLAMPED, BOTH = range(9)
        N = local("trips", [P, 9], I32)
        ROUND = local("round_keys", [P, FOUND])
        TAKEN, JOIN = local("taken_keys", [P, TAKE]), local("join", [P, 1])
        e_in, chain, counted, summed = sem("edges_in"), sem("edge_chain"), sem("counted"), sem("count_max")
        trips_made, zeroed, carried = sem("trips_made"), sem("zeroed"), sem("carried")
        found, picked, rest_taken = sem("found"), sem("picked"), sem("rest_taken")
        block = ctx.enter_context(nc.Block())
        KEY = SRC[:, :].bitcast(F32)

        @block.sync
        def _(sp):
            sp.dma_start(SRC[:, :], A["edge_index"][0].rearrange("(p e) -> p e", p=P)).then_inc(e_in, 16)
            sp.dma_start(DST, A["edge_index"][1].rearrange("(p e) -> p e", p=P)).then_inc(e_in, 16)
            prefetch(sp)
            sp.wait_ge(e_in, 32)

        @block.gpsimd
        def _(pool):
            pool.wait_ge(counted, 1)
            pool.partition_all_reduce(CNA[:, :], CNT[:, :], P, bass.bass_isa.ReduceOp.max).then_inc(summed, 1)
            pool.memset(KG[:, :], 0.0)
            pool.memset(KC[:, :], 0.0).then_inc(zeroed, 1)

        @block.vector
        def _(v):
            link = Chain(v, chain)
            v.wait_ge(e_in, 32)
            link(nc.vector.tensor_scalar(TMP, SRC[:, :], TOKENS - 1, NEAR >> NODE_BITS, ALU.is_lt, ALU.mult))
            link(nc.vector.tensor_scalar(SRC[:, :], SRC[:, :], TOKENS - 1, None, ALU.min))
            link(nc.vector.scalar_tensor_tensor(out=TMP, in0=TMP, scalar=VALID >> NODE_BITS, in1=DST, op0=ALU.add, op1=ALU.add))
            link(nc.vector.tensor_scalar(TMP, TMP, NODE_BITS, None, ALU.logical_shift_left))
            link(nc.vector.tensor_scalar(DST, DST, TOKENS, -1, ALU.is_lt, ALU.mult))
            link(nc.vector.tensor_tensor(SRC[:, :], SRC[:, :], TMP, ALU.bitwise_or))
            link(nc.vector.tensor_tensor(SRC[:, :], SRC[:, :], DST, ALU.bitwise_and))
            link(nc.vector.tensor_scalar(TMP, SRC[:, :], 4, None, ALU.logical_shift_right))
            link(nc.vector.tensor_scalar(TMP, TMP, 22, 1, ALU.logical_shift_right, ALU.bitwise_and))
            link(nc.vector.tensor_reduce(CNT[:, NEAR_N], TMP.rearrange("p (b e) -> p b e", b=BLOCKS), AX.X, ALU.add))
            link(nc.vector.tensor_reduce(CNT[:, ALL_N], DST.rearrange("p (b e) -> p b e", b=BLOCKS), AX.X, ALU.add))
            link(nc.vector.tensor_reduce(CNT[:, TOTAL_N], CNT[:, NEAR_N], AX.X, ALU.add))
            nc.vector.tensor_scalar(CNT[:, ALL_N], CNT[:, ALL_N], -1.0, None, ALU.mult).then_inc(counted, 1)
            v.wait_ge(summed, 1)
            link(nc.vector.tensor_reduce(TOPS[:, 0:2], CNA[:, 0:2 * BLOCKS].rearrange("p (a b) -> p a b", a=2), AX.X, ALU.max))
            link(nc.vector.tensor_copy(TOPS[:, 2:3], CNA[:, TOTAL_N]))
            n = lambda k: N[:, k:k + 1]

            def step(out, x, a, op0, b=None, op1=None):
                link(nc.vector.tensor_scalar(n(out), x, a, b, op0, *((op1,) if op1 is not None else ())))
            step(TMP_I, TOPS[:, 0:1], SLOT - 1.0, ALU.add)
            step(TMP_I, n(TMP_I), 3, ALU.logical_shift_right)
            step(TMP_I, n(TMP_I), 1, ALU.max, SEARCHES - 1, ALU.add)
            step(TMP_I, n(TMP_I), 205, ALU.mult)
            step(R, n(TMP_I), 10, ALU.logical_shift_right)
            step(NEAR_P, TOPS[:, 2:3], PAIR - 1.0, ALU.add)
            step(NEAR_P, n(NEAR_P), 4, ALU.logical_shift_right)
            step(NEAR_P, n(NEAR_P), STRIDE - 1, ALU.min, 1, ALU.max)
            step(REST_P, n(NEAR_P), -1, ALU.mult, STRIDE, ALU.add)
            step(REST, TOPS[:, 1:2], SLOT - 1.0, ALU.add)
            step(REST, n(REST), 3, ALU.logical_shift_right)
            step(TMP_I, n(R), -SEARCHES, ALU.mult)
            link(nc.vector.tensor_tensor(n(REST), n(REST), n(TMP_I), ALU.add))
            step(REST, n(REST), 1, ALU.max)
            step(BASE, n(R), STRIDE, ALU.mult)
            link(nc.vector.tensor_tensor(n(BASE), n(BASE), n(NEAR_P), ALU.subtract))
            step(TMP_I, n(R), STRIDE, ALU.mult, -STRIDE, ALU.add)
            link(nc.vector.tensor_tensor(n(GATHERED), n(TMP_I), n(NEAR_P), ALU.add))
            step(TMP_I, n(REST), TAKE // PAIR, ALU.mult)
            link(nc.vector.tensor_tensor(n(CLAMPED), n(TMP_I), n(BASE), ALU.add))
            step(BOTH, n(CLAMPED), WITH - 1, ALU.add)
            step(BOTH, n(BOTH), int(math.log2(WITH)), ALU.logical_shift_right)
            step(TMP_I, n(GATHERED), -1, ALU.add)
            link(nc.vector.tensor_tensor(n(BOTH), n(BOTH), n(TMP_I), ALU.min))
            link(nc.vector.tensor_scalar(TRIPS[:, 0:1], n(BOTH), 1, None, ALU.max))
            link(nc.vector.tensor_tensor(TRIPS[:, 1:2], n(GATHERED), TRIPS[:, 0:1], ALU.subtract))
            link(nc.vector.tensor_scalar(TRIPS[:, 1:2], TRIPS[:, 1:2], 1, None, ALU.max))
            step(TMP_I, TRIPS[:, 0:1], WITH, ALU.mult)
            link(nc.vector.tensor_tensor(TRIPS[:, 2:3], n(CLAMPED), n(TMP_I), ALU.subtract))
            nc.vector.tensor_scalar(TRIPS[:, 2:3], TRIPS[:, 2:3], 1, None, ALU.max).then_inc(trips_made, 1)
            v.wait_ge(trips_made, 1)
            trips = lambda k, top, least=1: v.value_load(N[0:1, k:k + 1], min_val=least, max_val=top)
            rounds, near_pairs, rest_pairs = trips(R, ROUNDS), trips(NEAR_P, STRIDE - 1), trips(REST_P, STRIDE - 1)
            rest, rest_base = trips(REST, BCOLS // SLOT), trips(BASE, ROUNDS * STRIDE - 1)
            v.wait_ge(zeroed, 1)
            v.sem_inc(found, AHEAD)
            v.sem_inc(picked, AHEAD)
            v.sem_inc(rest_taken, AHEAD)

            def wait(semaphore, count):
                v.wait_ge(semaphore, count)
                v.sem_inc(carried, 1)

            def search(keys, out):
                for b in range(BLOCKS):
                    last = nc.vector.max(out[:, b * SLOT:(b + 1) * SLOT], keys[:, b * BCOLS:(b + 1) * BCOLS])
                yield last
                for b in range(BLOCKS):
                    blk = keys[:, b * BCOLS:(b + 1) * BCOLS]
                    last = nc.vector.match_replace(blk, out[:, b * SLOT:(b + 1) * SLOT], blk, 0.0)
                yield last

            def pick(start, pairs, first, KEEP):
                with v.Fori(0, pairs) as i:
                    n_done = (start + i) * 5 + AHEAD
                    for k in range(2):
                        wait(picked, n_done + 2 * k)
                        nc.vector.max(TAKEN[:, k * SLOT:(k + 1) * SLOT], ROUND[:, :]).then_inc(picked, 1)
                        wait(picked, n_done + 2 * k + 1)
                        nc.vector.match_replace(ROUND[:, :], TAKEN[:, k * SLOT:(k + 1) * SLOT], ROUND[:, :], 0.0).then_inc(picked, 1)
                    wait(picked, n_done + 4)
                    nc.vector.tensor_copy(KEEP[:, ds((first + i) * PAIR, PAIR)], TAKEN[:, 0:PAIR]).then_inc(picked, 1)

            with v.Fori(0, rounds) as r:
                for k in range(SEARCHES):
                    steps = search(KEY, ROUND[:, k * TAKE:(k + 1) * TAKE])
                    wait(found, (r * SEARCHES + k) * 2 + AHEAD)
                    if k == 0:
                        wait(picked, r * (STRIDE * 5) + AHEAD)
                    next(steps).then_inc(found, 1)
                    wait(found, (r * SEARCHES + k) * 2 + 1 + AHEAD)
                    next(steps).then_inc(found, 1)
                wait(found, (r + 1) * (SEARCHES * 2) + AHEAD)
                pick(r * STRIDE, near_pairs, r * STRIDE, KG)
                pick(r * STRIDE + near_pairs, rest_pairs, r * STRIDE, KC)
            link(nc.vector.memset(JOIN[:, :], 0.0))
            with v.Fori(0, rest) as i:
                steps = search(KEY, TAKEN[:, :])
                wait(rest_taken, i * 3 + AHEAD)
                next(steps).then_inc(rest_taken, 1)
                wait(rest_taken, i * 3 + 1 + AHEAD)
                next(steps).then_inc(rest_taken, 1)
                wait(rest_taken, i * 3 + 2 + AHEAD)
                at = nc.s_assert_within(rest_base * PAIR + i * TAKE, 0, KCOLS - P - TAKE, skip_runtime_bounds_check_because=
                                        "rest and rest_base both follow from the rounds, and KC has room for any number of them")
                nc.vector.tensor_copy(KC[:, ds(at, TAKE)], TAKEN[:, :]).then_inc(rest_taken, 1)
            link(nc.vector.memset(JOIN[:, :], 0.0))


def turn_tokens(nc, sem, tag, ctx, X2, ident, mean, rstd, TT, W, width, OUT, eps, load_w):
    local = lambda n, s, d=F32: ctx.enter_context(nc.sbuf_tensor(f"sb_{tag}_{n}", s, d))
    pbank = lambda n: ctx.enter_context(nc.psum_tensor(f"{tag}_{n}", [P, BANK], F32))
    XN = local("xn", [P, 2, BANK])
    SG = local("sg", [P, 2, BANK])
    bn = local("bn", [P, TILES * 6])
    tmp = local("tmp", [P, 2, TILES])
    pt = [pbank(f"pt{k}") for k in range(2)]
    ph = [pbank(f"ph{k}") for k in range(2)]
    w_in, chain, var, root = sem(tag + "_w_in"), sem(tag + "_chain"), sem(tag + "_var"), sem(tag + "_root")
    normed, turned, staged, kept = (sem(f"{tag}_{n}") for n in ("normed", "turned", "staged", "kept"))
    mixed, mixed_out = sem(tag + "_mixed"), sem(tag + "_mixed_out")
    block = ctx.enter_context(nc.Block())

    @block.sync
    def _(sp):
        sp.dma_start(W, load_w, allow_slow_non_contiguous=True).then_inc(w_in, 16)
        sp.wait_ge(w_in, 16)

    @block.scalar
    def _(act):
        act.wait_ge(var, 1)
        act.sem_inc(mixed, AHEAD)
        nc.scalar.activation(tmp[:, 0, :], tmp[:, 1, :], ACT.Sqrt).then_inc(root, 1)
        with act.Fori(0, GROUPS // 2) as i:
            for u in range(2):
                g = i * 2 + u
                act.wait_ge(turned, g + 1 + AHEAD)
                nc.scalar.activation(TT[:, ds(g * BANK, BANK)], pt[u][:, :], ACT.Copy)
                act.wait_ge(mixed, i * 2 + AHEAD)
                nc.scalar.activation(SG[:, u, :], pt[u][:, :], ACT.Copy).then_inc(staged, 1)

    @block.vector
    def _(v):
        link = Chain(v, chain)
        v.sem_inc(turned, AHEAD)
        layer_statistics(nc, v, link, X2, bn, mean, rstd, tmp[:, 0, :])
        link(nc.vector.tensor_scalar(tmp[:, 1, :], rstd, eps, None, ALU.add))
        v.sem_inc(var, 1)
        v.wait_ge(root, 1)
        link(nc.vector.reciprocal(rstd, tmp[:, 0, :]))

        def out(g, u):
            v.wait_ge(mixed, g + 1 + AHEAD)
            nc.vector.tensor_copy(OUT[:, ds(g * GROUP, GROUP), :],
                                  ph[u][:, 0:GROUP * width].rearrange("p (t w) -> p t w", w=width)).then_inc(mixed_out, 1)

        with v.Fori(0, GROUPS // 2) as i:
            for u in range(2):
                g = i * 2 + u
                v.wait_ge(turned, i * 2 + AHEAD)
                for k in range(GROUP):
                    t = g * GROUP + k
                    last = nc.vector.tensor_scalar(XN[:, u, k * P:(k + 1) * P], X2[:, ds(t * C, C)],
                                                   mean[:, ds(t, 1)], rstd[:, ds(t, 1)], ALU.subtract, ALU.mult)
                last.then_inc(normed, 1)
            for u in range(2):
                out(i * 2 + u, u)

    @block.tensor
    def _(pe):
        pe.wait_ge(w_in, 16)
        pe.sem_inc(staged, AHEAD)
        pe.sem_inc(mixed_out, AHEAD)
        with pe.Fori(0, GROUPS // 2) as i:
            for u in range(2):
                g = i * 2 + u
                pe.wait_ge(normed, g + 1)
                pe.wait_ge(staged, i * 2 + AHEAD)
                for k in range(GROUP):
                    last = nc.tensor.transpose(pt[u][:, k * P:(k + 1) * P], XN[:, u, k * P:(k + 1) * P], ident[:, :])
                last.then_inc(turned, 1)
            for u in range(2):
                g = i * 2 + u
                pe.wait_ge(staged, g + 1 + AHEAD)
                pe.wait_ge(mixed_out, i * 2 + AHEAD)
                for k in range(GROUP):
                    last = nc.tensor.matmul(ph[u][:, k * width:(k + 1) * width], SG[:, u, k * P:(k + 1) * P], W,
                                            start=True, stop=True)
                last.then_inc(mixed, 1)


def graph_tables(nc, sem, A, H, GT, SRC_T, DST_T, LAST):
    with ExitStack() as ctx:
        local = lambda n, s, d=F32: ctx.enter_context(nc.sbuf_tensor("sb_gt_" + n, s, d))
        ATT = local("att", [P, 2, GF])
        PROD = local("prod", [P, TILES, GF])
        S, D = local("s", [P, TILES, GHEADS]), local("d", [P, TILES, GHEADS])
        M = local("m", [P, TILES, GHEADS])
        TOP, TOPA = local("top", [P, GHEADS]), local("topa", [P, GHEADS])
        ROWS = local("rows", [P, TILES, ROW])
        a_in, chain, topped, topped_all = sem("att_in"), sem("gt_chain"), sem("top"), sem("top_all")
        args, exps, rows_in, stored, last_in = sem("gt_args"), sem("gt_exps"), sem("gt_rows"), sem("gt_stored"), sem("last_in")
        block = ctx.enter_context(nc.Block())

        @block.sync
        def _(sp):
            for k, n in enumerate(("att_src", "att_dst")):
                sp.dma_start(ATT[:, k, :], A[n].rearrange("h e -> (h e)").partition_broadcast(P)).then_inc(a_in, 16)
            sp.wait_ge(rows_in, 1)
            sp.wait_ge(exps, 4)
            sp.dma_start(SRC_T.rearrange("(s r) w -> r s w", r=P), ROWS[:, :, :]).then_inc(stored, 16)
            sp.dma_start(DST_T.rearrange("(s r) w -> r s w", r=P), GT[:, :, 2 * GHEADS:]).then_inc(stored, 16)
            sp.wait_ge(stored, 32)
            sp.dma_start(LAST[:, :], SRC_T[TOKENS - 1, :].partition_broadcast(P)).then_inc(last_in, 16)
            sp.wait_ge(last_in, 16)

        @block.gpsimd
        def _(pool):
            pool.wait_ge(topped, 1)
            pool.partition_all_reduce(TOPA[:, :], TOP[:, :], P, bass.bass_isa.ReduceOp.max).then_inc(topped_all, 1)

        @block.scalar
        def _(act):
            act.wait_ge(args, 1)
            nc.scalar.activation(GT[:, :, 0:4], S[:, :, :], ACT.Exp).then_inc(exps, 1)
            nc.scalar.activation(GT[:, :, 4:8], S[:, :, :], ACT.Exp, scale=0.2).then_inc(exps, 1)
            act.wait_ge(args, 2)
            nc.scalar.activation(GT[:, :, 8:12], M[:, :, :], ACT.Exp).then_inc(exps, 1)
            nc.scalar.activation(GT[:, :, 12:16], D[:, :, :], ACT.Exp).then_inc(exps, 1)

        @block.vector
        def _(v):
            link = Chain(v, chain)
            v.wait_ge(a_in, 32)
            for k, dst in enumerate((S, D)):
                link(nc.vector.tensor_tensor(PROD[:, :, :], H[:, :, :], ATT[:, k, :].unsqueeze(1).to_broadcast([P, TILES, GF]),
                                             ALU.mult))
                link(nc.vector.tensor_reduce(dst[:, :, :], PROD[:, :, :].rearrange("p s (h e) -> p s h e", e=EXPERTS0),
                                             AX.X, ALU.add))
            link(nc.vector.tensor_reduce(TOP[:, :], S[:, :, :].rearrange("p s h -> p h s"), AX.X, ALU.max))
            v.sem_inc(topped, 1)
            v.wait_ge(topped_all, 1)
            top = TOPA[:, :].unsqueeze(1).to_broadcast([P, TILES, GHEADS])
            link(nc.vector.tensor_tensor(S[:, :, :], S[:, :, :], top, ALU.subtract))
            v.sem_inc(args, 1)
            link(nc.vector.tensor_tensor(D[:, :, :], D[:, :, :], top, ALU.add))
            link(nc.vector.scalar_tensor_tensor(out=M[:, :, :], in0=D[:, :, :], scalar=0.2, in1=D[:, :, :],
                                                op0=ALU.mult, op1=ALU.max))
            link(nc.vector.tensor_tensor(PROD[:, :, 0:4], D[:, :, :], M[:, :, :], ALU.subtract))
            link(nc.vector.scalar_tensor_tensor(out=D[:, :, :], in0=D[:, :, :], scalar=0.2, in1=M[:, :, :],
                                                op0=ALU.mult, op1=ALU.subtract))
            link(nc.vector.tensor_copy(M[:, :, :], PROD[:, :, 0:4]))
            v.sem_inc(args, 1)
            link(nc.vector.tensor_copy(ROWS[:, :, 0:GF], H[:, :, :]))
            v.wait_ge(exps, 2)
            nc.vector.tensor_copy(ROWS[:, :, GF:], GT[:, :, 0:8]).then_inc(rows_in, 1)


def graph_edges(nc, sem, KG, KC, SRC_T, DST_T, TRIPS, SUMS, CN):
    with ExitStack() as ctx:
        local = lambda n, s, d=F32: ctx.enter_context(nc.sbuf_tensor("sb_ge_" + n, s, d))
        iota_i = local("iota_i", [P, P], I32)
        iota_f = local("iota_f", [P, P])
        IDX = local("idx", [P, 2, 2, SLOT], I32)
        LO, HI = local("lo", [P, 2, SLOT], I32), local("hi", [P, 2, SLOT], I32)
        HIF = local("hif", [P, 2, SLOT])
        GS, GD = local("gs", [P, 2, SLOT, ROW]), local("gd", [P, 2, SLOT, 2 * GHEADS])
        W2 = local("w2", [P, SLOT, 2 * GHEADS])
        MSG = local("msg", [P, 2, SLOT, PART])
        OL = local("ol", [P, 2, SLOT, P])
        NB = 4
        B = local("b", [P, NB, TILES, PART])
        HALF = PAIR * WITH // 2
        PER = HALF // SLOT
        CLO, CHI = local("c_lo", [P, HALF], I32), local("c_hi", [P, HALF], I32)
        CLN = local("c_minus_lo", [P, 2, HALF])
        NC = 4
        CL, CH = local("c_onehot_lo", [P, NC, PER, P], BF16), local("c_onehot_hi", [P, NC, PER, TILES], BF16)
        AWAY = local("c_distance", [P, 2, PER, P], BF16)
        CHUNKS = ((0, 22), (22, 22), (44, 20))
        ACC = ctx.enter_context(nc.psum_tensor("acc", [P, 3, BANK], F32))
        COUNT = ctx.enter_context(nc.psum_tensor("p_count", [P, BANK], F32))
        gathers_on, iota_made = sem("ge_gathers_on"), sem("ge_iota")
        iota_cast = sem("ge_iota_cast")
        decoded, gathered_s, gathered_d = sem("ge_decoded"), [sem(f"ge_src{u}") for u in range(2)], [sem(f"ge_dst{u}") for u in range(2)]
        products, weights, messages, ol_made = sem("ge_products"), sem("ge_weights"), sem("ge_messages"), sem("ge_ol")
        b_made, b_free, half_used, acc_done, chain = sem("ge_b_made"), sem("ge_b_free"), sem("ge_half_used"), sem("ge_done"), sem("ge_chain")
        c_decoded, hot_hi, hot_lo, hot_free = sem("ge_c_decoded"), sem("ge_hot_hi"), sem("ge_hot_lo"), sem("ge_hot_free")
        lo_ready, away = sem("ge_lo_ready"), sem("ge_distance")
        block = ctx.enter_context(nc.Block())
        trips = lambda engine, k, top: engine.value_load(TRIPS[0:1, k:k + 1], min_val=1, max_val=top)
        MOST = ROUNDS * STRIDE
        MOST_BOTH = -(-(KCOLS - P) // (PAIR * WITH))
        both_trips = lambda engine: trips(engine, 0, MOST_BOTH)
        gather_trips = lambda engine: trips(engine, 1, MOST)
        count_trips = lambda engine: trips(engine, 2, (KCOLS - P) // PAIR)

        @block.gpsimd
        def _(pool):
            pool.iota(iota_i[:, :], pattern=[[1, P]], base=0, channel_multiplier=0).then_inc(iota_made, 1)
            n_both, n_gather = both_trips(pool), gather_trips(pool)

            def gather(n, u):
                pool.wait_ge(decoded, n + 1)
                pool.wait_ge(messages, n - 1 + 2)
                pool.sem_inc(gathers_on, 1)
                for k in range(SLOT):
                    pool.indirect_dma_start(GS[:, u, k, :], None, SRC_T,
                                            bass.IndirectOffsetOnAxis(ap=IDX[:, u, 0, k:k + 1], axis=0)).then_inc(gathered_s[u], 16)
                    pool.indirect_dma_start(GD[:, u, k, :], None, DST_T,
                                            bass.IndirectOffsetOnAxis(ap=IDX[:, u, 1, k:k + 1], axis=0)).then_inc(gathered_d[u], 16)

            n_all = n_both + n_gather
            with pool.Fori(0, n_all) as i:
                for u in range(2):
                    gather(i * 2 + u, u)
            gather(n_all * 2, 0)

        @block.scalar
        def _(act):
            act.wait_ge(iota_cast, 1)
            act.sem_inc(away, AHEAD)

            def one_hot_lo(made, u, k):
                act.wait_ge(away, made * 2 + AHEAD)
                for j in range(PER):
                    last = nc.scalar.activation(AWAY[:, k % 2, j, :], iota_f[:, :], ACT.Abs,
                                                bias=CLN[:, u, k * PER + j:k * PER + j + 1])
                last.then_inc(away, 1)
                act.wait_ge(hot_free, made + 1)
                act.wait_ge(away, made * 2 + 1 + AHEAD)
                nc.scalar.activation(CL[:, k % NC, :, :], AWAY[:, k % 2, :, :], ACT.Relu, bias=1.0, scale=-1.0).then_inc(away, 1)
                act.wait_ge(away, made * 2 + 2 + AHEAD)
                act.sem_inc(hot_lo, 1)

            n_both, n_count = both_trips(act), count_trips(act)
            with act.Fori(0, n_both) as i:
                for u in range(2):
                    act.wait_ge(lo_ready, i * 2 + u + 1)
                    for k in range(SLOT):
                        one_hot_lo((i * 2 + u) * SLOT + k, u, k)
            with act.Fori(0, n_count) as i:
                act.wait_ge(lo_ready, n_both * 2 + i + 1)
                for k in range(PAIR // PER):
                    one_hot_lo(n_both * (2 * SLOT) + i * (PAIR // PER) + k, 0, k)

        @block.vector
        def _(v):
            v.wait_ge(iota_made, 1)
            v.sem_inc(b_made, AHEAD)
            v.sem_inc(half_used, AHEAD)
            v.sem_inc(messages, 2)
            v.sem_inc(hot_hi, AHEAD)
            v.sem_inc(hot_lo, 2 * SLOT)
            nc.vector.tensor_copy(iota_f[:, :], iota_i[:, :]).then_inc(iota_cast, 1)

            def decode(n, u):
                at = nc.s_assert_within(n * SLOT, 0, KCOLS - SLOT, skip_runtime_bounds_check_because=
                                        "the trips are made from the number of KG's slots in use")
                bits = KG[:, ds(at, SLOT)].bitcast(I32)
                nc.vector.tensor_scalar(IDX[:, u, 0, :], bits, TOKENS - 1, None, ALU.bitwise_and)
                nc.vector.tensor_scalar(IDX[:, u, 1, :], bits, NODE_BITS, TOKENS - 1, ALU.logical_shift_right, ALU.bitwise_and)
                nc.vector.tensor_scalar(LO[:, u, :], bits, NODE_BITS, P - 1, ALU.logical_shift_right, ALU.bitwise_and)
                nc.vector.tensor_scalar(HI[:, u, :], bits, NODE_BITS + LO_BITS, (VALID >> 20) + TILES - 1,
                                        ALU.logical_shift_right, ALU.bitwise_and).then_inc(decoded, 1)

            def decode_clamped(first, slots):
                bits = KC[:, ds(first, slots)].bitcast(I32)
                nc.vector.tensor_scalar(CLO[:, 0:slots], bits, NODE_BITS, P - 1, ALU.logical_shift_right, ALU.bitwise_and)
                nc.vector.tensor_scalar(CHI[:, 0:slots], bits, NODE_BITS + LO_BITS, (VALID >> 20) + TILES - 1,
                                        ALU.logical_shift_right, ALU.bitwise_and).then_inc(c_decoded, 1)

            def ready_clamped(slots, u):
                nc.vector.tensor_scalar(CLN[:, u, 0:slots], CLO[:, 0:slots], -1.0, None, ALU.mult).then_inc(lo_ready, 1)
                nc.vector.tensor_scalar(CHI[:, 0:slots], CHI[:, 0:slots], VALID >> 20, None, ALU.subtract).then_inc(c_decoded, 1)

            def one_hot_hi(k):
                nc.vector.tensor_tensor(CH[:, k % NC, :, :], iota_i[:, 0:TILES].unsqueeze(1).to_broadcast([P, PER, TILES]),
                                        CHI[:, k * PER:(k + 1) * PER].unsqueeze(2).to_broadcast([P, PER, TILES]),
                                        ALU.is_equal).then_inc(hot_hi, 1)

            def low_bits(n, u):
                after(v, decoded, n + 1)
                after(v, half_used, n - 1 + AHEAD)
                nc.vector.tensor_scalar(HIF[:, u, :], HI[:, u, :], VALID >> 20, None, ALU.subtract)
                nc.vector.tensor_tensor(OL[:, u, :, :], iota_f[:, :].unsqueeze(1).to_broadcast([P, SLOT, P]),
                                        LO[:, u, :].unsqueeze(2).to_broadcast([P, SLOT, P]), ALU.is_equal).then_inc(ol_made, 1)

            def factors(n, i, u):
                v.wait_ge(gathered_s[u], (i + 1) * 16 * SLOT)
                v.wait_ge(gathered_d[u], (i + 1) * 16 * SLOT)
                after(v, weights, n)
                nc.vector.tensor_tensor(W2[:, :, :], GS[:, u, :, GF:], GD[:, u, :, :], ALU.mult).then_inc(products, 1)

            def weigh(n, u):
                after(v, products, n + 1)
                after(v, b_made, (n - 1) * SLOT + AHEAD)
                nc.vector.tensor_tensor(MSG[:, u, :, GF:], W2[:, :, 0:GHEADS], W2[:, :, GHEADS:], ALU.max).then_inc(weights, 1)

            def message(n, u):
                after(v, weights, n + 1)
                nc.vector.tensor_tensor(MSG[:, u, :, 0:GF].rearrange("p k (h e) -> p k h e", e=EXPERTS0),
                                        GS[:, u, :, 0:GF].rearrange("p k (h e) -> p k h e", e=EXPERTS0),
                                        MSG[:, u, :, GF:].unsqueeze(3).to_broadcast([P, SLOT, GHEADS, EXPERTS0]),
                                        ALU.mult).then_inc(messages, 1)

            def next_numbers(n, u):
                v.wait_ge(ol_made, n + 1)
                decode(n + 2, u)

            def half(n, i, u, counting):
                following = n + 1, 1 - u
                between = {3: lambda: low_bits(*following), 4: lambda: factors(n + 1, i + u, 1 - u), 5: lambda: weigh(*following),
                           6: lambda: message(*following), 7: lambda: next_numbers(*following)}
                if counting:
                    v.wait_ge(hot_hi, n * SLOT + AHEAD)
                    decode_clamped(n * HALF, HALF)
                v.wait_ge(messages, n + 1 + 2)
                for k in range(SLOT):
                    v.wait_ge(b_free, n * SLOT + k + 1)
                    nc.vector.scalar_tensor_tensor(
                        out=B[:, k % NB, :, :], in0=iota_f[:, 0:TILES].unsqueeze(2).to_broadcast([P, TILES, PART]),
                        scalar=HIF[:, u, k:k + 1], in1=MSG[:, u, k, :].unsqueeze(1).to_broadcast([P, TILES, PART]),
                        op0=ALU.is_equal, op1=ALU.mult).then_inc(b_made, 1)
                    if counting:
                        if k == 0:
                            v.wait_ge(c_decoded, n * 2 + 1)
                            v.wait_ge(hot_lo, (n + 1) * SLOT)
                            ready_clamped(HALF, u)
                            v.wait_ge(c_decoded, n * 2 + 2)
                        v.wait_ge(hot_free, n * SLOT + k + 1)
                        one_hot_hi(k)
                    if k in between:
                        between[k]()

            n_both, n_gather, n_count = both_trips(v), gather_trips(v), count_trips(v)
            v.wait_ge(iota_cast, 1)
            decode(0, 0)
            decode(1, 1)
            low_bits(0, 0)
            factors(0, 0, 0)
            weigh(0, 0)
            message(0, 0)
            next_numbers(0, 0)
            with v.Fori(0, n_both) as i:
                for u in range(2):
                    half(i * 2 + u, i, u, True)
            with v.Fori(0, n_gather) as i:
                for u in range(2):
                    half((n_both + i) * 2 + u, n_both + i, u, False)
            with v.Fori(0, n_count) as i:
                made = n_both * (2 * SLOT) + i * (PAIR // PER)
                v.wait_ge(hot_hi, made + AHEAD)
                at = nc.s_assert_within(n_both * (PAIR * WITH) + i * PAIR, 0, KCOLS - PAIR, skip_runtime_bounds_check_because=
                                        "the trips are made from the number of KC's slots in use")
                decode_clamped(at, PAIR)
                v.wait_ge(c_decoded, n_both * 4 + i * 2 + 1)
                v.wait_ge(hot_lo, made + 2 * SLOT)
                ready_clamped(PAIR, 0)
                v.wait_ge(c_decoded, n_both * 4 + i * 2 + 2)
                for k in range(PAIR // PER):
                    v.wait_ge(hot_free, made + k + 1)
                    one_hot_hi(k)
            v.wait_ge(acc_done, 1)
            for c, (h0, hn) in enumerate(CHUNKS):
                last = nc.vector.tensor_copy(SUMS[:, h0:h0 + hn, :], ACC[:, c, 0:hn * PART].rearrange("p (h w) -> p h w", w=PART))
            last.then_inc(chain, 1)
            nc.vector.tensor_copy(CN[:, :], COUNT[:, 0:TILES]).then_inc(chain, 1)
            v.wait_ge(chain, 2)

        @block.tensor
        def _(pe):
            n_both, n_gather, n_count = both_trips(pe), gather_trips(pe), count_trips(pe)
            zero = KG[:, KG.shape[1] - P:]
            zero_b = zero.bitcast(BF16)

            def add(left, right, **flags):
                for c, (h0, hn) in enumerate(CHUNKS):
                    last = nc.tensor.matmul(ACC[:, c, 0:hn * PART], left, right(h0, hn), skip_group_check=True, **flags)
                return last

            def count(q, made):
                pe.wait_ge(hot_hi, made + 1 + AHEAD)
                pe.wait_ge(hot_lo, made + 1 + 2 * SLOT)
                for k in range(PER):
                    last = nc.tensor.matmul(COUNT[:, 0:TILES], CL[:, q, k, :], CH[:, q, k, :], start=False, stop=False,
                                            skip_group_check=True)
                last.then_inc(hot_free, 1)

            def half(n, u, counting):
                pe.wait_ge(ol_made, n + 1)
                for k in range(SLOT):
                    pe.wait_ge(b_made, n * SLOT + k + 1 + AHEAD)
                    b = B[:, k % NB, :, :].rearrange("p h w -> p (h w)")
                    last = add(OL[:, u, k, :], lambda h0, hn: b[:, h0 * PART:(h0 + hn) * PART], start=False, stop=False)
                    last.then_inc(b_free, 1)
                    if counting and k > 0:
                        count((k - 1) % NC, n * SLOT + k - 1)
                if counting:
                    count((SLOT - 1) % NC, n * SLOT + SLOT - 1)
                pe.wait_ge(b_free, (n + 1) * SLOT + NB)
                pe.sem_inc(half_used, 1)

            zeros = lambda h0, hn: zero.unsqueeze(1).to_broadcast([P, 4, P])[:, :, 0:hn * 5]
            pe.sem_inc(b_free, NB)
            pe.sem_inc(hot_free, NC)
            add(zero, zeros, start=True, stop=False)
            nc.tensor.matmul(COUNT[:, 0:TILES], zero_b[:, 0:P], zero_b[:, 0:TILES], start=True, stop=False, skip_group_check=True)
            with pe.Fori(0, n_both) as i:
                for u in range(2):
                    half(i * 2 + u, u, True)
            with pe.Fori(0, n_gather) as i:
                for u in range(2):
                    half((n_both + i) * 2 + u, u, False)
            with pe.Fori(0, n_count) as i:
                for k in range(PAIR // PER):
                    count(k % NC, n_both * (2 * SLOT) + i * (PAIR // PER) + k)
            nc.tensor.matmul(COUNT[:, 0:TILES], zero_b[:, 0:P], zero_b[:, 0:TILES], start=False, stop=True, skip_group_check=True)
            add(zero, zeros, start=False, stop=True).then_inc(acc_done, 1)


def rank_gates(nc, link, score, experts, tmp, tmp2, tmp3, earlier, keep):
    shape = [P, TILES, experts, experts]
    view = lambda t: t.rearrange("p (s a b) -> p s a b", a=experts, b=experts)
    this, other = score.unsqueeze(3).to_broadcast(shape), score.unsqueeze(2).to_broadcast(shape)
    flat = lambda t: t
    link(nc.vector.tensor_tensor(view(tmp), other, this, ALU.is_gt))
    link(nc.vector.tensor_tensor(view(tmp2), other, this, ALU.is_equal))
    link(nc.vector.tensor_tensor(view(tmp2), view(tmp2),
                                 earlier.unsqueeze(1).to_broadcast(shape), ALU.mult))
    link(nc.vector.tensor_tensor(tmp, tmp, tmp2, ALU.add))
    link(nc.vector.tensor_reduce(keep, view(tmp), AX.X, ALU.add))
    link(nc.vector.tensor_scalar(keep, keep, 2.0, None, ALU.is_lt))


def earlier_mask(nc, pool, earlier, experts, made):
    pool.memset(earlier, 1.0).then_inc(made, 1)
    pool.wait_ge(made, 1)
    pool.affine_select(out=earlier, in_=earlier, compare_op=ALU.is_gt, fill=0.0, base=0,
                       pattern=[[1, experts], [-1, experts]], channel_multiplier=0).then_inc(made, 1)


def graph_gates(nc, sem, A, H, GT, LAST, SUMS, CN, G):
    with ExitStack() as ctx:
        local = lambda n, s, d=F32: ctx.enter_context(nc.sbuf_tensor("sb_gg_" + n, s, d))
        vec = local("vec", [P, 3, GF])
        W2 = local("w2", [P, TILES, 8])
        W1 = local("w1", [P, TILES, 4])
        M = local("m", [P, TILES, GF])
        AG = local("ag", [P, TILES, GF])
        st = local("st", [P, 4, TILES])
        RD = local("rd", [P, TILES, 4])
        t1, t2 = local("t1", [P, TILES * 16]), local("t2", [P, TILES * 16])
        earlier = local("earlier", [P, 4, 4])
        SC, KEEP = local("sc", [P, TILES, 4]), local("keep", [P, TILES, 4])
        v_in, made, chain, var, root, shifted, exped = (sem("gg_" + n) for n in ("in", "made", "chain", "var", "root", "shifted", "exped"))
        block = ctx.enter_context(nc.Block())

        @block.sync
        def _(sp):
            for k, n in enumerate(("b_gat", "ln_gamma", "ln_beta")):
                sp.dma_start(vec[:, k, :], A[n].partition_broadcast(P)).then_inc(v_in, 16)
            sp.wait_ge(v_in, 48)

        @block.gpsimd
        def _(pool):
            earlier_mask(nc, pool, earlier[:, :, :], 4, made)

        @block.scalar
        def _(act):
            act.wait_ge(var, 1)
            nc.scalar.activation(st[:, 2, :], st[:, 1, :], ACT.Sqrt).then_inc(root, 1)
            act.wait_ge(shifted, 1)
            nc.scalar.activation(SC[:, :, :], SC[:, :, :], ACT.Exp).then_inc(exped, 1)

        @block.vector
        def _(v):
            link = Chain(v, chain)
            h4 = lambda t: t.rearrange("p s (h e) -> p s h e", e=4)
            w4 = lambda: W1[:, :, :].unsqueeze(3).to_broadcast([P, TILES, 4, 4])
            v.wait_ge(v_in, 48)
            link(nc.vector.tensor_tensor(W2[:, :, :], GT[:, :, 0:8], GT[:, :, 8:16], ALU.mult))
            link(nc.vector.tensor_tensor(W1[:, :, :], W2[:, :, 0:4], W2[:, :, 4:8], ALU.max))
            link(nc.vector.tensor_tensor(h4(M[:, :, :]), h4(H[:, :, :]), w4(), ALU.mult))
            link(nc.vector.tensor_tensor(SUMS[:, :, 0:GF], SUMS[:, :, 0:GF], M[:, :, :], ALU.add))
            link(nc.vector.tensor_tensor(SUMS[:, :, GF:], SUMS[:, :, GF:], W1[:, :, :], ALU.add))
            link(nc.vector.tensor_tensor(W2[:, :, :], LAST[:, GF:].unsqueeze(1).to_broadcast([P, TILES, 8]), GT[:, :, 8:16], ALU.mult))
            link(nc.vector.tensor_tensor(W1[:, :, :], W2[:, :, 0:4], W2[:, :, 4:8], ALU.max))
            link(nc.vector.tensor_tensor(W1[:, :, :], W1[:, :, :], CN[:, :].unsqueeze(2).to_broadcast([P, TILES, 4]), ALU.mult))
            link(nc.vector.tensor_tensor(h4(M[:, :, :]), h4(LAST[:, 0:GF].unsqueeze(1).to_broadcast([P, TILES, GF])), w4(), ALU.mult))
            link(nc.vector.tensor_tensor(SUMS[:, :, 0:GF], SUMS[:, :, 0:GF], M[:, :, :], ALU.add))
            link(nc.vector.tensor_tensor(SUMS[:, :, GF:], SUMS[:, :, GF:], W1[:, :, :], ALU.add))
            link(nc.vector.tensor_scalar(RD[:, :, :], SUMS[:, :, GF:], 1e-16, None, ALU.add))
            link(nc.vector.reciprocal(RD[:, :, :], RD[:, :, :]))
            link(nc.vector.tensor_tensor(h4(AG[:, :, :]), h4(SUMS[:, :, 0:GF]), RD[:, :, :].unsqueeze(3).to_broadcast([P, TILES, 4, 4]), ALU.mult))
            bc = lambda k: vec[:, k, :].unsqueeze(1).to_broadcast([P, TILES, GF])
            link(nc.vector.tensor_tensor(AG[:, :, :], AG[:, :, :], bc(0), ALU.add))
            wide = lambda k: st[:, k, :].unsqueeze(2).to_broadcast([P, TILES, GF])
            link(nc.vector.tensor_reduce(st[:, 0, :], AG[:, :, :], AX.X, ALU.add))
            link(nc.vector.tensor_scalar(st[:, 0, :], st[:, 0, :], 1.0 / GF, None, ALU.mult))
            link(nc.vector.tensor_tensor(AG[:, :, :], AG[:, :, :], wide(0), ALU.subtract))
            link(nc.vector.tensor_tensor(M[:, :, :], AG[:, :, :], AG[:, :, :], ALU.mult))
            link(nc.vector.tensor_reduce(st[:, 1, :], M[:, :, :], AX.X, ALU.add))
            link(nc.vector.tensor_scalar(st[:, 1, :], st[:, 1, :], 1.0 / GF, EPS_T, ALU.mult, ALU.add))
            v.sem_inc(var, 1)
            v.wait_ge(root, 1)
            link(nc.vector.reciprocal(st[:, 3, :], st[:, 2, :]))
            link(nc.vector.tensor_tensor(AG[:, :, :], AG[:, :, :], wide(3), ALU.mult))
            link(nc.vector.tensor_tensor(AG[:, :, :], AG[:, :, :], bc(1), ALU.mult))
            link(nc.vector.tensor_tensor(AG[:, :, :], AG[:, :, :], bc(2), ALU.add))
            link(nc.vector.tensor_reduce(SC[:, :, :], AG[:, :, :].rearrange("p s (h e) -> p s e h", e=4), AX.X, ALU.add))
            link(nc.vector.tensor_scalar(SC[:, :, :], SC[:, :, :], 0.25, None, ALU.mult))
            v.wait_ge(made, 2)
            rank_gates(nc, link, SC[:, :, :], 4, t1[:, :], t2[:, :], None, earlier[:, :, :], KEEP[:, :, :])
            link(nc.vector.tensor_reduce(st[:, 0, :], SC[:, :, :], AX.X, ALU.max))
            link(nc.vector.tensor_tensor(SC[:, :, :], SC[:, :, :], st[:, 0, :].unsqueeze(2).to_broadcast([P, TILES, 4]), ALU.subtract))
            v.sem_inc(shifted, 1)
            v.wait_ge(exped, 1)
            link(nc.vector.tensor_tensor(SC[:, :, :], SC[:, :, :], KEEP[:, :, :], ALU.mult))
            link(nc.vector.tensor_reduce(st[:, 0, :], SC[:, :, :], AX.X, ALU.add))
            link(nc.vector.reciprocal(st[:, 1, :], st[:, 0, :]))
            link(nc.vector.tensor_tensor(G[:, :, :], SC[:, :, :], st[:, 1, :].unsqueeze(2).to_broadcast([P, TILES, 4]), ALU.mult))


def run_experts(nc, sem, tag, X2, TT, G, experts, chunks, W1, b1, W2, b2, ident, store=None):
    with ExitStack() as ctx:
        local = lambda n, s, d=F32: ctx.enter_context(nc.sbuf_tensor(f"sb_{tag}_{n}", s, d))
        pbank = lambda n: ctx.enter_context(nc.psum_tensor(f"{tag}_{n}", [P, BANK], F32))
        NCH = experts * chunks
        YB = experts * C // BANK
        w1 = local("w1", [C, NCH * P])
        w2 = local("w2", [P, NCH, C])
        bb1 = local("b1", [P, NCH])
        B2 = local("b2", [GROUP * experts, BANK])
        HT = local("ht", [P, 2, NCH, BANK])
        GC = local("gc", [P, 2, GROUP * experts])
        GTR = local("gtr", [GROUP * experts, P])
        PU = [pbank(f"pu{k}") for k in range(2)]
        NY = 4
        PY = [pbank(f"py{k}") for k in range(NY)]
        PB2, PG = pbank("pb2"), pbank("pg")
        w_in, zero, hidden, up_done = (sem(f"{tag}_{n}") for n in ("w_in", "zero", "hidden", "up_done"))
        gates_in, gates_turned, gates_out, bias_done, bias_added = (sem(f"{tag}_{n}") for n in ("gates_in", "gates_turned", "gates_out", "bias_done", "bias_added"))
        y_done, added, stored = (sem(f"{tag}_{n}") for n in ("y_done", "added", "stored"))
        term = sem(f"{tag}_term")
        block = ctx.enter_context(nc.Block())
        n_w = 3 + GROUP

        @block.sync
        def _(sp):
            sp.dma_start(w1[:, :].rearrange("c (e h) -> c e h", e=experts), W1.rearrange("e c h -> c e h")).then_inc(w_in, 16)
            sp.dma_start(w2[:, :, :], W2.rearrange("e (k p) c -> p (e k) c", p=P)).then_inc(w_in, 16)
            sp.dma_start(bb1[:, :], b1.rearrange("e (k p) -> p (e k)", p=P), allow_slow_non_contiguous=True).then_inc(w_in, 16)
            sp.wait_ge(zero, 1)
            for k in range(GROUP):
                sp.dma_start(B2[k * experts:(k + 1) * experts, k * C:(k + 1) * C], b2).then_inc(w_in, 16)
            sp.wait_ge(w_in, 16 * n_w)
            if store is not None:
                sent = 0
                for part in range(4):
                    sp.wait_ge(added, (part + 1) * GROUPS // 4 + AHEAD)
                    sent += store(sp, part, stored)
                sp.wait_ge(stored, 16 * sent)

        @block.gpsimd
        def _(pool):
            pool.memset(B2[:, :], 0.0).then_inc(zero, 1)

        @block.scalar
        def _(act):
            act.wait_ge(w_in, 16 * n_w)

            def hide(g, u):
                act.wait_ge(bias_done, g + 1)
                for c in range(NCH):
                    act.wait_ge(up_done, g * NCH + c + 1)
                    nc.scalar.activation(HT[:, u, c, :], PU[c % 2][:, :], ACT.Gelu, bias=bb1[:, c:c + 1])\
                        .then_inc(hidden, 1)
            with act.Fori(0, GROUPS // 2) as i:
                for u in range(2):
                    hide(i * 2 + u, u)

        @block.tensor
        def _(pe):
            pe.wait_ge(w_in, 16 * n_w)

            def up(g, c):
                pe.wait_ge(hidden, g * NCH + c + 1)
                nc.tensor.matmul(PU[c % 2][:, :], w1[:, c * P:(c + 1) * P], TT[:, ds(g * BANK, BANK)], start=True, stop=True)\
                    .then_inc(up_done, 1)

            def down(g, u, k):
                for b in range(YB):
                    n = (g * GROUP + k) * YB + b
                    pe.wait_ge(term, 4 * n + 4)
                    bank = PY[(k * YB + b) % NY]
                    for e in range(b * 4, b * 4 + 4):
                        for c in range(chunks):
                            last = nc.tensor.matmul(bank[:, (e % 4) * C:(e % 4 + 1) * C],
                                                    HT[:, u, e * chunks + c, k * P:(k + 1) * P], w2[:, e * chunks + c, :],
                                                    start=(c == 0), stop=(c == chunks - 1))
                    last.then_inc(y_done, 1)

            def biases(g, u):
                pe.wait_ge(gates_in, g + 1)
                nc.tensor.transpose(PG[0:GROUP * experts, 0:P], GC[:, u, :], ident[:, :]).then_inc(gates_turned, 1)
                pe.wait_ge(gates_out, g + 1)
                pe.wait_ge(added, g + AHEAD)
                nc.tensor.matmul(PB2[:, :], GTR[:, :], B2[:, :], start=True, stop=True).then_inc(bias_done, 1)

            pe.sem_inc(hidden, 2)
            pe.sem_inc(bias_done, 2)
            pe.sem_inc(term, 4 * NY)
            for c in range(NCH):
                up(0, c)

            def turn(g, u, more):
                pe.wait_ge(hidden, (g + 1) * NCH + 2)
                for c in range(NCH):
                    if more:
                        up(g + 1, c)
                    if c % 2 == 1:
                        if c // 2 < GROUP:
                            down(g, u, c // 2)
                biases(g, u)

            with pe.Fori(0, GROUPS // 2 - 1) as i:
                for u in range(2):
                    turn(i * 2 + u, u, True)
            turn(GROUPS - 2, 0, True)
            turn(GROUPS - 1, 1, False)

        @block.vector
        def _(v):
            v.wait_ge(w_in, 16 * n_w)
            v.sem_inc(gates_turned, AHEAD)
            v.sem_inc(added, AHEAD)

            def group(g, u):
                v.wait_ge(gates_turned, g + AHEAD)
                nc.vector.tensor_copy(GC[:, u, :].rearrange("p (t e) -> p t e", e=experts),
                                      G[:, ds(g * GROUP, GROUP), :]).then_inc(gates_in, 1)
                v.wait_ge(gates_in, g + 1)
                for k in range(GROUP):
                    xs = X2[:, ds((g * GROUP + k) * C, C)]
                    for e in range(experts):
                        n = (g * GROUP + k) * experts + e
                        b = e // 4
                        if e % 4 == 0:
                            v.wait_ge(y_done, (g * GROUP + k) * YB + b + 1)
                        v.wait_ge(term, n + 4 * NY)
                        last = nc.vector.scalar_tensor_tensor(
                            out=xs, in0=PY[(k * YB + b) % NY][:, (e % 4) * C:(e % 4 + 1) * C],
                            scalar=GC[:, u, k * experts + e:k * experts + e + 1], in1=xs, op0=ALU.mult, op1=ALU.add)
                        last.then_inc(term, 1)
                v.wait_ge(gates_turned, g + 1 + AHEAD)
                nc.vector.tensor_copy(GTR[:, :], PG[0:GROUP * experts, 0:P]).then_inc(gates_out, 1)
                v.wait_ge(bias_done, g + 3)
                v.wait_ge(term, (g + 1) * GROUP * experts + 4 * NY)
                xg = X2[:, ds(g * BANK, BANK)]
                nc.vector.tensor_tensor(xg, PB2[:, :], xg, ALU.add).then_inc(added, 1)

            with v.Fori(0, GROUPS // 2) as i:
                for u in range(2):
                    group(i * 2 + u, u)


def mix_weights(nc, sem, A, X, XN, XN_D, X_D, ident, mean, rstd, WT, U, CB):
    with ExitStack() as ctx:
        local = lambda n, s, d=F32: ctx.enter_context(nc.sbuf_tensor("sb_mw_" + n, s, d))
        pbank = lambda n: ctx.enter_context(nc.psum_tensor("mw_" + n, [P, BANK], F32))
        bn, tmp = local("bn", [P, TILES * 6]), local("tmp", [P, 2, TILES])
        unit = local("unit", [P, 1])
        ROW_M = local("row_m", [1, TOKENS])
        XM, XMT = local("xm", [F, C]), local("xmt", [C, F])
        WQK, BQK = local("wqk", [C, LH, C, 2]), local("bqk", [C, LH, 2])
        WV, WVT = local("wv", [C, LH * C]), local("wvt", [C, LH * C])
        WP = local("wp", [P, LH, C])
        BV, BP = local("bv", [P, LH]), local("bp", [P, 1])
        QK = local("qk", [C, LH, 2, F])
        SCO = local("sco", [F, LH, F])
        sm = local("sm", [F, 2, LH])
        pm = [pbank(f"pm{k}") for k in range(2)]
        px, pq, pv = pbank("px"), pbank("pq"), pbank("pv")
        w_in, chain, var, root, normed = (sem("mw_" + n) for n in ("in", "chain", "var", "root", "normed"))
        x_stored, n_stored, unit_set = sem("x_stored"), sem("n_stored"), sem("unit_set")
        m_done, m_out, rows_in, xm_turned, xmt_out = (sem("mw_" + n) for n in ("m_done", "m_out", "rows_in", "xm_turned", "xmt_out"))
        qk_done, qk_out, sc_done, shifted, exped, prob, wt_done = (sem("mw_" + n) for n in ("qk_done", "qk_out", "sc_done", "shifted", "exped", "prob", "wt_done"))
        wvt_done, wvt_out, u_done = (sem("mw_" + n) for n in ("wvt_done", "wvt_out", "u_done"))
        x_back = sem("x_back")
        block = ctx.enter_context(nc.Block())
        X2 = X[:, :, :].rearrange("p s c -> p (s c)")
        NORM = 4
        part = F // NORM

        @block.sync
        def _(sp):
            sp.dma_start(X_D.rearrange("f t c -> t f c"), X[:, :, :]).then_inc(x_stored, 16)
            sp.wait_ge(x_stored, 16)
            for k in range(NORM):
                sp.wait_ge(normed, (k + 1) * part // 4)
                sp.dma_start(XN_D[k * part:(k + 1) * part].rearrange("f t c -> t f c"),
                             XN[:, k * part * C:(k + 1) * part * C].rearrange("p (f c) -> p f c", c=C)).then_inc(n_stored, 16)
            for a in range(2):
                sp.dma_start(X[a * F:(a + 1) * F, :, :],
                             X_D.rearrange("f (j a) c -> a f j c", a=2)[a]).then_inc(x_back, 16)
            sp.wait_ge(m_out, F // GROUP)
            sp.dma_start(XM[:, :], ROW_M[0, :].rearrange("(f c) -> f c", c=C).unsqueeze(0) if False else ROW_M[0:1, :]).then_inc(rows_in, 16)
            sp.wait_ge(n_stored, 16 * NORM)
            sp.wait_ge(x_back, 32)
            sp.wait_ge(rows_in, 16)

        @block.scalar
        def _(act):
            for dst, src in ((WQK[:, :, :, :].rearrange("c h d k -> c (h d k)"), A["Wqk"]),
                             (BQK[:, :, :], A["bqk"].rearrange("(h d k) -> d h k", h=LH, k=2)),
                             (WV[:, :], A["Wv"]), (WP[:, :, :], A["Wproj"].rearrange("(h d) c -> d h c", h=LH)),
                             (BV[:, :], A["bv"].rearrange("(h d) -> d h", h=LH)), (BP[:, :], A["bproj"].unsqueeze(1))):
                act.dma_start(dst, src, allow_slow_non_contiguous=True).then_inc(w_in, 16)
            act.wait_ge(var, 1)
            nc.scalar.activation(tmp[:, 0, :], tmp[:, 1, :], ACT.Sqrt).then_inc(root, 1)
            for g in range(F // GROUP):
                act.wait_ge(m_done, g + 1)
                nc.scalar.activation(ROW_M[:, g * BANK:(g + 1) * BANK], pm[g % 2][0:1, :], ACT.Copy).then_inc(m_out, 1)
            act.wait_ge(shifted, 1)
            nc.scalar.activation(SCO[:, :, :], SCO[:, :, :], ACT.Exp).then_inc(exped, 1)
            act.wait_ge(w_in, 96)

        @block.vector
        def _(v):
            link = Chain(v, chain)
            nc.vector.memset(unit[:, :], 1.0 / T).then_inc(unit_set, 1)
            v.wait_ge(w_in, 96)
            layer_statistics(nc, v, link, X2, bn, mean, rstd, tmp[:, 0, :])
            link(nc.vector.tensor_scalar(tmp[:, 1, :], rstd, EPS_C, None, ALU.add))
            v.sem_inc(var, 1)
            v.wait_ge(root, 1)
            link(nc.vector.reciprocal(rstd, tmp[:, 0, :]))
            with v.Fori(0, GROUPS) as g:
                for k in range(GROUP):
                    t = g * GROUP + k
                    last = nc.vector.tensor_scalar(XN[:, ds(t * C, C)], X2[:, ds(t * C, C)],
                                                   mean[:, ds(t, 1)], rstd[:, ds(t, 1)], ALU.subtract, ALU.mult)
                last.then_inc(normed, 1)
            v.wait_ge(wvt_done, 1)
            nc.vector.tensor_copy(WVT[:, :], pv[:, :]).then_inc(wvt_out, 1)
            v.wait_ge(u_done, 1)
            link(nc.vector.tensor_copy(U[:, :, :].rearrange("p h c -> p (h c)"), pq[:, :]))
            link(nc.vector.tensor_tensor(CB[:, :], px[:, 0:1], BP[:, :], ALU.add))
            v.sem_inc(wvt_out, 1)
            v.wait_ge(xm_turned, 1)
            nc.vector.tensor_copy(XMT[:, :], pv[:, 0:F]).then_inc(xmt_out, 1)
            v.wait_ge(qk_done, 1)
            for h in range(LH):
                for k in range(2):
                    last = nc.vector.tensor_scalar(QK[:, h, k, :], pq[:, (h * 2 + k) * F:(h * 2 + k + 1) * F],
                                                   BQK[:, h, k:k + 1], 1.0 / math.sqrt(C), ALU.add, ALU.mult)
            last.then_inc(qk_out, 1)
            v.wait_ge(sc_done, 1)
            s3 = px[0:F, 0:LH * F].rearrange("p (h g) -> p h g", g=F)
            wide = lambda k: sm[:, k, :].unsqueeze(2).to_broadcast([F, LH, F])
            link(nc.vector.tensor_reduce(sm[:, 0, :], s3, AX.X, ALU.max))
            link(nc.vector.tensor_tensor(SCO[:, :, :], s3, wide(0), ALU.subtract))
            v.sem_inc(shifted, 1)
            v.wait_ge(exped, 1)
            link(nc.vector.tensor_reduce(sm[:, 0, :], SCO[:, :, :], AX.X, ALU.add))
            link(nc.vector.reciprocal(sm[:, 1, :], sm[:, 0, :]))
            nc.vector.tensor_tensor(SCO[:, :, :], SCO[:, :, :], wide(1), ALU.mult).then_inc(prob, 1)
            v.wait_ge(wt_done, 1)
            link(nc.vector.tensor_copy(WT[:, :], pv[0:F, 0:LH * F]))

        @block.tensor
        def _(pe):
            pe.wait_ge(unit_set, 1)
            pe.wait_ge(w_in, 96)
            for h in range(LH):
                last = nc.tensor.transpose(pv[:, h * C:(h + 1) * C], WV[:, h * C:(h + 1) * C], ident[:, :])
            last.then_inc(wvt_done, 1)
            pe.wait_ge(wvt_out, 1)
            for h in range(LH):
                nc.tensor.matmul(pq[:, h * C:(h + 1) * C], WVT[:, h * C:(h + 1) * C], WP[:, h, :], start=True, stop=True)
            for h in range(LH):
                last = nc.tensor.matmul(px[:, 0:1], WP[:, h, :], BV[:, h:h + 1], start=(h == 0), stop=(h == LH - 1))
            last.then_inc(u_done, 1)
            for g in range(F // GROUP):
                pe.wait_ge(normed, g + 1)
                if g >= 2:
                    pe.wait_ge(m_out, g - 1)
                nc.tensor.matmul(pm[g % 2][0:1, :], unit[:, :], XN[:, g * BANK:(g + 1) * BANK], start=True, stop=True).then_inc(m_done, 1)
            pe.wait_ge(rows_in, 16)
            pe.wait_ge(wvt_out, 2)
            nc.tensor.transpose(pv[:, 0:F], XM[:, :], ident[0:F, 0:F]).then_inc(xm_turned, 1)
            pe.wait_ge(xmt_out, 1)
            for h in range(LH):
                for k in range(2):
                    last = nc.tensor.matmul(pq[:, (h * 2 + k) * F:(h * 2 + k + 1) * F], WQK[:, h, :, k], XMT[:, :], start=True, stop=True)
            last.then_inc(qk_done, 1)
            pe.wait_ge(qk_out, 1)
            for h in range(LH):
                last = nc.tensor.matmul(px[0:F, h * F:(h + 1) * F], QK[:, h, 0, :], QK[:, h, 1, :], start=True, stop=True)
            last.then_inc(sc_done, 1)
            pe.wait_ge(prob, 1)
            for h in range(LH):
                last = nc.tensor.transpose(pv[0:F, h * F:(h + 1) * F], SCO[:, h, :], ident[0:F, 0:F])
            last.then_inc(wt_done, 1)


def mix_rows(nc, sem, X, XN_D, ident, WT, U, CB):
    TG = 8
    N = T // TG
    with ExitStack() as ctx:
        local = lambda n, s, d=F32: ctx.enter_context(nc.sbuf_tensor("sb_mr_" + n, s, d))
        pbank = lambda n: ctx.enter_context(nc.psum_tensor("mr_" + n, [P, BANK], F32))
        XG = local("xg", [F, 2, TG, C])
        ZT = local("zt", [C, 2, LH, TG * F])
        YT = local("yt", [C, 2, TG * F])
        pz = [pbank(f"pz{k}") for k in range(4)]
        py, pt = [pbank(f"py{k}") for k in range(2)], [pbank(f"pt{k}") for k in range(2)]
        loaded = [sem(f"mr_loaded{u}") for u in range(2)]
        z_done, za_out, zv_out, y_done, y_out, t_done, added = (sem("mr_" + n) for n in ("z", "za_out", "zv_out", "y", "y_out", "t", "added"))
        block = ctx.enter_context(nc.Block())
        X2 = X[:, :, :].rearrange("p s c -> p (s c)")
        XF = XN_D.rearrange("f t c -> f (t c)")

        @block.sync
        def _(sp):
            with sp.Fori(0, N // 2) as i:
                for u in range(2):
                    g = i * 2 + u
                    sp.wait_ge(z_done, i * 2 + AHEAD)
                    sp.dma_start(XG[:, u, :, :].rearrange("f t c -> f (t c)"), XF[:, ds(g * TG * C, TG * C)]).then_inc(loaded[u], 16)

        def z_copy(copy, g, u, b):
            return copy(ZT[:, u, :, b * 2 * F:(b + 1) * 2 * F].rearrange("p h (t f) -> p t h f", f=F),
                        pz[b][:, :].rearrange("p (t h f) -> p t h f", t=2, f=F))

        @block.scalar
        def _(act):
            with act.Fori(0, N // 2) as i:
                for u in range(2):
                    g = i * 2 + u
                    act.wait_ge(z_done, g + 1 + AHEAD)
                    act.wait_ge(y_done, i * 2 + AHEAD)
                    for b in (0, 2):
                        last = z_copy(lambda o, x: nc.scalar.activation(o, x, ACT.Copy), g, u, b)
                    last.then_inc(za_out, 1)
                    act.wait_ge(y_done, g + 1 + AHEAD)
                    act.wait_ge(t_done, i * 2 + AHEAD)
                    nc.scalar.activation(YT[:, u, :], py[u][:, :], ACT.Identity, bias=CB[:, :]).then_inc(y_out, 1)

        @block.vector
        def _(v):
            with v.Fori(0, N // 2) as i:
                for u in range(2):
                    g = i * 2 + u
                    v.wait_ge(z_done, g + 1 + AHEAD)
                    v.wait_ge(y_done, i * 2 + AHEAD)
                    for b in (1, 3):
                        last = z_copy(nc.vector.tensor_copy, g, u, b)
                    last.then_inc(zv_out, 1)
                    v.wait_ge(t_done, g + 1 + AHEAD)
                    xg = X2[:, ds(g * BANK, BANK)]
                    nc.vector.tensor_tensor(xg, pt[u][:, :], xg, ALU.add).then_inc(added, 1)

        @block.tensor
        def _(pe):
            def mix(g, u, i):
                pe.wait_ge(loaded[u], (i + 1) * 16)
                after(pe, za_out, g)
                after(pe, zv_out, g)
                for t in range(TG):
                    last = nc.tensor.matmul(pz[t // 2][:, (t % 2) * LH * F:(t % 2 + 1) * LH * F], XG[:, u, t, :], WT[:, :],
                                            start=True, stop=True)
                last.then_inc(z_done, 1)

            def project(g, u):
                pe.wait_ge(za_out, g + 1)
                pe.wait_ge(zv_out, g + 1)
                for h in range(LH):
                    last = nc.tensor.matmul(py[u][:, :], U[:, h, :], ZT[:, u, h, :], start=(h == 0), stop=(h == LH - 1))
                last.then_inc(y_done, 1)

            def turn(g, u):
                pe.wait_ge(y_out, g + 1)
                pe.wait_ge(added, g + AHEAD)
                for k in range(GROUP):
                    last = nc.tensor.transpose(pt[u][:, k * P:(k + 1) * P], YT[:, u, k * P:(k + 1) * P], ident[:, :])
                last.then_inc(t_done, 1)

            pe.sem_inc(z_done, AHEAD)
            pe.sem_inc(y_done, AHEAD)
            pe.sem_inc(t_done, AHEAD)
            pe.sem_inc(added, AHEAD)
            mix(0, 0, 0)
            with pe.Fori(0, N // 2 - 1) as i:
                mix(i * 2 + 1, 1, i)
                project(i * 2, 0)
                turn(i * 2, 0)
                mix(i * 2 + 2, 0, i + 1)
                project(i * 2 + 1, 1)
                turn(i * 2 + 1, 1)
            mix(N - 1, 1, N // 2 - 1)
            project(N - 2, 0)
            turn(N - 2, 0)
            project(N - 1, 1)
            turn(N - 1, 1)


def route_gates(nc, sem, X, LG, mean, rstd, G):
    E = EXPERTS1
    with ExitStack() as ctx:
        local = lambda n, s, d=F32: ctx.enter_context(nc.sbuf_tensor("sb_rg_" + n, s, d))
        t1, t2 = local("t1", [P, TILES * E * E]), local("t2", [P, TILES * E * E])
        earlier = local("earlier", [P, E, E])
        KEEP, st, scale, shift = local("keep", [P, TILES, E]), local("st", [P, 2, TILES]), local("scale", [P, TILES]), local("shift", [P, TILES])
        made, chain, shifted, exped = (sem("rg_" + n) for n in ("made", "chain", "shifted", "exped"))
        block = ctx.enter_context(nc.Block())
        X2 = X[:, :, :].rearrange("p s c -> p (s c)")

        @block.gpsimd
        def _(pool):
            earlier_mask(nc, pool, earlier[:, :, :], E, made)

        @block.scalar
        def _(act):
            act.wait_ge(shifted, 1)
            nc.scalar.activation(LG[:, :, :], LG[:, :, :], ACT.Exp).then_inc(exped, 1)

        @block.vector
        def _(v):
            link = Chain(v, chain)
            wide = lambda k: st[:, k, :].unsqueeze(2).to_broadcast([P, TILES, E])
            link(nc.vector.tensor_reduce(st[:, 0, :], LG[:, :, :], AX.X, ALU.max))
            link(nc.vector.tensor_tensor(LG[:, :, :], LG[:, :, :], wide(0), ALU.subtract))
            v.sem_inc(shifted, 1)
            link(nc.vector.tensor_scalar(scale[:, :], rstd, 1.0, None, ALU.add))
            link(nc.vector.tensor_tensor(shift[:, :], mean, rstd, ALU.mult))
            with v.Fori(0, TILES // 8) as i:
                for k in range(8):
                    t = i * 8 + k
                    xs = X2[:, ds(t * C, C)]
                    nc.vector.tensor_scalar(xs, xs, scale[:, ds(t, 1)], shift[:, ds(t, 1)], ALU.mult, ALU.subtract)
            v.wait_ge(exped, 1)
            link(nc.vector.tensor_reduce(st[:, 0, :], LG[:, :, :], AX.X, ALU.add))
            link(nc.vector.reciprocal(st[:, 1, :], st[:, 0, :]))
            link(nc.vector.tensor_tensor(LG[:, :, :], LG[:, :, :], wide(1), ALU.mult))
            v.wait_ge(made, 2)
            rank_gates(nc, link, LG[:, :, :], E, t1[:, :], t2[:, :], None, earlier[:, :, :], KEEP[:, :, :])
            link(nc.vector.tensor_tensor(LG[:, :, :], LG[:, :, :], KEEP[:, :, :], ALU.mult))
            link(nc.vector.tensor_reduce(st[:, 0, :], LG[:, :, :], AX.X, ALU.add))
            link(nc.vector.tensor_scalar(st[:, 0, :], st[:, 0, :], 1e-12, None, ALU.max))
            link(nc.vector.reciprocal(st[:, 1, :], st[:, 0, :]))
            link(nc.vector.tensor_tensor(G[:, :, :], LG[:, :, :], wide(1), ALU.mult))


def metaformer(nc, A, out):
    with ExitStack() as ctx:
        sem = lambda n: nc.alloc_semaphore(n)
        sb = lambda n, s, d=F32: ctx.enter_context(nc.sbuf_tensor("sb_" + n, s, d))
        part = lambda prefix: {n[len(prefix):]: a for n, a in A.items() if n.startswith(prefix)}
        c0, f0, c1, f1 = (part(p) for p in ("L0_conv_", "L0_ffn_", "L1_conv_", "L1_ffn_"))
        c0["x"] = A["x"]
        X = sb("X", [P, TILES, C])
        ident = sb("ident", [P, P])
        st = sb("st", [P, 2, TILES])
        mean, rstd = st[:, 0, :], st[:, 1, :]
        X2 = X[:, :, :].rearrange("p s c -> p (s c)")
        SRC_T = nc.dram_tensor("source_rows", [TOKENS, ROW], F32).ap()
        DST_T = nc.dram_tensor("target_rows", [TOKENS, 2 * GHEADS], F32).ap()
        XN_D = nc.dram_tensor("normed_rows", [F, T, C], F32).ap()
        X_D = nc.dram_tensor("x_rows", [F, T, C], F32).ap()
        CN = sb("CN", [P, TILES])
        PB = sb("PB", [P, HEADS, T])
        TRIPS = sb("TRIPS", [P, 3], I32)
        TT = sb("TT", [P, TOKENS])
        G0, LAST, SUMS, Wg = sb("G0", [P, TILES, EXPERTS0]), sb("LAST", [P, ROW]), sb("SUMS", [P, TILES, PART]), sb("Wg", [C, GF])
        H, GT = sb("H", [P, TILES, GF]), sb("GT", [P, TILES, GF])
        WT, U, CB = sb("WT", [F, LH * F]), sb("U", [C, LH, C]), sb("CB", [C, 1])
        Wr, LG, G1 = sb("Wr", [C, EXPERTS1]), sb("LG", [P, TILES, EXPERTS1]), sb("G1", [P, TILES, EXPERTS1])
        with ExitStack() as c_keys:
            KG, KC = (c_keys.enter_context(nc.sbuf_tensor(n, [P, KCOLS], F32)) for n in ("sb_KG", "sb_KC"))
            with nc.cleanup_on_exit():
                loads = z_in, x_in, m_in = sem("z_in"), sem("x_in"), sem("mask_in")
                MB = TT[:, :]
                with nc.sbuf_tensor("sb_z", [P, T * CZ], F32) as z:
                    def prefetch(sp):
                        sp.dma_start(z[:, :], c0["z"][0].rearrange("q k c -> q (k c)")).then_inc(z_in, 16)
                        sp.dma_start(X[:, :, :], c0["x"][0].rearrange("s r c -> r s c")).then_inc(x_in, 16)
                        sp.dma_start(MB, c0["mask"][0].rearrange("s k -> (s k)").partition_broadcast(P)).then_inc(m_in, 16)

                    compact_edges(nc, sem, f0, KG, KC, TRIPS, prefetch)
                    pair_bias(nc, sem, c0, X, z, PB, MB, loads, ident, mean, rstd)
                row_attention(nc, sem, c0, X, PB, MB, ident, mean, rstd)
            with ExitStack() as c:
                turn_tokens(nc, sem, "t0", c, X2, ident, mean, rstd, TT, Wg[:, :], GF, H, EPS_T, f0["W_gat"])
            graph_tables(nc, sem, f0, H, GT, SRC_T, DST_T, LAST)
            graph_edges(nc, sem, KG, KC, SRC_T, DST_T, TRIPS, SUMS, CN)
        graph_gates(nc, sem, f0, H, GT, LAST, SUMS, CN, G0)
        run_experts(nc, sem, "x0", X2, TT, G0, EXPERTS0, HID0 // P, f0["W1"], f0["b1"], f0["W2"], f0["b2"], ident)
        mix_weights(nc, sem, c1, X, TT, XN_D, X_D, ident, mean, rstd, WT, U, CB)
        mix_rows(nc, sem, X, XN_D, ident, WT, U, CB)
        with ExitStack() as c:
            turn_tokens(nc, sem, "t1", c, X2, ident, mean, rstd, TT, Wr[:, :], EXPERTS1, LG, EPS_T,
                        f1["router_w"].rearrange("e c -> c e"))
        route_gates(nc, sem, X, LG, mean, rstd, G1)
        out_v = out[0].rearrange("f (j a) c -> a f j c", a=2)
        quarter = TILES // 4

        def store(sp, k, stored):
            for a in range(2):
                sp.dma_start(out_v[a, :, k * quarter:(k + 1) * quarter, :],
                             X[a * F:(a + 1) * F, k * quarter:(k + 1) * quarter, :]).then_inc(stored, 16)
            return 2
        run_experts(nc, sem, "x1", X2, TT, G1, EXPERTS1, 1, f1["w1"], f1["b1"], f1["w2"], f1["b2"], ident, store)


def kernel(**inputs):
    import numpy as _np
    import concourse.bacc as _bacc
    from concourse import mybir as _mybir
    from concourse.bass_utils import run_bass_kernel_spmd as _run

    nc = _bacc.Bacc("TRN2", target_bir_lowering=False, num_devices=1)
    arrays, A = {}, {}
    for name, a in inputs.items():
        a = _np.ascontiguousarray(a)
        arrays[f"in_{name}"] = a
        A[name] = nc.dram_tensor(f"in_{name}", a.shape, _mybir.dt.from_np(a.dtype), kind="ExternalInput").ap()
    out = nc.dram_tensor("out", (1, F, T, C), F32, kind="ExternalOutput").ap()
    metaformer(nc, A, out)
    r = _run(nc, [arrays], core_ids=[0])
    return r.results[0]["out"]
```

```python
import math
from contextlib import ExitStack

import concourse.bass as bass
from concourse import mybir

F32 = mybir.dt.float32
BF16 = mybir.dt.bfloat16
I32 = mybir.dt.int32
ALU = mybir.AluOpType
ACT = mybir.ActivationFunctionType
AX = mybir.AxisListType
ds = bass.ds

P = 128
F, T, C = 64, 128, 128
TOKENS = F * T
TILES = TOKENS // P
HEADS, DH = 8, 32
HD = HEADS * DH
CZ = 64
INF = 1e9
EPS_C, EPS_T = 1e-6, 1e-5
AHEAD = 1
BANK = 512
GROUP = BANK // P
GROUPS = TILES // GROUP

GHEADS, EXPERTS0 = 4, 4
GF = GHEADS * EXPERTS0
EDGES = 524288
ECOLS = EDGES // P
NODE_BITS = 13
LO_BITS = 7
SLOT = 8
PAIR = 2 * SLOT
BLOCKS = 16
BCOLS = ECOLS // BLOCKS
TAKE = BLOCKS * SLOT
SEARCHES = 5
FOUND = SEARCHES * TAKE
HALF = 5 * SLOT
ROUNDS = -(-BCOLS // SLOT // SEARCHES)
STRIDE = FOUND // PAIR
GCOLS = ROUNDS * FOUND + TAKE + P
KCOLS = GCOLS + FOUND + HALF
PART = 20
ROW = GF + 2 * GHEADS
HID0 = 256
EXPERTS1 = 8
LH = 4

VALID = 1 << 30
NEAR = 1 << 26


class Chain:

    def __init__(self, engine, semaphore):
        self.engine, self.semaphore, self.steps = engine, semaphore, 0

    def __call__(self, instruction):
        self.steps += 1
        instruction.then_inc(self.semaphore, 1)
        self.engine.wait_ge(self.semaphore, self.steps)


def identity(nc, pool, tile, made, first):
    pool.memset(tile, 0.0).then_inc(made, 1)
    pool.wait_ge(made, first + 1)
    pool.affine_select(out=tile, in_=tile, compare_op=ALU.not_equal, fill=1.0, base=0,
                       pattern=[[-1, P]], channel_multiplier=1).then_inc(made, 1)


def layer_statistics(nc, v, link, bn, mean, spread, tmp):
    link(nc.vector.tensor_tensor(mean, bn[:, :, 1], bn[:, :, 4], ALU.add))
    link(nc.vector.tensor_scalar(mean, mean, 0.5, None, ALU.mult))
    link(nc.vector.tensor_tensor(spread, bn[:, :, 1], bn[:, :, 4], ALU.subtract))
    link(nc.vector.scalar_tensor_tensor(out=spread, in0=spread, scalar=0.25, in1=spread,
                                        op0=ALU.mult, op1=ALU.mult))
    link(nc.vector.tensor_tensor(tmp, bn[:, :, 2], bn[:, :, 5], ALU.add))
    link(nc.vector.scalar_tensor_tensor(out=spread, in0=tmp, scalar=1.0 / C, in1=spread,
                                        op0=ALU.mult, op1=ALU.add))


def tile_statistics(nc, BN, X2, tile):
    return nc.vector.bn_stats(BN[:, :, :].rearrange("p t k -> p (t k)")[:, ds(tile * 6, 6)], X2[:, ds(tile * C, C)])


def pair_bias(nc, sem, X, BN, zs, pz, pbc, PB, x_in, mean, rstd):
    with ExitStack() as ctx:
        tmp = ctx.enter_context(nc.sbuf_tensor("sb_stat_tmp", [P, 2, TILES], F32))
        z_var, z_root, chain = sem("z_variance"), sem("z_root"), sem("pair_chain")
        x_root, x_var = sem("x_root"), sem("x_variance")
        block = ctx.enter_context(nc.Block())
        X2 = X[:, :, :].rearrange("p s c -> p (s c)")

        @block.scalar
        def _(act):
            act.wait_ge(z_var, 1)
            nc.scalar.activation(zs[:, 2, :], zs[:, 1, :], ACT.Sqrt).then_inc(z_root, 1)
            for k in range(2):
                act.wait_ge(x_var, k + 1)
                nc.scalar.activation(tmp[:, 0, :], tmp[:, 1, :], ACT.Sqrt).then_inc(x_root, 1)

        @block.vector
        def _(v):
            link = Chain(v, chain)
            nc.vector.tensor_scalar(zs[:, 1, :], zs[:, 1, :], EPS_T, None, ALU.add).then_inc(z_var, 1)
            v.wait_ge(x_in, 16)
            with v.Fori(0, TILES // 16 - 1) as i:
                for k in range(16):
                    tile_statistics(nc, BN, X2, i * 16 + k)
            for t in range(TILES - 16, TILES):
                last = tile_statistics(nc, BN, X2, t)
            link(last)
            layer_statistics(nc, v, link, BN, mean, rstd, tmp[:, 0, :])
            link(nc.vector.tensor_scalar(tmp[:, 1, :], rstd, EPS_C, None, ALU.add))
            v.sem_inc(x_var, 1)
            v.wait_ge(z_root, 1)
            link(nc.vector.reciprocal(zs[:, 3, :], zs[:, 2, :]))
            half = T // 2
            for n in range(2):
                bias = PB[:, :, n * half:(n + 1) * half]
                link(nc.vector.tensor_tensor(
                    bias, pz[n][:, :].rearrange("p (k h) -> p h k", h=HEADS),
                    zs[:, 3, n * half:(n + 1) * half].unsqueeze(1).to_broadcast([P, HEADS, half]), ALU.mult))
                link(nc.vector.tensor_tensor(bias, bias, pbc[:, :].unsqueeze(2).to_broadcast([P, HEADS, half]), ALU.add))
            v.wait_ge(x_root, 1)
            link(nc.vector.reciprocal(tmp[:, 0, :], tmp[:, 0, :]))
            link(nc.vector.tensor_tensor(tmp[:, 1, :], tmp[:, 0, :], tmp[:, 0, :], ALU.mult))
            link(nc.vector.tensor_tensor(tmp[:, 1, :], tmp[:, 1, :], rstd, ALU.mult))
            link(nc.vector.tensor_copy(rstd, tmp[:, 0, :]))
            link(nc.vector.tensor_scalar(tmp[:, 1, :], tmp[:, 1, :], EPS_T, None, ALU.add))
            v.sem_inc(x_var, 1)
            v.wait_ge(x_root, 2)
            link(nc.vector.reciprocal(tmp[:, 0, :], tmp[:, 0, :]))
            link(nc.vector.tensor_tensor(rstd, rstd, tmp[:, 0, :], ALU.mult))


def after(engine, semaphore, n):
    if not isinstance(n, int) or n > 0:
        engine.wait_ge(semaphore, n)


def row_attention(nc, sem, A, X, BN, PB, MB, ident, mean, rstd):
    with ExitStack() as ctx:
        local = lambda n, s, d=F32: ctx.enter_context(nc.sbuf_tensor("sb_" + n, s, d))
        bank = lambda n, s=(P, BANK): ctx.enter_context(nc.psum_tensor(n, list(s), F32))
        QUAD = P // DH
        BM = local("bias", [P, 2, HEADS, T])
        wq, wk, wv, wg = (local(n, [C, HD]) for n in ("wq", "wk", "wv", "wg"))
        wo = local("wo", [P, 2, C])
        lnw, lnb = local("lnw", [C, 1]), local("lnb", [C, 1])
        ones = local("ones", [1, P])
        bg, bo = local("bg", [P, 2]), local("bo", [1, C])
        XN = local("xn", [P, C])
        SNT = local("snT", [C, T])
        QT = local("qT", [P, 2, T])
        KT = local("kT", [P, 2, QUAD, T])
        V, TH = local("v", [T, 2, HD]), local("gateT", [P, 2, 2, T])
        LG = local("logits", [T, HEADS, T])
        PR = local("probs", [T, 2, HEADS, T])
        NM = local("neg_max", [T, HEADS])
        SM, RI = local("row_sum", [T, 2, HEADS]), local("inv_sum", [T, HEADS])
        PT = local("probsT", [T, HEADS, T])
        OG, OGT = local("heads_out", [T, HD]), local("gatedT", [P, 2, T])
        L = bank("p_logits", (P, 2, BANK))
        TA, TB = bank("p_turned_a"), bank("p_turned_b")
        QPS, PRV, TURN, O = bank("p_q"), bank("p_vg"), bank("p_xn"), bank("p_out")
        w_in, ones_set, kt_zero, bg_half = sem("att_w_in"), sem("ones_set"), sem("kt_zero"), sem("bg_half")
        bias_made = sem("bias_made")
        xn_made, xn_turned, sn_made = sem("xn_made"), sem("xn_turned"), sem("sn_made")
        qk_done, q_out, k_out = sem("qk_done"), sem("q_out"), sem("k_out")
        vg_done, v_out, th_out = sem("vg_done"), sem("v_out"), sem("th_out")
        score_done, logit_made, max_made, exp_a, exp_b = sem("score_done"), sem("logit_made"), sem("max_made"), sem("exp_a"), sem("exp_b")
        ta_done, tb_done, ta_out, tb_out = sem("ta_done"), sem("tb_done"), sem("ta_out"), sem("tb_out")
        pv_done, inv_made, og_made = sem("pv_done"), sem("inv_made"), sem("og_made")
        og_turned, ogt_made, out_done, x_added = sem("og_turned"), sem("ogt_made"), sem("out_done"), sem("x_added")
        block = ctx.enter_context(nc.Block())
        X2 = X[:, :, :].rearrange("p s c -> p (s c)")
        carried = sem("att_carried")
        N_W = 10
        real = lambda s: not isinstance(s, int) or 0 <= s < F

        def turns(engine, turn):
            for s in (-2, -1, 0, 1):
                turn(s, s % 2)
            with engine.Fori(0, (F - 4) // 4) as i:
                for u in range(4):
                    turn(i * 4 + (2 + u), u % 2)
            for s in (F - 2, F - 1, F, F + 1):
                turn(s, s % 2)

        @block.sync
        def _(sp):
            for dst, src in ((wq[:, :], A["w_q"]), (wk[:, :], A["w_k"]), (wv[:, :], A["w_v"]), (wg[:, :], A["w_g"]),
                             (wo[:, :, :], A["w_o"].rearrange("(a p) c -> p a c", a=2)),
                             (lnw[:, :], A["ln_s_w"].unsqueeze(1)), (lnb[:, :], A["ln_s_b"].unsqueeze(1)),
                             (bg[:, 0:1], A["b_g"][0:P].unsqueeze(1)), (bg[:, 1:2], A["b_g"][P:HD].unsqueeze(1)),
                             (bo[:, :], A["b_o"].unsqueeze(0))):
                sp.dma_start(dst, src).then_inc(w_in, 16)
            sp.wait_ge(w_in, 16 * N_W)

        @block.gpsimd
        def _(pool):
            pool.memset(KT[:, :, :, :], 0.0).then_inc(kt_zero, 1)

            def bias(s, u):
                nc.gpsimd.tensor_tensor(
                    BM[:, u, :, :], PB[:, :, :],
                    MB[:, ds(s * T, T)].unsqueeze(1).to_broadcast([P, HEADS, T]), ALU.add).then_inc(bias_made, 1)

            bias(0, 0)
            bias(1, 1)
            with pool.Fori(0, F // 2 - 1) as it:
                for u in range(2):
                    pool.wait_ge(logit_made, it * 2 + u + 1)
                    bias(it * 2 + u + 2, u)

        @block.vector
        def _(v):
            nc.vector.memset(ones[:, :], 1.0).then_inc(ones_set, 1)
            v.wait_ge(w_in, 16 * N_W)
            v.wait_ge(kt_zero, 1)
            nc.vector.tensor_scalar(bg[:, :], bg[:, :], 0.5, None, ALU.mult).then_inc(bg_half, 1)

            def turn(s, u):
                if real(s + 2):
                    after(v, xn_turned, s + 2)
                    nc.vector.tensor_scalar(XN[:, :], X2[:, ds((s + 2) * C, C)], mean[:, ds(s + 2, 1)], rstd[:, ds(s + 2, 1)],
                                            ALU.subtract, ALU.mult).then_inc(xn_made, 1)
                if real(s):
                    after(v, score_done, s + 1)
                    after(v, bias_made, s + 1)
                    after(v, exp_b, s)
                    nc.vector.scalar_tensor_tensor(
                        out=LG[:, :, :].rearrange("p (j r) k -> p j (r k)", j=2),
                        in0=L[:, :, :], scalar=1.0 / math.sqrt(DH),
                        in1=BM[:, u, :, :].rearrange("p (j r) k -> p j (r k)", j=2),
                        op0=ALU.mult, op1=ALU.add).then_inc(logit_made, 1)
                if real(s - 2):
                    after(v, out_done, s - 1)
                    xs = X2[:, ds((s - 2) * C, C)]
                    nc.vector.tensor_tensor(xs, O[:, 0:C], xs, ALU.add).then_inc(x_added, 1)
                if real(s):
                    after(v, logit_made, s + 1)
                    nc.vector.tensor_reduce(NM[:, :], LG[:, :, :], AX.X, ALU.max, negate=True).then_inc(max_made, 1)
                if real(s + 1):
                    after(v, qk_done, s + 2)
                    after(v, score_done, s + 1)
                    for r in range(QUAD):
                        rows = slice(r * DH, (r + 1) * DH)
                        last = nc.vector.tensor_copy(KT[rows, :, r, :], TURN[rows, T:T + HD].rearrange("p (j k) -> p j k", j=2))
                    last.then_inc(k_out, 1)
                if real(s - 2):
                    v.wait_ge(x_added, s - 1)
                    v.sem_inc(carried, 1)
                    tile_statistics(nc, BN, X2, s - 2)
                if real(s - 1):
                    after(v, exp_b, s)
                    after(v, og_made, s - 1)
                    nc.vector.reciprocal(RI[:, :], SM[:, 1 - u, :]).then_inc(inv_made, 1)
                    after(v, inv_made, s)
                    after(v, pv_done, s)
                    after(v, og_turned, s - 1)
                    nc.vector.scalar_tensor_tensor(
                        out=OG[:, :].rearrange("p (h d) -> p h d", d=DH), in0=O[:, 0:HD].rearrange("p (h d) -> p h d", d=DH),
                        scalar=0.5, in1=RI[:, :].unsqueeze(2).to_broadcast([P, HEADS, DH]),
                        op0=ALU.mult, op1=ALU.mult).then_inc(og_made, 1)
                if real(s + 2):
                    after(v, xn_turned, s + 3)
                    nc.vector.tensor_scalar(SNT[:, :], TURN[:, 0:T], lnw[:, :], lnb[:, :],
                                            ALU.mult, ALU.add).then_inc(sn_made, 1)
                if real(s - 1):
                    after(v, og_turned, s)
                    after(v, th_out, s)
                    after(v, out_done, s - 1)
                    nc.vector.scalar_tensor_tensor(out=OGT[:, :, :], in0=TH[:, 1 - u, :, :], scalar=1.0,
                                                   in1=TA[:, 0:HD].rearrange("p (a q) -> p a q", a=2),
                                                   op0=ALU.add, op1=ALU.mult).then_inc(ogt_made, 1)

            turns(v, turn)

        @block.scalar
        def _(act):
            act.wait_ge(w_in, 16 * N_W)
            act.wait_ge(kt_zero, 1)
            act.wait_ge(bg_half, 1)

            def softmax(s, u, first):
                for h in range(first, first + 4):
                    last = nc.scalar.activation(PR[:, u, h, :], LG[:, h, :], ACT.Exp, bias=NM[:, h:h + 1],
                                                accum_out=SM[:, u, h:h + 1])
                return last

            def turn(s, u):
                if real(s - 1):
                    after(act, ta_done, s)
                    after(act, pv_done, s - 1)
                    nc.scalar.activation(PT[:, 0:4, :], TA[:, :].rearrange("p (h k) -> p h k", k=T), ACT.Copy).then_inc(ta_out, 1)
                    after(act, tb_done, s)
                    nc.scalar.activation(PT[:, 4:8, :], TB[:, :].rearrange("p (h k) -> p h k", k=T), ACT.Copy).then_inc(tb_out, 1)
                if real(s):
                    after(act, max_made, s + 1)
                    after(act, tb_done, s - 1)
                    after(act, inv_made, s - 1)
                    softmax(s, u, 0).then_inc(exp_a, 1)
                if real(s + 1):
                    after(act, qk_done, s + 2)
                    after(act, score_done, s + 1)
                    nc.scalar.activation(QT[:, :, :], QPS[:, 0:HD].rearrange("p (a q) -> p a q", a=2), ACT.Copy).then_inc(q_out, 1)
                if real(s):
                    softmax(s, u, 4).then_inc(exp_b, 1)
                if real(s + 1):
                    after(act, vg_done, s + 2)
                    after(act, pv_done, s)
                    nc.scalar.activation(V[:, 1 - u, :], PRV[:, 0:HD], ACT.Copy).then_inc(v_out, 1)
                    after(act, ogt_made, s)
                    for a in range(2):
                        last = nc.scalar.activation(TH[:, 1 - u, a, :], PRV[:, HD + a * T:HD + (a + 1) * T], ACT.Tanh,
                                                    scale=0.5, bias=bg[:, a:a + 1])
                    last.then_inc(th_out, 1)

            turns(act, turn)

        @block.tensor
        def _(pe):
            pe.wait_ge(w_in, 16 * N_W)
            pe.wait_ge(ones_set, 1)

            def turn(s, u):
                if real(s):
                    after(pe, q_out, s + 1)
                    after(pe, k_out, s + 1)
                    after(pe, logit_made, s)
                    for j in range(2):
                        last = nc.tensor.matmul(L[:, j, :], QT[:, j, :], KT[:, j, :, :].rearrange("p r k -> p (r k)"),
                                                start=True, stop=True)
                    last.then_inc(score_done, 1)
                if real(s - 2):
                    after(pe, ogt_made, s - 1)
                    for a in range(2):
                        nc.tensor.matmul(O[:, 0:C], OGT[:, a, :], wo[:, a, :], start=(a == 0), stop=False)
                    nc.tensor.matmul(O[:, 0:C], ones[:, :], bo[:, :], start=False, stop=True).then_inc(out_done, 1)
                if real(s - 1):
                    after(pe, exp_a, s)
                    after(pe, ogt_made, s - 1)
                    for h in range(4):
                        last = nc.tensor.transpose(TA[:, h * T:(h + 1) * T], PR[:, 1 - u, h, :], ident[:, :])
                    last.then_inc(ta_done, 1)
                    after(pe, exp_b, s)
                    after(pe, tb_out, s - 1)
                    for h in range(4):
                        last = nc.tensor.transpose(TB[:, h * T:(h + 1) * T], PR[:, 1 - u, 4 + h, :], ident[:, :])
                    last.then_inc(tb_done, 1)
                if real(s + 1):
                    after(pe, sn_made, s + 2)
                    after(pe, q_out, s + 1)
                    after(pe, k_out, s + 1)
                    for bank_of, w, col in ((QPS, wq, 0), (TURN, wk, T)):
                        for a in range(2):
                            last = nc.tensor.matmul(bank_of[:, col + a * T:col + (a + 1) * T], w[:, a * P:(a + 1) * P],
                                                    SNT[:, :], start=True, stop=True)
                    last.then_inc(qk_done, 1)
                if real(s - 1):
                    after(pe, ta_out, s)
                    after(pe, v_out, s)
                    after(pe, x_added, s - 1)
                    after(pe, og_made, s - 1)
                    for h in range(8):
                        if h == 4:
                            after(pe, tb_out, s)
                        last = nc.tensor.matmul(O[:, h * DH:(h + 1) * DH], PT[:, h, :], V[:, 1 - u, h * DH:(h + 1) * DH],
                                                start=True, stop=True)
                    last.then_inc(pv_done, 1)
                if real(s + 1):
                    after(pe, th_out, s + 1)
                    nc.tensor.matmul(PRV[:, 0:HD], SNT[:, :], wv[:, :], start=True, stop=True)
                    for a in range(2):
                        last = nc.tensor.matmul(PRV[:, HD + a * T:HD + (a + 1) * T], wg[:, a * P:(a + 1) * P], SNT[:, :],
                                                start=True, stop=True)
                    last.then_inc(vg_done, 1)
                if real(s + 2):
                    after(pe, xn_made, s + 3)
                    after(pe, sn_made, s + 2)
                    after(pe, k_out, s + 2)
                    nc.tensor.transpose(TURN[:, 0:T], XN[:, :], ident[:, :]).then_inc(xn_turned, 1)
                if real(s - 1):
                    after(pe, og_made, s)
                    for a in range(2):
                        last = nc.tensor.transpose(TA[:, a * T:(a + 1) * T], OG[:, a * P:(a + 1) * P], ident[:, :])
                    last.then_inc(og_turned, 1)

            turns(pe, turn)


def compact_edges(nc, sem, A, pair, KG, KC, TRIPS, prefetch, z, zs, pz, pbc, MB, ident, loads):
    with ExitStack() as ctx:
        local = lambda n, s, d=F32: ctx.enter_context(nc.sbuf_tensor("sb_" + n, s, d))
        SRC = local("src", [P, ECOLS], I32)
        DST, TMP = KG[:, 0:ECOLS].bitcast(I32), KC[:, 0:ECOLS].bitcast(I32)
        NEAR_N, ALL_N, TOTAL_N = slice(0, BLOCKS), slice(BLOCKS, 2 * BLOCKS), slice(2 * BLOCKS, 2 * BLOCKS + 1)
        CNT, CNA = local("counts", [P, 2 * BLOCKS + 1]), local("counts_max", [P, 2 * BLOCKS + 1])
        TOPS = local("tops", [P, 3])
        R, NEAR_P, REST, TMP_I, GATHERED, CLAMPED, BOTH = range(7)
        N = local("trips", [P, 7], I32)
        ROUND = local("round_keys", [P, FOUND])
        NZ = 4
        SQ = local("z_squares", [P, T // NZ, CZ])
        z_in, x_in, m_in = loads
        ztr = local("z_tr", [P, 2, BANK])
        wz, wzr = local("wz", [P, 2, HEADS]), local("wzr", [P, 2])
        b_bc = local("b_bc", [CZ, P])
        ptr = [ctx.enter_context(nc.psum_tensor(f"z_ptr{k}", [P, BANK], F32)) for k in range(2)]
        pcc = ctx.enter_context(nc.psum_tensor("pcc", [P, BANK], F32))
        zw_in, id_made, wz_made, w_scaled = sem("zw_in"), sem("id_made"), sem("wz_made"), sem("wz_scaled")
        ztd, zev, zmm, const_mm = sem("z_transposed"), sem("z_evacuated"), sem("z_projected"), sem("pair_const")
        N_Z = T * CZ // (GROUP * P)
        squared, squares_used, z_chain = sem("z_squared"), sem("squares_used"), sem("z_chain")
        TAKEN, JOIN = local("taken_keys", [P, TAKE]), local("join", [P, 1])
        e_in, chain, counted, summed = sem("edges_in"), sem("edge_chain"), sem("counted"), sem("count_max")
        trips_made, zeroed, carried = sem("trips_made"), sem("zeroed"), sem("carried")
        found, picked, rest_taken = sem("found"), sem("picked"), sem("rest_taken")
        flagged, block_counts = sem("flagged"), sem("block_counts")
        block = ctx.enter_context(nc.Block())
        KEY = SRC[:, :].bitcast(F32)

        @block.sync
        def _(sp):
            sp.dma_start(SRC[:, :], A["edge_index"][0].rearrange("(p e) -> p e", p=P)).then_inc(e_in, 16)
            sp.dma_start(DST, A["edge_index"][1].rearrange("(p e) -> p e", p=P)).then_inc(e_in, 16)
            sp.wait_ge(wz_made, 1)
            for k in range(2):
                sp.dma_start(wz[k * CZ:(k + 1) * CZ, k, :], pair["w_z"]).then_inc(zw_in, 16)
                sp.dma_start(wzr[k * CZ:(k + 1) * CZ, 0:1], pair["ln_z_w"].unsqueeze(1)).then_inc(zw_in, 16)
            sp.dma_start(wzr[0:CZ, 1:2], pair["ln_z_b"].unsqueeze(1)).then_inc(zw_in, 16)
            prefetch(sp)
            sp.wait_ge(e_in, 32)

        @block.gpsimd
        def _(pool):
            pool.memset(wz[:, :, :], 0.0).then_inc(wz_made, 1)
            pool.memset(b_bc[:, :], 1.0).then_inc(wz_made, 1)
            identity(nc, pool, ident[:, :], id_made, 0)
            pool.wait_ge(counted, 1)
            pool.partition_all_reduce(CNA[:, :], CNT[:, :], P, bass.bass_isa.ReduceOp.max).then_inc(summed, 1)
            pool.memset(KG[:, :], 0.0)
            pool.memset(KC[:, :], 0.0).then_inc(zeroed, 1)
            link = Chain(pool, z_chain)
            zz = z[:, :].rearrange("p (k c) -> p k c", c=CZ)
            pool.wait_ge(z_in, 16)
            quarter = lambda n: slice(n * T // NZ, (n + 1) * T // NZ)

            def total(x, out):
                wide = CZ // 2
                while wide >= 1:
                    to = SQ[:, :, 0:wide] if wide > 1 else out.unsqueeze(2)
                    link(nc.gpsimd.tensor_tensor(to, x[:, :, 0:wide], x[:, :, wide:2 * wide], ALU.add))
                    x, wide = SQ[:, :, :], wide // 2

            for n in range(NZ):
                total(zz[:, quarter(n), :], zs[:, 0, quarter(n)])
            link(nc.gpsimd.tensor_scalar(zs[:, 0, :], zs[:, 0, :], 1.0 / CZ, None, ALU.mult))
            link(nc.gpsimd.tensor_tensor(zz, zz, zs[:, 0, :].unsqueeze(2).to_broadcast([P, T, CZ]), ALU.subtract))
            pool.sem_inc(squares_used, 1)
            for n in range(NZ):
                pool.wait_ge(squared, n + 1)
                total(SQ[:, :, :], zs[:, 1, quarter(n)])
                pool.sem_inc(squares_used, 1)
            link(nc.gpsimd.tensor_scalar(zs[:, 1, :], zs[:, 1, :], 1.0 / CZ, None, ALU.mult))
            pool.wait_ge(m_in, 16)
            nc.gpsimd.tensor_scalar(MB, MB, 1.0, INF, ALU.subtract, ALU.mult)

        @block.scalar
        def _(act):
            act.wait_ge(zw_in, 80)
            act.wait_ge(wz_made, 2)
            nc.scalar.activation(b_bc[:, :], b_bc[:, :], ACT.Copy, scale=wzr[0:CZ, 1:2]).then_inc(w_scaled, 1)
            act.wait_ge(const_mm, 1)
            nc.scalar.activation(pbc[:, :], pcc[:, 0:HEADS], ACT.Copy)
            nc.scalar.activation(wz[:, :, :], wz[:, :, :], ACT.Copy, scale=wzr[:, 0:1]).then_inc(w_scaled, 1)
            act.wait_ge(flagged, 1)
            link = Chain(act, block_counts)
            unused = SQ[:, :, :].rearrange("p k c -> p (k c)")
            for b in range(BLOCKS):
                for first, flags, sign in ((0, TMP, 1.0), (BLOCKS, DST, -1.0)):
                    link(nc.scalar.activation(unused[:, 0:BCOLS], flags[:, b * BCOLS:(b + 1) * BCOLS], ACT.Copy, scale=sign,
                                              accum_out=CNT[:, first + b:first + b + 1]))
            nc.scalar.activation(unused[:, 0:BLOCKS], CNT[:, NEAR_N], ACT.Copy, accum_out=CNT[:, TOTAL_N]).then_inc(counted, 1)
            zz = z[:, :].rearrange("p (k c) -> p k c", c=CZ)
            for n in range(NZ):
                act.wait_ge(squares_used, n + 1)
                nc.scalar.activation(SQ[:, :, :], zz[:, n * T // NZ:(n + 1) * T // NZ, :], ACT.Square).then_inc(squared, 1)
            for g in range(N_Z):
                act.wait_ge(ztd, g + 1)
                if g >= 2:
                    act.wait_ge(zmm, g - 1)
                nc.scalar.activation(ztr[:, g % 2, :], ptr[g % 2][:, :], ACT.Copy).then_inc(zev, 1)

        @block.tensor
        def _(pe):
            pe.wait_ge(w_scaled, 1)
            nc.tensor.matmul(pcc[:, 0:HEADS], b_bc[:, :], wz[0:CZ, 0, :], start=True, stop=True)\
                .then_inc(const_mm, 1)
            pe.wait_ge(id_made, 2)
            pe.wait_ge(w_scaled, 2)
            pe.wait_ge(squares_used, 1)

            def turn(g):
                if g >= 2:
                    pe.wait_ge(zev, g - 1)
                for j in range(GROUP):
                    c = (g * GROUP + j) * P
                    last = nc.tensor.transpose(ptr[g % 2][:, j * P:(j + 1) * P], z[:, c:c + P], ident[:, :])
                last.then_inc(ztd, 1)

            def project(g):
                pe.wait_ge(zev, g + 1)
                for j in range(GROUP):
                    tile = g * GROUP + j
                    bank, col = pz[tile // 32], tile % 32
                    last = nc.tensor.matmul(bank[:, col * 2 * HEADS:(col + 1) * 2 * HEADS],
                                            ztr[:, g % 2, j * P:(j + 1) * P],
                                            wz[:, :, :].rearrange("p a h -> p (a h)"), start=True, stop=True)
                last.then_inc(zmm, 1)

            turn(0)
            for g in range(1, N_Z):
                turn(g)
                project(g - 1)
            project(N_Z - 1)

        @block.vector
        def _(v):
            link = Chain(v, chain)

            def wait(semaphore, count):
                v.wait_ge(semaphore, count)
                v.sem_inc(carried, 1)

            def search(keys, out):
                for b in range(BLOCKS):
                    last = nc.vector.max(out[:, b * SLOT:(b + 1) * SLOT], keys[:, b * BCOLS:(b + 1) * BCOLS])
                yield last
                for b in range(BLOCKS):
                    blk = keys[:, b * BCOLS:(b + 1) * BCOLS]
                    last = nc.vector.match_replace(blk, out[:, b * SLOT:(b + 1) * SLOT], blk, 0.0)
                yield last

            def search_round(done):
                for k in range(SEARCHES):
                    steps = search(KEY, ROUND[:, k * TAKE:(k + 1) * TAKE])
                    for j in range(2):
                        wait(found, done + (2 * k + j + AHEAD))
                        next(steps).then_inc(found, 1)

            v.wait_ge(e_in, 32)
            link(nc.vector.tensor_scalar(TMP, SRC[:, :], TOKENS - 1, NEAR >> NODE_BITS, ALU.is_lt, ALU.mult))
            link(nc.vector.tensor_scalar(SRC[:, :], SRC[:, :], TOKENS - 1, None, ALU.min))
            link(nc.vector.scalar_tensor_tensor(out=TMP, in0=TMP, scalar=VALID >> NODE_BITS, in1=DST, op0=ALU.add, op1=ALU.add))
            link(nc.vector.tensor_scalar(TMP, TMP, NODE_BITS, None, ALU.logical_shift_left))
            link(nc.vector.tensor_scalar(DST, DST, TOKENS, -1, ALU.is_lt, ALU.mult))
            link(nc.vector.tensor_tensor(SRC[:, :], SRC[:, :], TMP, ALU.bitwise_or))
            link(nc.vector.tensor_tensor(SRC[:, :], SRC[:, :], DST, ALU.bitwise_and))
            link(nc.vector.tensor_scalar(TMP, SRC[:, :], 4, None, ALU.logical_shift_right))
            link(nc.vector.tensor_scalar(TMP, TMP, 22, 1, ALU.logical_shift_right, ALU.bitwise_and))
            v.sem_inc(flagged, 1)
            v.sem_inc(found, AHEAD)
            search_round(0)
            v.wait_ge(summed, 1)
            link(nc.vector.tensor_reduce(TOPS[:, 0:2], CNA[:, 0:2 * BLOCKS].rearrange("p (a b) -> p a b", a=2), AX.X, ALU.max))
            link(nc.vector.tensor_copy(TOPS[:, 2:3], CNA[:, TOTAL_N]))
            n = lambda k: N[:, k:k + 1]

            def step(out, x, a, op0, b=None, op1=None):
                link(nc.vector.tensor_scalar(n(out), x, a, b, op0, *((op1,) if op1 is not None else ())))
            step(TMP_I, TOPS[:, 0:1], SLOT - 1.0, ALU.add)
            step(TMP_I, n(TMP_I), 3, ALU.logical_shift_right)
            step(TMP_I, n(TMP_I), 1, ALU.max, SEARCHES - 1, ALU.add)
            step(TMP_I, n(TMP_I), 205, ALU.mult)
            step(R, n(TMP_I), 10, ALU.logical_shift_right)
            step(NEAR_P, TOPS[:, 2:3], PAIR - 1.0, ALU.add)
            step(NEAR_P, n(NEAR_P), 4, ALU.logical_shift_right)
            step(NEAR_P, n(NEAR_P), STRIDE, ALU.min, 1, ALU.max)
            step(CLAMPED, n(R), SEARCHES, ALU.mult, SEARCHES, ALU.add)
            step(REST, TOPS[:, 1:2], SLOT - 1.0, ALU.add)
            step(REST, n(REST), 3, ALU.logical_shift_right)
            link(nc.vector.tensor_tensor(n(REST), n(REST), n(CLAMPED), ALU.subtract))
            step(REST, n(REST), 1, ALU.max)
            step(TMP_I, n(R), STRIDE, ALU.mult, -STRIDE, ALU.add)
            link(nc.vector.tensor_tensor(n(GATHERED), n(TMP_I), n(NEAR_P), ALU.add))
            link(nc.vector.tensor_tensor(n(CLAMPED), n(CLAMPED), n(REST), ALU.add))
            step(CLAMPED, n(CLAMPED), TAKE // SLOT, ALU.mult, HALF // SLOT - 1, ALU.add)
            step(CLAMPED, n(CLAMPED), 205, ALU.mult)
            step(CLAMPED, n(CLAMPED), 10, ALU.logical_shift_right)
            step(BOTH, n(CLAMPED), 1, ALU.add)
            step(BOTH, n(BOTH), 1, ALU.logical_shift_right)
            step(TMP_I, n(GATHERED), -1, ALU.add)
            link(nc.vector.tensor_tensor(n(BOTH), n(BOTH), n(TMP_I), ALU.min))
            link(nc.vector.tensor_scalar(TRIPS[:, 0:1], n(BOTH), 1, None, ALU.max))
            link(nc.vector.tensor_tensor(TRIPS[:, 1:2], n(GATHERED), TRIPS[:, 0:1], ALU.subtract))
            link(nc.vector.tensor_scalar(TRIPS[:, 1:2], TRIPS[:, 1:2], 1, None, ALU.max))
            step(TMP_I, TRIPS[:, 0:1], 2, ALU.mult)
            link(nc.vector.tensor_tensor(TRIPS[:, 2:3], n(CLAMPED), n(TMP_I), ALU.subtract))
            nc.vector.tensor_scalar(TRIPS[:, 2:3], TRIPS[:, 2:3], 1, None, ALU.max).then_inc(trips_made, 1)
            v.wait_ge(trips_made, 1)
            trips = lambda k, top, least=1: v.value_load(N[0:1, k:k + 1], min_val=least, max_val=top)
            rounds, near_pairs, rest = trips(R, ROUNDS), trips(NEAR_P, STRIDE), trips(REST, BCOLS // SLOT)
            v.wait_ge(zeroed, 1)
            v.sem_inc(picked, AHEAD)
            v.sem_inc(rest_taken, AHEAD)

            picked_reg = v.alloc_register("picked_before")
            v.reg_mov(picked_reg, 0)
            with v.Fori(0, rounds) as r:
                picked_before = v.snap(picked_reg, min_val=0, max_val=ROUNDS * STRIDE * 5)
                done = r * (2 * SEARCHES + 2) + 2 * SEARCHES
                wait(found, done + AHEAD)
                with v.Fori(0, near_pairs) as i:
                    for k in range(2):
                        wait(picked, picked_before + (i * 5 + 2 * k + AHEAD))
                        nc.vector.max(TAKEN[:, k * SLOT:(k + 1) * SLOT], ROUND[:, :]).then_inc(picked, 1)
                        wait(picked, picked_before + (i * 5 + 2 * k + 1 + AHEAD))
                        nc.vector.match_replace(ROUND[:, :], TAKEN[:, k * SLOT:(k + 1) * SLOT], ROUND[:, :], 0.0).then_inc(picked, 1)
                    wait(picked, picked_before + (i * 5 + 4 + AHEAD))
                    nc.vector.tensor_copy(KG[:, ds((r * STRIDE + i) * PAIR, PAIR)], TAKEN[:, 0:PAIR]).then_inc(picked, 1)
                nc.vector.memset(JOIN[:, :], 0.0).then_inc(found, 1)
                v.reg_add(picked_reg, picked_reg, near_pairs * 5)
                wait(found, done + (1 + AHEAD))
                nc.vector.tensor_copy(KC[:, ds(r * FOUND, FOUND)], ROUND[:, :]).then_inc(found, 1)
                search_round(done + 2)
            link(nc.vector.memset(JOIN[:, :], 0.0))
            nc.vector.tensor_copy(KC[:, ds(rounds * FOUND, FOUND)], ROUND[:, :])
            with v.Fori(0, rest) as i:
                steps = search(KEY, TAKEN[:, :])
                wait(rest_taken, i * 3 + AHEAD)
                next(steps).then_inc(rest_taken, 1)
                wait(rest_taken, i * 3 + 1 + AHEAD)
                next(steps).then_inc(rest_taken, 1)
                wait(rest_taken, i * 3 + 2 + AHEAD)
                at = nc.s_assert_within(rounds * FOUND + FOUND + i * TAKE, 0, KCOLS - P - TAKE, skip_runtime_bounds_check_because=
                                        "the rest is what the rounds leave, and KC has room for all searches")
                nc.vector.tensor_copy(KC[:, ds(at, TAKE)], TAKEN[:, :]).then_inc(rest_taken, 1)
            link(nc.vector.memset(JOIN[:, :], 0.0))


def turn_tokens(nc, sem, tag, ctx, X2, BN, ident, mean, rstd, TT, W, width, OUT, eps, load_w, residual=False):
    local = lambda n, s, d=F32: ctx.enter_context(nc.sbuf_tensor(f"sb_{tag}_{n}", s, d))
    pbank = lambda n: ctx.enter_context(nc.psum_tensor(f"{tag}_{n}", [P, BANK], F32))
    AHEAD_N = 4
    XN = local("xn", [P, AHEAD_N, BANK])
    SG = local("sg", [P, 2, BANK])
    tmp = local("tmp", [P, 2, TILES])
    pt = [pbank(f"pt{k}") for k in range(2)]
    ph = [pbank(f"ph{k}") for k in range(2)]
    w_in, chain, var, root = sem(tag + "_w_in"), sem(tag + "_chain"), sem(tag + "_var"), sem(tag + "_root")
    normed, turned, staged = (sem(f"{tag}_{n}") for n in ("normed", "turned", "staged"))
    mixed, mixed_out, normed_added = sem(tag + "_mixed"), sem(tag + "_mixed_out"), sem(tag + "_normed_added")
    block = ctx.enter_context(nc.Block())

    @block.sync
    def _(sp):
        sp.dma_start(W, load_w, allow_slow_non_contiguous=True).then_inc(w_in, 16)
        sp.wait_ge(w_in, 16)

    @block.scalar
    def _(act):
        act.wait_ge(var, 1)
        nc.scalar.activation(tmp[:, 0, :], tmp[:, 1, :], ACT.Sqrt).then_inc(root, 1)
        act.sem_inc(mixed, 2)
        with act.Fori(0, GROUPS // 2) as i:
            for u in range(2):
                g = i * 2 + u
                act.wait_ge(turned, g + 1)
                act.wait_ge(mixed, g + 1)
                nc.scalar.activation(SG[:, u, :], pt[u][:, :], ACT.Copy)
                nc.scalar.activation(TT[:, ds(g * BANK, BANK)], pt[u][:, :], ACT.Copy).then_inc(staged, 1)

    @block.gpsimd
    def _(pool):
        if residual:
            with pool.Fori(0, GROUPS // AHEAD_N) as i:
                for u in range(AHEAD_N):
                    g = i * AHEAD_N + u
                    xg = X2[:, ds(g * BANK, BANK)]
                    pool.wait_ge(normed, g + 1)
                    nc.gpsimd.tensor_tensor(xg, XN[:, u, :], xg, ALU.add).then_inc(normed_added, 1)

    @block.vector
    def _(v):
        link = Chain(v, chain)
        layer_statistics(nc, v, link, BN, mean, rstd, tmp[:, 0, :])
        link(nc.vector.tensor_scalar(tmp[:, 1, :], rstd, eps, None, ALU.add))
        v.sem_inc(var, 1)
        v.wait_ge(root, 1)
        link(nc.vector.reciprocal(rstd, tmp[:, 0, :]))

        def norm(g, u):
            after(v, turned, g - AHEAD_N + 1)
            if residual:
                after(v, normed_added, g - AHEAD_N + 1)
            for k in range(GROUP):
                t = g * GROUP + k
                last = nc.vector.tensor_scalar(XN[:, u, k * P:(k + 1) * P], X2[:, ds(t * C, C)],
                                               mean[:, ds(t, 1)], rstd[:, ds(t, 1)], ALU.subtract, ALU.mult)
            last.then_inc(normed, 1)

        def out(g, u):
            v.wait_ge(mixed, g + 1 + 2)
            nc.vector.tensor_copy(OUT[:, ds(g * GROUP, GROUP), :],
                                  ph[u % 2][:, 0:GROUP * width].rearrange("p (t w) -> p t w", w=width)).then_inc(mixed_out, 1)

        for u in range(AHEAD_N):
            norm(u, u)
        with v.Fori(0, GROUPS // AHEAD_N - 1) as i:
            for u in range(AHEAD_N):
                out(i * AHEAD_N + u, u)
                norm(i * AHEAD_N + AHEAD_N + u, u)
        for u in range(AHEAD_N):
            out(GROUPS - AHEAD_N + u, u)

    @block.tensor
    def _(pe):
        pe.wait_ge(w_in, 16)

        def turn(g, u):
            pe.wait_ge(normed, g + 1)
            after(pe, staged, g - 1)
            for k in range(GROUP):
                last = nc.tensor.transpose(pt[u % 2][:, k * P:(k + 1) * P], XN[:, u, k * P:(k + 1) * P], ident[:, :])
            last.then_inc(turned, 1)

        def multiply(g, u):
            pe.wait_ge(staged, g + 1)
            pe.wait_ge(mixed_out, g + 1)
            for k in range(GROUP):
                last = nc.tensor.matmul(ph[u][:, k * width:(k + 1) * width], SG[:, u, k * P:(k + 1) * P], W,
                                        start=True, stop=True)
            last.then_inc(mixed, 1)

        pe.sem_inc(mixed_out, 2)
        for u in range(2):
            turn(u, u)
        with pe.Fori(0, GROUPS // AHEAD_N - 1) as i:
            for u in range(AHEAD_N):
                turn(i * AHEAD_N + u + 2, (u + 2) % AHEAD_N)
                multiply(i * AHEAD_N + u, u % 2)
        for g in range(GROUPS - AHEAD_N, GROUPS):
            if g + 2 < GROUPS:
                turn(g + 2, (g + 2) % AHEAD_N)
            multiply(g, g % 2)


def graph_tables(nc, sem, A, H, GT, SRC_T, DST_T, LAST):
    with ExitStack() as ctx:
        local = lambda n, s, d=F32: ctx.enter_context(nc.sbuf_tensor("sb_gt_" + n, s, d))
        ATT = local("att", [P, 2, GF])
        PROD = local("prod", [P, TILES, GF])
        S, D = local("s", [P, TILES, GHEADS]), local("d", [P, TILES, GHEADS])
        M = local("m", [P, TILES, GHEADS])
        TOP, TOPA = local("top", [P, GHEADS]), local("topa", [P, GHEADS])
        ROWS = local("rows", [P, TILES, ROW])
        a_in, chain, topped, topped_all = sem("att_in"), sem("gt_chain"), sem("top"), sem("top_all")
        args, exps, rows_in, stored, last_in = sem("gt_args"), sem("gt_exps"), sem("gt_rows"), sem("gt_stored"), sem("last_in")
        block = ctx.enter_context(nc.Block())

        @block.sync
        def _(sp):
            for k, n in enumerate(("att_src", "att_dst")):
                sp.dma_start(ATT[:, k, :], A[n].rearrange("h e -> (h e)").partition_broadcast(P)).then_inc(a_in, 16)
            sp.wait_ge(rows_in, 1)
            sp.wait_ge(exps, 4)
            sp.dma_start(SRC_T.rearrange("(s r) w -> r s w", r=P), ROWS[:, :, :]).then_inc(stored, 16)
            sp.dma_start(DST_T.rearrange("(s r) w -> r s w", r=P), GT[:, :, 2 * GHEADS:]).then_inc(stored, 16)
            sp.wait_ge(stored, 32)
            sp.dma_start(LAST[:, :], SRC_T[TOKENS - 1, :].partition_broadcast(P)).then_inc(last_in, 16)
            sp.wait_ge(last_in, 16)

        @block.gpsimd
        def _(pool):
            pool.wait_ge(topped, 1)
            pool.partition_all_reduce(TOPA[:, :], TOP[:, :], P, bass.bass_isa.ReduceOp.max).then_inc(topped_all, 1)

        @block.scalar
        def _(act):
            act.wait_ge(args, 1)
            nc.scalar.activation(GT[:, :, 0:4], S[:, :, :], ACT.Exp).then_inc(exps, 1)
            nc.scalar.activation(GT[:, :, 4:8], S[:, :, :], ACT.Exp, scale=0.2).then_inc(exps, 1)
            act.wait_ge(args, 2)
            nc.scalar.activation(GT[:, :, 8:12], M[:, :, :], ACT.Exp).then_inc(exps, 1)
            nc.scalar.activation(GT[:, :, 12:16], D[:, :, :], ACT.Exp).then_inc(exps, 1)

        @block.vector
        def _(v):
            link = Chain(v, chain)
            v.wait_ge(a_in, 32)
            for k, dst in enumerate((S, D)):
                link(nc.vector.tensor_tensor(PROD[:, :, :], H[:, :, :], ATT[:, k, :].unsqueeze(1).to_broadcast([P, TILES, GF]),
                                             ALU.mult))
                link(nc.vector.tensor_reduce(dst[:, :, :], PROD[:, :, :].rearrange("p s (h e) -> p s h e", e=EXPERTS0),
                                             AX.X, ALU.add))
            link(nc.vector.tensor_reduce(TOP[:, :], S[:, :, :].rearrange("p s h -> p h s"), AX.X, ALU.max))
            v.sem_inc(topped, 1)
            v.wait_ge(topped_all, 1)
            top = TOPA[:, :].unsqueeze(1).to_broadcast([P, TILES, GHEADS])
            link(nc.vector.tensor_tensor(S[:, :, :], S[:, :, :], top, ALU.subtract))
            v.sem_inc(args, 1)
            link(nc.vector.tensor_tensor(D[:, :, :], D[:, :, :], top, ALU.add))
            link(nc.vector.scalar_tensor_tensor(out=M[:, :, :], in0=D[:, :, :], scalar=0.2, in1=D[:, :, :],
                                                op0=ALU.mult, op1=ALU.max))
            link(nc.vector.tensor_tensor(PROD[:, :, 0:4], D[:, :, :], M[:, :, :], ALU.subtract))
            link(nc.vector.scalar_tensor_tensor(out=D[:, :, :], in0=D[:, :, :], scalar=0.2, in1=M[:, :, :],
                                                op0=ALU.mult, op1=ALU.subtract))
            link(nc.vector.tensor_copy(M[:, :, :], PROD[:, :, 0:4]))
            v.sem_inc(args, 1)
            link(nc.vector.tensor_copy(ROWS[:, :, 0:GF], H[:, :, :]))
            v.wait_ge(exps, 2)
            nc.vector.tensor_copy(ROWS[:, :, GF:], GT[:, :, 0:8]).then_inc(rows_in, 1)


def graph_edges(nc, sem, KG, KC, SRC_T, DST_T, TRIPS, SUMS, CN):
    with ExitStack() as ctx:
        local = lambda n, s, d=F32: ctx.enter_context(nc.sbuf_tensor("sb_ge_" + n, s, d))
        iota_i = local("iota_i", [P, P], I32)
        iota_f = local("iota_f", [P, P])
        IDX = local("idx", [P, 2, 2, SLOT], I32)
        LO, HI = local("lo", [P, 2, SLOT], I32), local("hi", [P, 2, SLOT], I32)
        HIF = local("hif", [P, 2, SLOT])
        GS, GD = local("gs", [P, 2, SLOT, ROW]), local("gd", [P, 2, SLOT, 2 * GHEADS])
        W2 = local("w2", [P, SLOT, 2 * GHEADS])
        MSG = local("msg", [P, 2, SLOT, PART])
        OL = local("ol", [P, 2, SLOT, P])
        NB = 4
        B = local("b", [P, NB, TILES, PART])
        PER = HALF // SLOT
        CLO, CHI = local("c_lo", [P, HALF], I32), local("c_hi", [P, 2, HALF], I32)
        CLN = local("c_minus_lo", [P, 2, HALF])
        NC = 4
        CL, CH = local("c_onehot_lo", [P, NC, PER, P], BF16), local("c_onehot_hi", [P, NC, PER, TILES], BF16)
        AWAY = local("c_distance", [P, 2, PER, P], BF16)
        CHUNKS = ((0, 22), (22, 22), (44, 20))
        ACC = ctx.enter_context(nc.psum_tensor("acc", [P, 3, BANK], F32))
        COUNT = ctx.enter_context(nc.psum_tensor("p_count", [P, BANK], F32))
        gathers_on, iota_made = sem("ge_gathers_on"), sem("ge_iota")
        iota_cast = sem("ge_iota_cast")
        decoded, gathered_s, gathered_d = sem("ge_decoded"), [sem(f"ge_src{u}") for u in range(2)], [sem(f"ge_dst{u}") for u in range(2)]
        products, weights, messages, ol_made = sem("ge_products"), sem("ge_weights"), sem("ge_messages"), sem("ge_ol")
        b_made, b_free, half_used, acc_done, chain = sem("ge_b_made"), sem("ge_b_free"), sem("ge_half_used"), sem("ge_done"), sem("ge_chain")
        c_decoded, hot_hi, hot_lo, hot_free = sem("ge_c_decoded"), sem("ge_hot_hi"), sem("ge_hot_lo"), sem("ge_hot_free")
        lo_ready, away = sem("ge_lo_ready"), sem("ge_distance")
        block = ctx.enter_context(nc.Block())
        trips = lambda engine, k, top: engine.value_load(TRIPS[0:1, k:k + 1], min_val=1, max_val=top)
        MOST = ROUNDS * STRIDE
        MOST_COUNT = -(-((ROUNDS + 1) * FOUND + TAKE) // HALF) + 1
        both_trips = lambda engine: trips(engine, 0, (MOST_COUNT + 1) // 2)
        gather_trips = lambda engine: trips(engine, 1, MOST)
        count_trips = lambda engine: trips(engine, 2, MOST_COUNT)

        @block.gpsimd
        def _(pool):
            pool.iota(iota_i[:, :], pattern=[[1, P]], base=0, channel_multiplier=0).then_inc(iota_made, 1)
            n_both, n_gather = both_trips(pool), gather_trips(pool)

            def gather(n, u):
                pool.wait_ge(decoded, n + 1)
                pool.wait_ge(messages, n - 1 + 2)
                pool.sem_inc(gathers_on, 1)
                for k in range(SLOT):
                    pool.indirect_dma_start(GS[:, u, k, :], None, SRC_T,
                                            bass.IndirectOffsetOnAxis(ap=IDX[:, u, 0, k:k + 1], axis=0)).then_inc(gathered_s[u], 16)
                    pool.indirect_dma_start(GD[:, u, k, :], None, DST_T,
                                            bass.IndirectOffsetOnAxis(ap=IDX[:, u, 1, k:k + 1], axis=0)).then_inc(gathered_d[u], 16)

            n_all = n_both + n_gather
            with pool.Fori(0, n_all) as i:
                for u in range(2):
                    gather(i * 2 + u, u)
            gather(n_all * 2, 0)

        @block.scalar
        def _(act):
            act.wait_ge(iota_cast, 1)

            def one_hots_lo(n, u):
                def distances(k):
                    act.wait_ge(hot_lo, n * SLOT + k - 1 + 2 * SLOT)
                    for j in range(PER):
                        last = nc.scalar.activation(AWAY[:, k % 2, j, :], iota_f[:, :], ACT.Abs,
                                                    bias=CLN[:, u, k * PER + j:k * PER + j + 1])
                    last.then_inc(away, 1)

                act.wait_ge(lo_ready, n + 1)
                distances(0)
                for k in range(SLOT):
                    if k + 1 < SLOT:
                        distances(k + 1)
                    act.wait_ge(hot_free, n * SLOT + k + 1)
                    act.wait_ge(away, n * SLOT + k + 1)
                    nc.scalar.activation(CL[:, k % NC, :, :], AWAY[:, k % 2, :, :], ACT.Relu, bias=1.0, scale=-1.0).then_inc(hot_lo, 1)

            n_both, n_count = both_trips(act), count_trips(act)
            with act.Fori(0, n_both) as i:
                for u in range(2):
                    one_hots_lo(i * 2 + u, u)
            with act.Fori(0, n_count) as i:
                one_hots_lo(n_both * 2 + i, 0)

        @block.vector
        def _(v):
            v.wait_ge(iota_made, 1)
            v.sem_inc(b_made, AHEAD)
            v.sem_inc(half_used, AHEAD)
            v.sem_inc(messages, 2)
            v.sem_inc(hot_hi, AHEAD)
            v.sem_inc(hot_lo, 2 * SLOT)
            nc.vector.tensor_copy(iota_f[:, :], iota_i[:, :]).then_inc(iota_cast, 1)

            def decode(n, u):
                at = nc.s_assert_within(n * SLOT, 0, GCOLS - SLOT, skip_runtime_bounds_check_because=
                                        "the trips are made from the number of KG's slots in use")
                bits = KG[:, ds(at, SLOT)].bitcast(I32)
                nc.vector.tensor_scalar(IDX[:, u, 0, :], bits, TOKENS - 1, None, ALU.bitwise_and)
                nc.vector.tensor_scalar(IDX[:, u, 1, :], bits, NODE_BITS, TOKENS - 1, ALU.logical_shift_right, ALU.bitwise_and)
                nc.vector.tensor_scalar(LO[:, u, :], bits, NODE_BITS, P - 1, ALU.logical_shift_right, ALU.bitwise_and)
                nc.vector.tensor_scalar(HI[:, u, :], bits, NODE_BITS + LO_BITS, (VALID >> 20) + TILES - 1,
                                        ALU.logical_shift_right, ALU.bitwise_and).then_inc(decoded, 1)

            def decode_clamped(n, u, buffers=2):
                after(v, c_decoded, n * 2)
                after(v, hot_hi, (n + 1 - buffers) * SLOT + AHEAD)
                at = n * HALF if isinstance(n, int) else nc.s_assert_within(
                    n * HALF, 0, KCOLS - HALF, skip_runtime_bounds_check_because=
                    "the trips are made from the number of KC's slots in use")
                bits = KC[:, ds(at, HALF)].bitcast(I32)
                nc.vector.tensor_scalar(CLO[:, :], bits, NODE_BITS, P - 1, ALU.logical_shift_right, ALU.bitwise_and)
                nc.vector.tensor_scalar(CHI[:, u, :], bits, NODE_BITS + LO_BITS, (VALID >> 20) + TILES - 1,
                                        ALU.logical_shift_right, ALU.bitwise_and).then_inc(c_decoded, 1)

            def ready_clamped(n, u, buffers=2):
                v.wait_ge(c_decoded, n * 2 + 1)
                v.wait_ge(hot_lo, (n + 3 - buffers) * SLOT)
                nc.vector.tensor_scalar(CLN[:, u, :], CLO[:, :], -1.0, None, ALU.mult).then_inc(lo_ready, 1)
                nc.vector.tensor_scalar(CHI[:, u, :], CHI[:, u, :], VALID >> 20, None, ALU.subtract).then_inc(c_decoded, 1)

            def one_hot_hi(n, u, k):
                if k == 0:
                    v.wait_ge(c_decoded, n * 2 + 2)
                v.wait_ge(hot_free, n * SLOT + k + 1)
                nc.vector.tensor_tensor(CH[:, k % NC, :, :], iota_i[:, 0:TILES].unsqueeze(1).to_broadcast([P, PER, TILES]),
                                        CHI[:, u, k * PER:(k + 1) * PER].unsqueeze(2).to_broadcast([P, PER, TILES]),
                                        ALU.is_equal).then_inc(hot_hi, 1)

            def low_bits(n, u):
                after(v, decoded, n + 1)
                after(v, half_used, n - 1 + AHEAD)
                nc.vector.tensor_scalar(HIF[:, u, :], HI[:, u, :], VALID >> 20, None, ALU.subtract)
                nc.vector.tensor_tensor(OL[:, u, :, :], iota_f[:, :].unsqueeze(1).to_broadcast([P, SLOT, P]),
                                        LO[:, u, :].unsqueeze(2).to_broadcast([P, SLOT, P]), ALU.is_equal).then_inc(ol_made, 1)

            def factors(n, i, u):
                v.wait_ge(gathered_s[u], (i + 1) * 16 * SLOT)
                v.wait_ge(gathered_d[u], (i + 1) * 16 * SLOT)
                after(v, weights, n)
                nc.vector.tensor_tensor(W2[:, :, :], GS[:, u, :, GF:], GD[:, u, :, :], ALU.mult).then_inc(products, 1)

            def weigh(n, u):
                after(v, products, n + 1)
                after(v, b_made, (n - 1) * SLOT + AHEAD)
                nc.vector.tensor_tensor(MSG[:, u, :, GF:], W2[:, :, 0:GHEADS], W2[:, :, GHEADS:], ALU.max).then_inc(weights, 1)

            def message(n, u):
                after(v, weights, n + 1)
                nc.vector.tensor_tensor(MSG[:, u, :, 0:GF].rearrange("p k (h e) -> p k h e", e=EXPERTS0),
                                        GS[:, u, :, 0:GF].rearrange("p k (h e) -> p k h e", e=EXPERTS0),
                                        MSG[:, u, :, GF:].unsqueeze(3).to_broadcast([P, SLOT, GHEADS, EXPERTS0]),
                                        ALU.mult).then_inc(messages, 1)

            def next_numbers(n, u):
                v.wait_ge(ol_made, n + 1)
                decode(n + 2, u)

            def half(n, i, u, counting):
                following = n + 1, 1 - u
                between = {3: lambda: low_bits(*following), 4: lambda: factors(n + 1, i + u, 1 - u), 5: lambda: weigh(*following),
                           6: lambda: message(*following), 7: lambda: next_numbers(*following)}
                if counting:
                    between.update({1: lambda: decode_clamped(*following), 2: lambda: ready_clamped(*following)})
                v.wait_ge(messages, n + 1 + 2)
                for k in range(SLOT):
                    v.wait_ge(b_free, n * SLOT + k + 1)
                    nc.vector.scalar_tensor_tensor(
                        out=B[:, k % NB, :, :], in0=iota_f[:, 0:TILES].unsqueeze(2).to_broadcast([P, TILES, PART]),
                        scalar=HIF[:, u, k:k + 1], in1=MSG[:, u, k, :].unsqueeze(1).to_broadcast([P, TILES, PART]),
                        op0=ALU.is_equal, op1=ALU.mult).then_inc(b_made, 1)
                    if counting:
                        one_hot_hi(n, u, k)
                    if k in between:
                        between[k]()

            n_both, n_gather, n_count = both_trips(v), gather_trips(v), count_trips(v)
            v.wait_ge(iota_cast, 1)
            decode(0, 0)
            decode(1, 1)
            decode_clamped(0, 0)
            ready_clamped(0, 0)
            low_bits(0, 0)
            factors(0, 0, 0)
            weigh(0, 0)
            message(0, 0)
            next_numbers(0, 0)
            with v.Fori(0, n_both) as i:
                for u in range(2):
                    half(i * 2 + u, i, u, True)
            with v.Fori(0, n_gather) as i:
                for u in range(2):
                    half((n_both + i) * 2 + u, n_both + i, u, False)
            with v.Fori(0, n_count) as i:
                n = n_both * 2 + i
                for k in range(SLOT):
                    one_hot_hi(n, 0, k)
                decode_clamped(n + 1, 0, 1)
                ready_clamped(n + 1, 0, 1)
            v.wait_ge(acc_done, 1)
            for c, (h0, hn) in enumerate(CHUNKS):
                last = nc.vector.tensor_copy(SUMS[:, h0:h0 + hn, :], ACC[:, c, 0:hn * PART].rearrange("p (h w) -> p h w", w=PART))
            last.then_inc(chain, 1)
            nc.vector.tensor_copy(CN[:, :], COUNT[:, 0:TILES]).then_inc(chain, 1)
            v.wait_ge(chain, 2)

        @block.tensor
        def _(pe):
            n_both, n_gather, n_count = both_trips(pe), gather_trips(pe), count_trips(pe)
            zero = KG[:, KG.shape[1] - P:]
            zero_b = zero.bitcast(BF16)

            def add(left, right, **flags):
                for c, (h0, hn) in enumerate(CHUNKS):
                    last = nc.tensor.matmul(ACC[:, c, 0:hn * PART], left, right(h0, hn), skip_group_check=True, **flags)
                return last

            def count(q, made):
                pe.wait_ge(hot_hi, made + 1 + AHEAD)
                pe.wait_ge(hot_lo, made + 1 + 2 * SLOT)
                for k in range(PER):
                    last = nc.tensor.matmul(COUNT[:, 0:TILES], CL[:, q, k, :], CH[:, q, k, :], start=False, stop=False,
                                            skip_group_check=True)
                last.then_inc(hot_free, 1)

            def half(n, u, counting):
                pe.wait_ge(ol_made, n + 1)
                for k in range(SLOT):
                    pe.wait_ge(b_made, n * SLOT + k + 1 + AHEAD)
                    b = B[:, k % NB, :, :].rearrange("p h w -> p (h w)")
                    last = add(OL[:, u, k, :], lambda h0, hn: b[:, h0 * PART:(h0 + hn) * PART], start=False, stop=False)
                    last.then_inc(b_free, 1)
                    if counting and k > 0:
                        count((k - 1) % NC, n * SLOT + k - 1)
                if counting:
                    count((SLOT - 1) % NC, n * SLOT + SLOT - 1)
                pe.wait_ge(b_free, (n + 1) * SLOT + NB)
                pe.sem_inc(half_used, 1)

            zeros = lambda h0, hn: zero.unsqueeze(1).to_broadcast([P, 4, P])[:, :, 0:hn * 5]
            pe.sem_inc(b_free, NB)
            pe.sem_inc(hot_free, NC)
            add(zero, zeros, start=True, stop=False)
            nc.tensor.matmul(COUNT[:, 0:TILES], zero_b[:, 0:P], zero_b[:, 0:TILES], start=True, stop=False, skip_group_check=True)
            with pe.Fori(0, n_both) as i:
                for u in range(2):
                    half(i * 2 + u, u, True)
            with pe.Fori(0, n_gather) as i:
                for u in range(2):
                    half((n_both + i) * 2 + u, u, False)
            with pe.Fori(0, n_count) as i:
                for k in range(SLOT):
                    count(k % NC, (n_both * 2 + i) * SLOT + k)
            nc.tensor.matmul(COUNT[:, 0:TILES], zero_b[:, 0:P], zero_b[:, 0:TILES], start=False, stop=True, skip_group_check=True)
            add(zero, zeros, start=False, stop=True).then_inc(acc_done, 1)


def rank_gates(nc, link, score, experts, tmp, tmp2, earlier, keep):
    shape = [P, TILES, experts, experts]
    view = lambda t: t.rearrange("p (s a b) -> p s a b", a=experts, b=experts)
    this, other = score.unsqueeze(3).to_broadcast(shape), score.unsqueeze(2).to_broadcast(shape)
    link(nc.vector.tensor_tensor(view(tmp), other, this, ALU.is_gt))
    link(nc.vector.tensor_tensor(view(tmp2), other, this, ALU.is_equal))
    link(nc.vector.tensor_tensor(view(tmp2), view(tmp2),
                                 earlier.unsqueeze(1).to_broadcast(shape), ALU.mult))
    link(nc.vector.tensor_tensor(tmp, tmp, tmp2, ALU.add))
    link(nc.vector.tensor_reduce(keep, view(tmp), AX.X, ALU.add))
    link(nc.vector.tensor_scalar(keep, keep, 2.0, None, ALU.is_lt))


def earlier_mask(nc, pool, earlier, experts, made):
    pool.memset(earlier, 1.0).then_inc(made, 1)
    pool.wait_ge(made, 1)
    pool.affine_select(out=earlier, in_=earlier, compare_op=ALU.is_gt, fill=0.0, base=0,
                       pattern=[[1, experts], [-1, experts]], channel_multiplier=0).then_inc(made, 1)


def graph_gates(nc, sem, A, H, GT, LAST, SUMS, CN, G, clear, load):
    with ExitStack() as ctx:
        local = lambda n, s, d=F32: ctx.enter_context(nc.sbuf_tensor("sb_gg_" + n, s, d))
        vec = local("vec", [P, 3, GF])
        W2 = local("w2", [P, TILES, 8])
        W1 = local("w1", [P, TILES, 4])
        M = local("m", [P, TILES, GF])
        AG = local("ag", [P, TILES, GF])
        st = local("st", [P, 4, TILES])
        RD = local("rd", [P, TILES, 4])
        t1, t2 = local("t1", [P, TILES * 16]), local("t2", [P, TILES * 16])
        earlier = local("earlier", [P, 4, 4])
        SC, KEEP = local("sc", [P, TILES, 4]), local("keep", [P, TILES, 4])
        v_in, made, chain, var, root, shifted, exped = (sem("gg_" + n) for n in ("in", "made", "chain", "var", "root", "shifted", "exped"))
        block = ctx.enter_context(nc.Block())

        @block.sync
        def _(sp):
            for k, n in enumerate(("b_gat", "ln_gamma", "ln_beta")):
                sp.dma_start(vec[:, k, :], A[n].partition_broadcast(P)).then_inc(v_in, 16)
            load(sp)
            sp.wait_ge(v_in, 48)

        @block.gpsimd
        def _(pool):
            clear(pool)
            earlier_mask(nc, pool, earlier[:, :, :], 4, made)

        @block.scalar
        def _(act):
            act.wait_ge(var, 1)
            nc.scalar.activation(st[:, 2, :], st[:, 1, :], ACT.Sqrt).then_inc(root, 1)
            act.wait_ge(shifted, 1)
            nc.scalar.activation(SC[:, :, :], SC[:, :, :], ACT.Exp).then_inc(exped, 1)

        @block.vector
        def _(v):
            link = Chain(v, chain)
            h4 = lambda t: t.rearrange("p s (h e) -> p s h e", e=4)
            w4 = lambda: W1[:, :, :].unsqueeze(3).to_broadcast([P, TILES, 4, 4])
            v.wait_ge(v_in, 48)
            link(nc.vector.tensor_tensor(W2[:, :, :], GT[:, :, 0:8], GT[:, :, 8:16], ALU.mult))
            link(nc.vector.tensor_tensor(W1[:, :, :], W2[:, :, 0:4], W2[:, :, 4:8], ALU.max))
            link(nc.vector.tensor_tensor(h4(M[:, :, :]), h4(H[:, :, :]), w4(), ALU.mult))
            link(nc.vector.tensor_tensor(SUMS[:, :, 0:GF], SUMS[:, :, 0:GF], M[:, :, :], ALU.add))
            link(nc.vector.tensor_tensor(SUMS[:, :, GF:], SUMS[:, :, GF:], W1[:, :, :], ALU.add))
            link(nc.vector.tensor_tensor(W2[:, :, :], LAST[:, GF:].unsqueeze(1).to_broadcast([P, TILES, 8]), GT[:, :, 8:16], ALU.mult))
            link(nc.vector.tensor_tensor(W1[:, :, :], W2[:, :, 0:4], W2[:, :, 4:8], ALU.max))
            link(nc.vector.tensor_tensor(W1[:, :, :], W1[:, :, :], CN[:, :].unsqueeze(2).to_broadcast([P, TILES, 4]), ALU.mult))
            link(nc.vector.tensor_tensor(h4(M[:, :, :]), h4(LAST[:, 0:GF].unsqueeze(1).to_broadcast([P, TILES, GF])), w4(), ALU.mult))
            link(nc.vector.tensor_tensor(SUMS[:, :, 0:GF], SUMS[:, :, 0:GF], M[:, :, :], ALU.add))
            link(nc.vector.tensor_tensor(SUMS[:, :, GF:], SUMS[:, :, GF:], W1[:, :, :], ALU.add))
            link(nc.vector.tensor_scalar(RD[:, :, :], SUMS[:, :, GF:], 1e-16, None, ALU.add))
            link(nc.vector.reciprocal(RD[:, :, :], RD[:, :, :]))
            link(nc.vector.tensor_tensor(h4(AG[:, :, :]), h4(SUMS[:, :, 0:GF]), RD[:, :, :].unsqueeze(3).to_broadcast([P, TILES, 4, 4]), ALU.mult))
            bc = lambda k: vec[:, k, :].unsqueeze(1).to_broadcast([P, TILES, GF])
            link(nc.vector.tensor_tensor(AG[:, :, :], AG[:, :, :], bc(0), ALU.add))
            wide = lambda k: st[:, k, :].unsqueeze(2).to_broadcast([P, TILES, GF])
            link(nc.vector.tensor_reduce(st[:, 0, :], AG[:, :, :], AX.X, ALU.add))
            link(nc.vector.tensor_scalar(st[:, 0, :], st[:, 0, :], 1.0 / GF, None, ALU.mult))
            link(nc.vector.tensor_tensor(AG[:, :, :], AG[:, :, :], wide(0), ALU.subtract))
            link(nc.vector.tensor_tensor(M[:, :, :], AG[:, :, :], AG[:, :, :], ALU.mult))
            link(nc.vector.tensor_reduce(st[:, 1, :], M[:, :, :], AX.X, ALU.add))
            link(nc.vector.tensor_scalar(st[:, 1, :], st[:, 1, :], 1.0 / GF, EPS_T, ALU.mult, ALU.add))
            v.sem_inc(var, 1)
            v.wait_ge(root, 1)
            link(nc.vector.reciprocal(st[:, 3, :], st[:, 2, :]))
            link(nc.vector.tensor_tensor(AG[:, :, :], AG[:, :, :], wide(3), ALU.mult))
            link(nc.vector.tensor_tensor(AG[:, :, :], AG[:, :, :], bc(1), ALU.mult))
            link(nc.vector.tensor_tensor(AG[:, :, :], AG[:, :, :], bc(2), ALU.add))
            link(nc.vector.tensor_reduce(SC[:, :, :], AG[:, :, :].rearrange("p s (h e) -> p s e h", e=4), AX.X, ALU.add))
            link(nc.vector.tensor_scalar(SC[:, :, :], SC[:, :, :], 0.25, None, ALU.mult))
            v.wait_ge(made, 2)
            rank_gates(nc, link, SC[:, :, :], 4, t1[:, :], t2[:, :], earlier[:, :, :], KEEP[:, :, :])
            link(nc.vector.tensor_reduce(st[:, 0, :], SC[:, :, :], AX.X, ALU.max))
            link(nc.vector.tensor_tensor(SC[:, :, :], SC[:, :, :], st[:, 0, :].unsqueeze(2).to_broadcast([P, TILES, 4]), ALU.subtract))
            v.sem_inc(shifted, 1)
            v.wait_ge(exped, 1)
            link(nc.vector.tensor_tensor(SC[:, :, :], SC[:, :, :], KEEP[:, :, :], ALU.mult))
            link(nc.vector.tensor_reduce(st[:, 0, :], SC[:, :, :], AX.X, ALU.add))
            link(nc.vector.reciprocal(st[:, 1, :], st[:, 0, :]))
            link(nc.vector.tensor_tensor(G[:, :, :], SC[:, :, :], st[:, 1, :].unsqueeze(2).to_broadcast([P, TILES, 4]), ALU.mult))


def expert_weights(nc, sem, ctx, tag, experts, chunks, W1, b1, W2, b2):
    local = lambda n, s: ctx.enter_context(nc.sbuf_tensor(f"sb_{tag}_{n}", s, F32))
    n_pieces = experts * chunks
    w1 = local("w1", [C, n_pieces * P])
    w2 = local("w2", [P, n_pieces, C])
    bb1 = local("b1", [P, n_pieces])
    B2 = local("b2", [GROUP * experts, BANK])
    w_in, zero = sem(tag + "_w_in"), sem(tag + "_zero")

    def clear(pool):
        pool.memset(B2[:, :], 0.0).then_inc(zero, 1)

    def load(queue):
        queue.dma_start(w1[:, :].rearrange("c (e h) -> c e h", e=experts), W1.rearrange("e c h -> c e h")).then_inc(w_in, 16)
        queue.dma_start(w2[:, :, :], W2.rearrange("e (k p) c -> p (e k) c", p=P)).then_inc(w_in, 16)
        queue.dma_start(bb1[:, :], b1.rearrange("e (k p) -> p (e k)", p=P), allow_slow_non_contiguous=True).then_inc(w_in, 16)
        queue.wait_ge(zero, 1)
        for k in range(GROUP):
            queue.dma_start(B2[k * experts:(k + 1) * experts, k * C:(k + 1) * C], b2).then_inc(w_in, 16)
        queue.wait_ge(w_in, 16 * (3 + GROUP))

    return (w1, w2, bb1, B2), clear, load


def run_experts(nc, sem, tag, X2, TT, G, experts, chunks, weights, ident, store, BN=None):
    with ExitStack() as ctx:
        local = lambda n, s, d=F32: ctx.enter_context(nc.sbuf_tensor(f"sb_{tag}_{n}", s, d))
        pbank = lambda n: ctx.enter_context(nc.psum_tensor(f"{tag}_{n}", [P, BANK], F32))
        NCH = experts * chunks
        YB = experts * C // BANK
        w1, w2, bb1, B2 = weights
        HT = local("ht", [P, 2, NCH, BANK])
        GC = local("gc", [P, 2, GROUP * experts])
        GTR = local("gtr", [GROUP * experts, P])
        PU = [pbank(f"pu{k}") for k in range(2)]
        NY = 4
        PY = [pbank(f"py{k}") for k in range(NY)]
        PB2, PG = pbank("pb2"), pbank("pg")
        hidden, up_done = sem(tag + "_hidden"), sem(tag + "_up_done")
        gates_in, gates_turned, gates_out, bias_done = (sem(f"{tag}_{n}") for n in ("gates_in", "gates_turned", "gates_out", "bias_done"))
        y_done, added, stored = (sem(f"{tag}_{n}") for n in ("y_done", "added", "stored"))
        term, carried = sem(f"{tag}_term"), sem(f"{tag}_carried")
        block = ctx.enter_context(nc.Block())

        @block.sync
        def _(sp):
            sent = 0
            for part in range(4):
                sp.wait_ge(added, (part + 1) * GROUPS // 4 + AHEAD)
                sent += store(sp, part, stored)
            sp.wait_ge(stored, 16 * sent)

        @block.scalar
        def _(act):
            def hide(g, u):
                act.wait_ge(bias_done, g + 1)
                for c in range(NCH):
                    act.wait_ge(up_done, g * NCH + c + 1)
                    nc.scalar.activation(HT[:, u, c, :], PU[c % 2][:, :], ACT.Gelu, bias=bb1[:, c:c + 1])\
                        .then_inc(hidden, 1)
            with act.Fori(0, GROUPS // 2) as i:
                for u in range(2):
                    hide(i * 2 + u, u)

        @block.tensor
        def _(pe):
            def up(g, c):
                pe.wait_ge(hidden, g * NCH + c + 1)
                nc.tensor.matmul(PU[c % 2][:, :], w1[:, c * P:(c + 1) * P], TT[:, ds(g * BANK, BANK)], start=True, stop=True)\
                    .then_inc(up_done, 1)

            def down(g, u, k):
                for b in range(YB):
                    n = (g * GROUP + k) * YB + b
                    pe.wait_ge(term, 4 * n + 4)
                    bank = PY[(k * YB + b) % NY]
                    for e in range(b * 4, b * 4 + 4):
                        for c in range(chunks):
                            last = nc.tensor.matmul(bank[:, (e % 4) * C:(e % 4 + 1) * C],
                                                    HT[:, u, e * chunks + c, k * P:(k + 1) * P], w2[:, e * chunks + c, :],
                                                    start=(c == 0), stop=(c == chunks - 1))
                    last.then_inc(y_done, 1)

            def turn_gates(g, u):
                pe.wait_ge(gates_in, g + 1)
                nc.tensor.transpose(PG[0:GROUP * experts, 0:P], GC[:, u, :], ident[:, :]).then_inc(gates_turned, 1)

            def biases(g):
                pe.wait_ge(gates_out, g + 1)
                pe.wait_ge(added, g + AHEAD)
                nc.tensor.matmul(PB2[:, :], GTR[:, :], B2[:, :], start=True, stop=True).then_inc(bias_done, 1)

            pe.sem_inc(hidden, 2)
            pe.sem_inc(bias_done, 2)
            pe.sem_inc(term, 4 * NY)
            for c in range(NCH):
                up(0, c)

            def turn(g, u, more):
                pe.wait_ge(hidden, (g + 1) * NCH + 2)
                for c in range(NCH):
                    if more:
                        up(g + 1, c)
                    if c % 2 == 1:
                        if c // 2 < GROUP:
                            down(g, u, c // 2)
                        if c == 1:
                            turn_gates(g, u)
                biases(g)

            with pe.Fori(0, GROUPS // 2 - 1) as i:
                for u in range(2):
                    turn(i * 2 + u, u, True)
            turn(GROUPS - 2, 0, True)
            turn(GROUPS - 1, 1, False)

        @block.vector
        def _(v):
            v.sem_inc(gates_turned, AHEAD)
            v.sem_inc(added, AHEAD)

            def group(g, u):
                v.wait_ge(gates_turned, g + AHEAD)
                nc.vector.tensor_copy(GC[:, u, :].rearrange("p (t e) -> p t e", e=experts),
                                      G[:, ds(g * GROUP, GROUP), :]).then_inc(gates_in, 1)
                if not isinstance(g, int) or g > 0:
                    statistics(g - 1)
                v.wait_ge(gates_in, g + 1)
                for k in range(GROUP):
                    xs = X2[:, ds((g * GROUP + k) * C, C)]
                    for e in range(experts):
                        n = (g * GROUP + k) * experts + e
                        b = e // 4
                        if e % 4 == 0:
                            v.wait_ge(y_done, (g * GROUP + k) * YB + b + 1)
                        v.wait_ge(term, n + 4 * NY)
                        last = nc.vector.scalar_tensor_tensor(
                            out=xs, in0=PY[(k * YB + b) % NY][:, (e % 4) * C:(e % 4 + 1) * C],
                            scalar=GC[:, u, k * experts + e:k * experts + e + 1], in1=xs, op0=ALU.mult, op1=ALU.add)
                        last.then_inc(term, 1)
                    if k == 1:
                        v.wait_ge(gates_turned, g + 1 + AHEAD)
                        v.wait_ge(bias_done, g + 2)
                        nc.vector.tensor_copy(GTR[:, :], PG[0:GROUP * experts, 0:P]).then_inc(gates_out, 1)
                v.wait_ge(bias_done, g + 3)
                v.wait_ge(term, (g + 1) * GROUP * experts + 4 * NY)
                xg = X2[:, ds(g * BANK, BANK)]
                nc.vector.tensor_tensor(xg, PB2[:, :], xg, ALU.add).then_inc(added, 1)

            def statistics(g):
                if BN is not None:
                    v.wait_ge(added, g + 1 + AHEAD)
                    v.sem_inc(carried, 1)
                    for k in range(GROUP):
                        tile_statistics(nc, BN, X2, g * GROUP + k)

            for u in range(2):
                group(u, u)
            with v.Fori(1, GROUPS // 2) as i:
                for u in range(2):
                    group(i * 2 + u, u)
            statistics(GROUPS - 1)


def mix_weights(nc, sem, A, X, BN, XN, XN_D, X_D, mean, rstd, WT, U, CB, ident, x_back):
    with ExitStack() as ctx:
        local = lambda n, s, d=F32: ctx.enter_context(nc.sbuf_tensor("sb_mw_" + n, s, d))
        pbank = lambda n: ctx.enter_context(nc.psum_tensor("mw_" + n, [P, BANK], F32))
        tmp = local("tmp", [P, 2, TILES])
        unit = local("unit", [P, 2 * F - 1])
        XM, XMT = local("xm", [F, C]), local("xmt", [C, F])
        WQK, BQK = local("wqk", [C, LH, C, 2]), local("bqk", [C, LH, 2])
        WV, WVT = local("wv", [C, LH * C]), local("wvt", [C, LH * C])
        WP = local("wp", [P, LH, C])
        BV, BP = local("bv", [P, LH]), local("bp", [P, 1])
        QK = local("qk", [C, LH, 2, F])
        SCO = local("sco", [F, LH, F])
        sm = local("sm", [F, 2, LH])
        p_mean, p_score, p_qk, p_wv, p_u, p_c = (pbank(n) for n in ("mean", "score", "qk", "wv", "u", "c"))
        w_in, chain, var, root, normed = (sem("mw_" + n) for n in ("in", "chain", "var", "root", "normed"))
        shift = local("shift", [P, TILES])
        shift_made, normed_s = sem("mw_shift_made"), sem("mw_normed_s")
        n_stored, unit_set = sem("n_stored"), sem("unit_set")
        mean_done, xm_out, xm_turned, xmt_out = (sem("mw_" + n) for n in ("mean_done", "xm_out", "xm_turned", "xmt_out"))
        qk_done, qk_out, sc_done, shifted, exped, prob, wt_done = (sem("mw_" + n) for n in ("qk_done", "qk_out", "sc_done", "shifted", "exped", "prob", "wt_done"))
        wvt_done, wvt_out, u_done = (sem("mw_" + n) for n in ("wvt_done", "wvt_out", "u_done"))
        block = ctx.enter_context(nc.Block())
        X2 = X[:, :, :].rearrange("p s c -> p (s c)")
        NORM = 4
        part = F // NORM

        @block.sync
        def _(sp):
            for k in range(NORM):
                sp.wait_ge(normed, (k + 1) * part // GROUP)
                sp.wait_ge(normed_s, (k + 1) * part // GROUP)
                sp.dma_start(XN_D[k * part:(k + 1) * part].rearrange("f t c -> t f c"),
                             XN[:, k * part * C:(k + 1) * part * C].rearrange("p (f c) -> p f c", c=C)).then_inc(n_stored, 16)
            for a in range(2):
                sp.dma_start(X[a * F:(a + 1) * F, :, :],
                             X_D.rearrange("f (j a) c -> a f j c", a=2)[a]).then_inc(x_back, 16)
            sp.wait_ge(n_stored, 16 * NORM)

        @block.scalar
        def _(act):
            for dst, src in ((WV[:, :], A["Wv"]), (WP[:, :, :], A["Wproj"].rearrange("(h d) c -> d h c", h=LH)),
                             (WQK[:, :, :, :].rearrange("c h d k -> c (h d k)"), A["Wqk"]),
                             (BQK[:, :, :], A["bqk"].rearrange("(h d k) -> d h k", h=LH, k=2)),
                             (BV[:, :], A["bv"].rearrange("(h d) -> d h", h=LH)), (BP[:, :], A["bproj"].unsqueeze(1))):
                act.dma_start(dst, src, allow_slow_non_contiguous=True).then_inc(w_in, 16)
            act.wait_ge(var, 1)
            nc.scalar.activation(tmp[:, 0, :], tmp[:, 1, :], ACT.Sqrt).then_inc(root, 1)
            act.wait_ge(wvt_done, 1)
            nc.scalar.activation(WVT[:, :], p_wv[:, :], ACT.Copy).then_inc(wvt_out, 1)
            act.wait_ge(shift_made, 1)
            for t in range(1, TILES, 2):
                last = nc.scalar.activation(XN[:, t * C:(t + 1) * C], X2[:, t * C:(t + 1) * C], ACT.Identity,
                                            bias=shift[:, t:t + 1], scale=rstd[:, t:t + 1])
                if t % GROUP == GROUP - 1:
                    last.then_inc(normed_s, 1)
            act.wait_ge(u_done, 1)
            act.wait_ge(w_in, 96)
            nc.scalar.activation(U[:, :, :].rearrange("p h c -> p (h c)"), p_u[:, :], ACT.Copy)
            nc.scalar.activation(CB[:, :], p_c[:, 0:1], ACT.Identity, bias=BP[:, :])
            act.wait_ge(shifted, 1)
            nc.scalar.activation(SCO[:, :, :], SCO[:, :, :], ACT.Exp).then_inc(exped, 1)

        @block.vector
        def _(v):
            link = Chain(v, chain)
            link(nc.vector.memset(unit[:, :], 0.0))
            nc.vector.memset(unit[:, F - 1:F], 1.0 / T).then_inc(unit_set, 1)
            layer_statistics(nc, v, link, BN, mean, rstd, tmp[:, 0, :])
            link(nc.vector.tensor_scalar(tmp[:, 1, :], rstd, EPS_C, None, ALU.add))
            v.sem_inc(var, 1)
            v.wait_ge(root, 1)
            link(nc.vector.reciprocal(rstd, tmp[:, 0, :]))
            link(nc.vector.scalar_tensor_tensor(out=shift[:, :], in0=mean, scalar=-1.0, in1=rstd, op0=ALU.mult, op1=ALU.mult))
            v.sem_inc(shift_made, 1)
            with v.Fori(0, GROUPS // 4) as i:
                for j in range(4):
                    for k in range(0, GROUP, 2):
                        t = (i * 4 + j) * GROUP + k
                        last = nc.vector.tensor_scalar(XN[:, ds(t * C, C)], X2[:, ds(t * C, C)],
                                                       mean[:, ds(t, 1)], rstd[:, ds(t, 1)], ALU.subtract, ALU.mult)
                    last.then_inc(normed, 1)
            v.wait_ge(mean_done, 1)
            nc.vector.tensor_copy(XM[:, :], p_mean[0:F, 0:C]).then_inc(xm_out, 1)
            v.wait_ge(xm_turned, 1)
            nc.vector.tensor_copy(XMT[:, :], p_score[:, 0:F]).then_inc(xmt_out, 1)
            v.wait_ge(w_in, 96)
            v.wait_ge(qk_done, 1)
            for h in range(LH):
                for k in range(2):
                    last = nc.vector.tensor_scalar(QK[:, h, k, :], p_qk[:, (h * 2 + k) * F:(h * 2 + k + 1) * F],
                                                   BQK[:, h, k:k + 1], 1.0 / math.sqrt(C), ALU.add, ALU.mult)
            last.then_inc(qk_out, 1)
            v.wait_ge(sc_done, 1)
            s3 = p_score[0:F, 0:LH * F].rearrange("p (h g) -> p h g", g=F)
            wide = lambda k: sm[:, k, :].unsqueeze(2).to_broadcast([F, LH, F])
            link(nc.vector.tensor_reduce(sm[:, 0, :], s3, AX.X, ALU.max))
            link(nc.vector.tensor_tensor(SCO[:, :, :], s3, wide(0), ALU.subtract))
            v.sem_inc(shifted, 1)
            v.wait_ge(exped, 1)
            link(nc.vector.tensor_reduce(sm[:, 0, :], SCO[:, :, :], AX.X, ALU.add))
            link(nc.vector.reciprocal(sm[:, 1, :], sm[:, 0, :]))
            nc.vector.tensor_tensor(SCO[:, :, :], SCO[:, :, :], wide(1), ALU.mult).then_inc(prob, 1)
            v.wait_ge(wt_done, 1)
            link(nc.vector.tensor_copy(WT[:, :], p_mean[0:F, 0:LH * F]))

        @block.tensor
        def _(pe):
            pe.wait_ge(unit_set, 1)
            pe.wait_ge(w_in, 96)
            for h in range(LH):
                last = nc.tensor.transpose(p_wv[:, h * C:(h + 1) * C], WV[:, h * C:(h + 1) * C], ident[:, :])
            last.then_inc(wvt_done, 1)
            pe.wait_ge(wvt_out, 1)
            for h in range(LH):
                nc.tensor.matmul(p_u[:, h * C:(h + 1) * C], WVT[:, h * C:(h + 1) * C], WP[:, h, :], start=True, stop=True)
            for h in range(LH):
                last = nc.tensor.matmul(p_c[:, 0:1], WP[:, h, :], BV[:, h:h + 1], start=(h == 0), stop=(h == LH - 1))
            last.then_inc(u_done, 1)
            for f in range(F):
                if f % GROUP == 0:
                    pe.wait_ge(normed, f // GROUP + 1)
                    pe.wait_ge(normed_s, f // GROUP + 1)
                last = nc.tensor.matmul(p_mean[0:F, 0:C], unit[:, F - 1 - f:2 * F - 1 - f], XN[:, f * C:(f + 1) * C],
                                        start=(f == 0), stop=(f == F - 1))
            last.then_inc(mean_done, 1)
            pe.wait_ge(xm_out, 1)
            nc.tensor.transpose(p_score[:, 0:F], XM[:, :], ident[0:F, 0:F]).then_inc(xm_turned, 1)
            pe.wait_ge(xmt_out, 1)
            for h in range(LH):
                for k in range(2):
                    last = nc.tensor.matmul(p_qk[:, (h * 2 + k) * F:(h * 2 + k + 1) * F], WQK[:, h, :, k], XMT[:, :], start=True, stop=True)
            last.then_inc(qk_done, 1)
            pe.wait_ge(qk_out, 1)
            for h in range(LH):
                last = nc.tensor.matmul(p_score[0:F, h * F:(h + 1) * F], QK[:, h, 0, :], QK[:, h, 1, :], start=True, stop=True)
            last.then_inc(sc_done, 1)
            pe.wait_ge(prob, 1)
            for h in range(LH):
                last = nc.tensor.transpose(p_mean[0:F, h * F:(h + 1) * F], SCO[:, h, :], ident[0:F, 0:F])
            last.then_inc(wt_done, 1)


def mix_rows(nc, sem, X, BN, XN_D, ident, WT, U, CB, x_back):
    TG = 8
    N = T // TG
    with ExitStack() as ctx:
        local = lambda n, s, d=F32: ctx.enter_context(nc.sbuf_tensor("sb_mr_" + n, s, d))
        pbank = lambda n: ctx.enter_context(nc.psum_tensor("mr_" + n, [P, BANK], F32))
        XG = local("xg", [F, 2, TG, C])
        ZT = local("zt", [C, 2, LH, TG * F])
        YT = local("yt", [C, 2, TG * F])
        pz = [pbank(f"pz{k}") for k in range(4)]
        py, pt = [pbank(f"py{k}") for k in range(2)], [pbank(f"pt{k}") for k in range(2)]
        loaded = [sem(f"mr_loaded{u}") for u in range(2)]
        z_done, za_out, zv_out, y_done, y_out, t_done, added = (sem("mr_" + n) for n in ("z", "za_out", "zv_out", "y", "y_out", "t", "added"))
        carried = sem("mr_carried")
        block = ctx.enter_context(nc.Block())
        X2 = X[:, :, :].rearrange("p s c -> p (s c)")
        XF = XN_D.rearrange("f t c -> f (t c)")

        @block.sync
        def _(sp):
            def load(g, u):
                after(sp, z_done, g - 1 + AHEAD)
                sp.dma_start(XG[:, u, :, :].rearrange("f t c -> f (t c)"), XF[:, ds(g * TG * C, TG * C)]).then_inc(loaded[u], 16)

            sp.dma_start(XG[:, 0, :, :].rearrange("f t c -> f (t c)"), XF[:, 0:TG * C]).then_inc(loaded[0], 16)
            load(1, 1)
            with sp.Fori(1, N // 2) as i:
                for u in range(2):
                    load(i * 2 + u, u)

        def z_copy(copy, g, u, b):
            return copy(ZT[:, u, :, b * 2 * F:(b + 1) * 2 * F].rearrange("p h (t f) -> p t h f", f=F),
                        pz[b][:, :].rearrange("p (t h f) -> p t h f", t=2, f=F))

        @block.scalar
        def _(act):
            def mixed_out(g, u):
                act.wait_ge(z_done, g + 1 + AHEAD)
                after(act, y_done, g - 1 + AHEAD)
                for b in (0, 2):
                    last = z_copy(lambda o, x: nc.scalar.activation(o, x, ACT.Copy), g, u, b)
                last.then_inc(za_out, 1)

            def projected_out(g, u):
                act.wait_ge(y_done, g + 1 + AHEAD)
                after(act, t_done, g - 1 + AHEAD)
                nc.scalar.activation(YT[:, u, :], py[u][:, :], ACT.Identity, bias=CB[:, :]).then_inc(y_out, 1)

            mixed_out(0, 0)
            mixed_out(1, 1)
            projected_out(0, 0)
            with act.Fori(0, N // 2 - 1) as i:
                mixed_out(i * 2 + 2, 0)
                projected_out(i * 2 + 1, 1)
                mixed_out(i * 2 + 3, 1)
                projected_out(i * 2 + 2, 0)
            projected_out(N - 1, 1)

        @block.vector
        def _(v):
            def mixed_out(g, u):
                v.wait_ge(z_done, g + 1 + AHEAD)
                after(v, y_done, g - 1 + AHEAD)
                for b in (1, 3):
                    last = z_copy(nc.vector.tensor_copy, g, u, b)
                last.then_inc(zv_out, 1)

            def add(g, u):
                v.wait_ge(t_done, g + 1 + AHEAD)
                xg = X2[:, ds(g * BANK, BANK)]
                nc.vector.tensor_tensor(xg, pt[u][:, :], xg, ALU.add).then_inc(added, 1)

            def statistics(g):
                v.wait_ge(added, g + 1 + 2)
                v.sem_inc(carried, 1)
                for k in range(GROUP):
                    tile_statistics(nc, BN, X2, g * GROUP + k)

            mixed_out(0, 0)
            mixed_out(1, 1)
            mixed_out(2, 0)
            v.wait_ge(x_back, 32)
            add(0, 0)
            mixed_out(3, 1)
            statistics(0)
            add(1, 1)
            with v.Fori(1, N // 2 - 1) as i:
                for u in range(2):
                    mixed_out(i * 2 + 2 + u, u)
                    statistics(i * 2 + u - 1)
                    add(i * 2 + u, u)
            for g in (N - 2, N - 1):
                statistics(g - 1)
                add(g, g % 2)
            statistics(N - 1)

        @block.tensor
        def _(pe):
            def mix(g, u, i):
                pe.wait_ge(loaded[u], (i + 1) * 16)
                after(pe, za_out, g)
                after(pe, zv_out, g)
                for t in range(TG):
                    last = nc.tensor.matmul(pz[t // 2][:, (t % 2) * LH * F:(t % 2 + 1) * LH * F], XG[:, u, t, :], WT[:, :],
                                            start=True, stop=True)
                last.then_inc(z_done, 1)

            def project(g, u):
                pe.wait_ge(za_out, g + 1)
                pe.wait_ge(zv_out, g + 1)
                for h in range(LH):
                    last = nc.tensor.matmul(py[u][:, :], U[:, h, :], ZT[:, u, h, :], start=(h == 0), stop=(h == LH - 1))
                last.then_inc(y_done, 1)

            def turn(g, u):
                pe.wait_ge(y_out, g + 1)
                pe.wait_ge(added, g - 1 + 2)
                for k in range(GROUP):
                    last = nc.tensor.transpose(pt[u][:, k * P:(k + 1) * P], YT[:, u, k * P:(k + 1) * P], ident[:, :])
                last.then_inc(t_done, 1)

            for counted in (z_done, y_done, t_done):
                pe.sem_inc(counted, AHEAD)
            pe.sem_inc(added, 2)
            mix(0, 0, 0)
            mix(1, 1, 0)
            project(0, 0)
            with pe.Fori(0, N // 2 - 1) as i:
                mix(i * 2 + 2, 0, i + 1)
                turn(i * 2, 0)
                project(i * 2 + 1, 1)
                mix(i * 2 + 3, 1, i + 1)
                turn(i * 2 + 1, 1)
                project(i * 2 + 2, 0)
            turn(N - 2, 0)
            project(N - 1, 1)
            turn(N - 1, 1)


def route_gates(nc, sem, LG, G, clear, load):
    E = EXPERTS1
    with ExitStack() as ctx:
        local = lambda n, s, d=F32: ctx.enter_context(nc.sbuf_tensor("sb_rg_" + n, s, d))
        t1, t2 = local("t1", [P, TILES * E * E]), local("t2", [P, TILES * E * E])
        earlier = local("earlier", [P, E, E])
        KEEP, st = local("keep", [P, TILES, E]), local("st", [P, 2, TILES])
        made, chain, shifted, exped = (sem("rg_" + n) for n in ("made", "chain", "shifted", "exped"))
        block = ctx.enter_context(nc.Block())

        @block.sync
        def _(sp):
            load(sp)

        @block.gpsimd
        def _(pool):
            clear(pool)
            earlier_mask(nc, pool, earlier[:, :, :], E, made)

        @block.scalar
        def _(act):
            act.wait_ge(shifted, 1)
            nc.scalar.activation(LG[:, :, :], LG[:, :, :], ACT.Exp).then_inc(exped, 1)

        @block.vector
        def _(v):
            link = Chain(v, chain)
            wide = lambda k: st[:, k, :].unsqueeze(2).to_broadcast([P, TILES, E])
            link(nc.vector.tensor_reduce(st[:, 0, :], LG[:, :, :], AX.X, ALU.max))
            link(nc.vector.tensor_tensor(LG[:, :, :], LG[:, :, :], wide(0), ALU.subtract))
            v.sem_inc(shifted, 1)
            v.wait_ge(exped, 1)
            link(nc.vector.tensor_reduce(st[:, 0, :], LG[:, :, :], AX.X, ALU.add))
            link(nc.vector.reciprocal(st[:, 1, :], st[:, 0, :]))
            link(nc.vector.tensor_tensor(LG[:, :, :], LG[:, :, :], wide(1), ALU.mult))
            v.wait_ge(made, 2)
            rank_gates(nc, link, LG[:, :, :], E, t1[:, :], t2[:, :], earlier[:, :, :], KEEP[:, :, :])
            link(nc.vector.tensor_tensor(LG[:, :, :], LG[:, :, :], KEEP[:, :, :], ALU.mult))
            link(nc.vector.tensor_reduce(st[:, 0, :], LG[:, :, :], AX.X, ALU.add))
            link(nc.vector.tensor_scalar(st[:, 0, :], st[:, 0, :], 1e-12, None, ALU.max))
            link(nc.vector.reciprocal(st[:, 1, :], st[:, 0, :]))
            link(nc.vector.tensor_tensor(G[:, :, :], LG[:, :, :], wide(1), ALU.mult))


def metaformer(nc, A, out):
    with ExitStack() as ctx:
        sem = lambda n: nc.alloc_semaphore(n)
        sb = lambda n, s, d=F32: ctx.enter_context(nc.sbuf_tensor("sb_" + n, s, d))
        part = lambda prefix: {n[len(prefix):]: a for n, a in A.items() if n.startswith(prefix)}
        c0, f0, c1, f1 = (part(p) for p in ("L0_conv_", "L0_ffn_", "L1_conv_", "L1_ffn_"))
        c0["x"] = A["x"]
        X = sb("X", [P, TILES, C])
        ident = sb("ident", [P, P])
        st = sb("st", [P, 2, TILES])
        mean, rstd = st[:, 0, :], st[:, 1, :]
        X2 = X[:, :, :].rearrange("p s c -> p (s c)")
        SRC_T = nc.dram_tensor("source_rows", [TOKENS, ROW], F32).ap()
        DST_T = nc.dram_tensor("target_rows", [TOKENS, 2 * GHEADS], F32).ap()
        XN_D = nc.dram_tensor("normed_rows", [F, T, C], F32).ap()
        X_D = nc.dram_tensor("x_rows", [F, T, C], F32).ap()
        CN = sb("CN", [P, TILES])
        PB = sb("PB", [P, HEADS, T])
        BN = sb("BN", [P, TILES, 6])
        TRIPS = sb("TRIPS", [P, 3], I32)
        TT = sb("TT", [P, TOKENS])
        G0, LAST, SUMS, Wg = sb("G0", [P, TILES, EXPERTS0]), sb("LAST", [P, ROW]), sb("SUMS", [P, TILES, PART]), sb("Wg", [C, GF])
        H, GT = sb("H", [P, TILES, GF]), sb("GT", [P, TILES, GF])
        WT, U, CB = sb("WT", [F, LH * F]), sb("U", [C, LH, C]), sb("CB", [C, 1])
        Wr, LG, G1 = sb("Wr", [C, EXPERTS1]), sb("LG", [P, TILES, EXPERTS1]), sb("G1", [P, TILES, EXPERTS1])
        with ExitStack() as c_keys:
            KG, KC = (c_keys.enter_context(nc.sbuf_tensor("sb_" + n, [P, w], F32)) for n, w in (("KG", GCOLS), ("KC", KCOLS)))
            with nc.cleanup_on_exit():
                loads = z_in, x_in, m_in = sem("z_in"), sem("x_in"), sem("mask_in")
                MB = TT[:, :]
                with ExitStack() as c:
                    z, zs, pbc = (c.enter_context(nc.sbuf_tensor("sb_" + n, shape, F32)) for n, shape in
                                  (("z", [P, T * CZ]), ("z_stat", [P, 4, T]), ("pbc", [P, HEADS])))
                    pz = [c.enter_context(nc.psum_tensor(f"p_z{k}", [P, BANK], F32)) for k in range(2)]

                    def prefetch(sp):
                        sp.dma_start(z[:, :], c0["z"][0].rearrange("q k c -> q (k c)")).then_inc(z_in, 16)
                        sp.dma_start(X[:, :, :], c0["x"][0].rearrange("s r c -> r s c")).then_inc(x_in, 16)
                        sp.dma_start(MB, c0["mask"][0].rearrange("s k -> (s k)").partition_broadcast(P)).then_inc(m_in, 16)

                    compact_edges(nc, sem, f0, c0, KG, KC, TRIPS, prefetch, z, zs, pz, pbc, MB, ident, loads)
                    pair_bias(nc, sem, X, BN, zs, pz, pbc, PB, x_in, mean, rstd)
                row_attention(nc, sem, c0, X, BN, PB, MB, ident, mean, rstd)
            with ExitStack() as c:
                turn_tokens(nc, sem, "t0", c, X2, BN, ident, mean, rstd, TT, Wg[:, :], GF, H, EPS_T, f0["W_gat"])
            graph_tables(nc, sem, f0, H, GT, SRC_T, DST_T, LAST)
            graph_edges(nc, sem, KG, KC, SRC_T, DST_T, TRIPS, SUMS, CN)
        quarter = TILES // 4

        def keep(sp, k, stored):
            sp.dma_start(X_D.rearrange("f t c -> t f c")[:, k * quarter:(k + 1) * quarter, :],
                         X[:, k * quarter:(k + 1) * quarter, :]).then_inc(stored, 16)
            return 1

        with ExitStack() as c:
            weights, clear, load = expert_weights(nc, sem, c, "x0", EXPERTS0, HID0 // P, f0["W1"], f0["b1"], f0["W2"], f0["b2"])
            graph_gates(nc, sem, f0, H, GT, LAST, SUMS, CN, G0, clear, load)
            run_experts(nc, sem, "x0", X2, TT, G0, EXPERTS0, HID0 // P, weights, ident, keep, BN)
        x_back = sem("x_back")
        mix_weights(nc, sem, c1, X, BN, TT, XN_D, X_D, mean, rstd, WT, U, CB, ident, x_back)
        mix_rows(nc, sem, X, BN, XN_D, ident, WT, U, CB, x_back)
        with ExitStack() as c:
            turn_tokens(nc, sem, "t1", c, X2, BN, ident, mean, rstd, TT, Wr[:, :], EXPERTS1, LG, EPS_T,
                        f1["router_w"].rearrange("e c -> c e"), residual=True)
        out_v = out[0].rearrange("f (j a) c -> a f j c", a=2)

        def store(sp, k, stored):
            for a in range(2):
                sp.dma_start(out_v[a, :, k * quarter:(k + 1) * quarter, :],
                             X[a * F:(a + 1) * F, k * quarter:(k + 1) * quarter, :]).then_inc(stored, 16)
            return 2
        with ExitStack() as c:
            weights, clear, load = expert_weights(nc, sem, c, "x1", EXPERTS1, 1, f1["w1"], f1["b1"], f1["w2"], f1["b2"])
            route_gates(nc, sem, LG, G1, clear, load)
            run_experts(nc, sem, "x1", X2, TT, G1, EXPERTS1, 1, weights, ident, store)


def kernel(**inputs):
    import numpy as _np
    import concourse.bacc as _bacc
    from concourse import mybir as _mybir
    from concourse.bass_utils import run_bass_kernel_spmd as _run

    nc = _bacc.Bacc("TRN2", target_bir_lowering=False, num_devices=1)
    arrays, A = {}, {}
    for name, a in inputs.items():
        a = _np.ascontiguousarray(a)
        arrays[f"in_{name}"] = a
        A[name] = nc.dram_tensor(f"in_{name}", a.shape, _mybir.dt.from_np(a.dtype), kind="ExternalInput").ap()
    out = nc.dram_tensor("out", (1, F, T, C), F32, kind="ExternalOutput").ap()
    metaformer(nc, A, out)
    r = _run(nc, [arrays], core_ids=[0])
    return r.results[0]["out"]
```
